# Optimizing a Trainium2 kernel written in Bass

```python
import numpy as np
import jax
import jax.numpy as jnp

def _softmax(x, axis=-1):
    return jax.nn.softmax(x, axis=axis)

def _gelu(x):
    return jax.nn.gelu(x, approximate=True)

def _silu(x):
    return jax.nn.silu(x)

def _sigmoid(x):
    return jax.nn.sigmoid(x)

def _layernorm(x, axis=-1, eps=1e-05):
    m = jnp.mean(x, axis=axis, keepdims=True)
    v = jnp.var(x, axis=axis, keepdims=True)
    return (x - m) / jnp.sqrt(v + eps)

def _scatter_add(tgt, idx, src, axis=0):
    return tgt.at[idx].add(src)

def _segment_sum(src, seg, n):
    return jax.ops.segment_sum(src, seg, n)
kernel_name = 'mk_perceiver_d1_seqx_r4_ec94cd'

def setup_inputs(seed: int=0):
    np.random.seed(seed)
    _w = jnp.asarray

    def _rec_inputs():
        import jax
        import jax.numpy as jnp
        _rk = jax.random.key(seed)
        x = -0.0002928 + 1 * jax.random.normal(jax.random.fold_in(_rk, 1), (4, 64, 256), jnp.float32)
        _lenS = 64 - jax.random.randint(jax.random.fold_in(_rk, 7), (4,), 0, max(1, 64 // 4) + 1, jnp.int32)
        _lenS2 = 1024 - jax.random.randint(jax.random.fold_in(_rk, 8), (4,), 0, max(1, 1024 // 4) + 1, jnp.int32)
        _ctx_1024P = jax.random.normal(jax.random.fold_in(_rk, 11), (4, 16, 256), jnp.float32)
        _ctx_1024c = jax.random.dirichlet(jax.random.fold_in(_rk, 511), 0.3 * jnp.ones((16,), jnp.float32), (4, 1024))
        _ctx_1024t = jnp.einsum('bsk,bkd->bsd', _ctx_1024c, _ctx_1024P)
        _ctx_1024t = _ctx_1024t * jax.lax.rsqrt(jnp.mean(jnp.square(_ctx_1024t)) + 1e-12) * 0.953939
        ctx_1024 = -1.39393e-06 + 0.999914 * (_ctx_1024t + 0.3 * jax.random.normal(jax.random.fold_in(_rk, 611), (4, 1024, 256), jnp.float32))
        return (x, ctx_1024)
    x, ctx_1024 = _rec_inputs()

    def _L0_xattn_setup():
        import jax, jax.numpy as jnp
        import numpy as np
        HEADS = 16
        DIM_HEAD = 64
        QUERY_DIM = 256
        CTX_DIM = 256
        INNER = HEADS * DIM_HEAD
        key = jax.random.key(seed)
        ks = jax.random.split(key, 7)
        B, N, M = (2, 512, 512)
        s = 0.02
        return {'x': jax.random.normal(ks[0], (B, N, QUERY_DIM), dtype=jnp.float32), 'context': jax.random.normal(ks[1], (B, M, CTX_DIM), dtype=jnp.float32), 'Wq': jax.random.normal(ks[2], (QUERY_DIM, INNER), dtype=jnp.float32) * s, 'Wk': jax.random.normal(ks[3], (CTX_DIM, INNER), dtype=jnp.float32) * s, 'Wv': jax.random.normal(ks[4], (CTX_DIM, INNER), dtype=jnp.float32) * s, 'Wo': jax.random.normal(ks[5], (INNER, QUERY_DIM), dtype=jnp.float32) * s, 'bo': jnp.zeros((QUERY_DIM,), dtype=jnp.float32)}
    _L0_xattn_all = _L0_xattn_setup()
    _L0_xattn_in = {k: v for k, v in _L0_xattn_all.items() if k in ('Wq', 'Wk', 'Wv', 'Wo', 'bo')}
    del _L0_xattn_all

    def _L0_attn_setup():
        import jax, jax.numpy as jnp
        import numpy as np
        B, S, D, H = (2, 512, 256, 16)
        HD = D // H
        EPS = 1e-05
        key = jax.random.key(seed)
        kx, kq, kk, kv, kb = jax.random.split(key, 5)
        sc = 0.02
        return {'x': jax.random.normal(kx, (B, S, D), dtype=jnp.float32), 'Wq': jax.random.normal(kq, (D, D), dtype=jnp.float32) * sc, 'Wk': jax.random.normal(kk, (D, D), dtype=jnp.float32) * sc, 'Wv': jax.random.normal(kv, (D, D), dtype=jnp.float32) * sc, 'rel_bias_table': jax.random.normal(kb, (2 * S - 1, H), dtype=jnp.float32) * sc, 'ln_gamma': jnp.ones((D,), dtype=jnp.float32), 'ln_beta': jnp.zeros((D,), dtype=jnp.float32)}
    _L0_attn_all = _L0_attn_setup()
    _L0_attn_in = {k: v for k, v in _L0_attn_all.items() if k in ('Wq', 'Wk', 'Wv', 'rel_bias_table', 'ln_gamma', 'ln_beta')}
    del _L0_attn_all

    def _L0_ffn_setup():
        import jax, jax.numpy as jnp
        import numpy as np
        B, T, D, H, E, K = (2, 256, 256, 16, 8, 2)
        HS = D // H
        FF = 4 * D

        def layernorm(x, g, b, eps=1e-05):
            m = jnp.mean(x, axis=-1, keepdims=True)
            v = jnp.mean((x - m) ** 2, axis=-1, keepdims=True)
            return (x - m) * jax.lax.rsqrt(v + eps) * g + b
        key = jax.random.key(seed)
        ks = jax.random.split(key, 10)
        s = 0.02
        return {'x': jax.random.normal(ks[0], (B, T, D), jnp.float32), 'Wq': jax.random.normal(ks[1], (H, D, HS), jnp.float32) * s, 'Wk': jax.random.normal(ks[2], (H, D, HS), jnp.float32) * s, 'Wv': jax.random.normal(ks[3], (H, D, HS), jnp.float32) * s, 'gate_W': jax.random.normal(ks[4], (D, E), jnp.float32) * s, 'W1': jax.random.normal(ks[5], (E, D, FF), jnp.float32) * s, 'b1': jnp.zeros((E, FF), jnp.float32), 'W2': jax.random.normal(ks[6], (E, FF, D), jnp.float32) * s, 'b2': jnp.zeros((E, D), jnp.float32), 'ln1_g': jnp.ones((D,), jnp.float32), 'ln1_b': jnp.zeros((D,), jnp.float32), 'ln2_g': jnp.ones((D,), jnp.float32), 'ln2_b': jnp.zeros((D,), jnp.float32)}
    _L0_ffn_all = _L0_ffn_setup()
    _L0_ffn_in = {k: v for k, v in _L0_ffn_all.items() if k in ('Wq', 'Wk', 'Wv', 'gate_W', 'W1', 'b1', 'W2', 'b2', 'ln1_g', 'ln1_b', 'ln2_g', 'ln2_b')}
    del _L0_ffn_all
    return {'x': x, 'ctx_1024': ctx_1024, 'L0_xattn_Wq': _L0_xattn_in['Wq'], 'L0_xattn_Wk': _L0_xattn_in['Wk'], 'L0_xattn_Wv': _L0_xattn_in['Wv'], 'L0_xattn_Wo': _L0_xattn_in['Wo'], 'L0_xattn_bo': _L0_xattn_in['bo'], 'L0_attn_Wq': _L0_attn_in['Wq'], 'L0_attn_Wk': _L0_attn_in['Wk'], 'L0_attn_Wv': _L0_attn_in['Wv'], 'L0_attn_rel_bias_table': _L0_attn_in['rel_bias_table'], 'L0_attn_ln_gamma': _L0_attn_in['ln_gamma'], 'L0_attn_ln_beta': _L0_attn_in['ln_beta'], 'L0_ffn_Wq': _L0_ffn_in['Wq'], 'L0_ffn_Wk': _L0_ffn_in['Wk'], 'L0_ffn_Wv': _L0_ffn_in['Wv'], 'L0_ffn_gate_W': _L0_ffn_in['gate_W'], 'L0_ffn_W1': _L0_ffn_in['W1'], 'L0_ffn_b1': _L0_ffn_in['b1'], 'L0_ffn_W2': _L0_ffn_in['W2'], 'L0_ffn_b2': _L0_ffn_in['b2'], 'L0_ffn_ln1_g': _L0_ffn_in['ln1_g'], 'L0_ffn_ln1_b': _L0_ffn_in['ln1_b'], 'L0_ffn_ln2_g': _L0_ffn_in['ln2_g'], 'L0_ffn_ln2_b': _L0_ffn_in['ln2_b']}

def reference(x, ctx_1024, L0_xattn_Wq, L0_xattn_Wk, L0_xattn_Wv, L0_xattn_Wo, L0_xattn_bo, L0_attn_Wq, L0_attn_Wk, L0_attn_Wv, L0_attn_rel_bias_table, L0_attn_ln_gamma, L0_attn_ln_beta, L0_ffn_Wq, L0_ffn_Wk, L0_ffn_Wv, L0_ffn_gate_W, L0_ffn_W1, L0_ffn_b1, L0_ffn_W2, L0_ffn_b2, L0_ffn_ln1_g, L0_ffn_ln1_b, L0_ffn_ln2_g, L0_ffn_ln2_b):
    import jax
    import jax.numpy as jnp

    def _L0_xattn_ref(x, context, Wq, Wk, Wv, Wo, bo):
        import jax, jax.numpy as jnp
        import numpy as np
        HEADS = 16
        DIM_HEAD = 64
        QUERY_DIM = 256
        CTX_DIM = 256
        INNER = HEADS * DIM_HEAD
        B, N, _ = x.shape
        M = context.shape[1]
        scale = DIM_HEAD ** (-0.5)
        q = (x @ Wq).reshape(B, N, HEADS, DIM_HEAD).transpose(0, 2, 1, 3)
        k = (context @ Wk).reshape(B, M, HEADS, DIM_HEAD).transpose(0, 2, 1, 3)
        v = (context @ Wv).reshape(B, M, HEADS, DIM_HEAD).transpose(0, 2, 1, 3)
        sim = jnp.einsum('bhid,bhjd->bhij', q, k) * scale
        attn = jax.nn.softmax(sim, axis=-1)
        out = jnp.einsum('bhij,bhjd->bhid', attn, v)
        out = out.transpose(0, 2, 1, 3).reshape(B, N, INNER)
        return out @ Wo + bo

    def _L0_attn_ref(x, Wq, Wk, Wv, rel_bias_table, ln_gamma, ln_beta):
        import jax, jax.numpy as jnp
        import numpy as np
        B, S, D, H = (2, 512, 256, 16)
        HD = D // H
        EPS = 1e-05
        bs, seq_len, d_model = x.shape
        scale = d_model ** (-0.5)
        q = jnp.einsum('bsd,ed->bse', x, Wq).reshape(bs, seq_len, H, HD).transpose(0, 2, 1, 3)
        k = jnp.einsum('bsd,ed->bse', x, Wk).reshape(bs, seq_len, H, HD).transpose(0, 2, 1, 3)
        v = jnp.einsum('bsd,ed->bse', x, Wv).reshape(bs, seq_len, H, HD).transpose(0, 2, 1, 3)
        attn = jax.nn.softmax(jnp.einsum('bhqd,bhkd->bhqk', q, k) * scale, axis=-1)
        idx = jnp.arange(seq_len)[:, None] - jnp.arange(seq_len)[None, :] + (seq_len - 1)
        rel_bias = rel_bias_table[idx]
        rel_bias = rel_bias.transpose(2, 0, 1)[None]
        attn = attn + rel_bias
        out = jnp.einsum('bhqk,bhkd->bhqd', attn, v)
        out = out.transpose(0, 2, 1, 3).reshape(bs, seq_len, d_model)
        mu = jnp.mean(out, axis=-1, keepdims=True)
        var = jnp.var(out, axis=-1, keepdims=True)
        out = (out - mu) * jax.lax.rsqrt(var + EPS)
        return out * ln_gamma + ln_beta

    def _L0_ffn_ref(x, Wq, Wk, Wv, gate_W, W1, b1, W2, b2, ln1_g, ln1_b, ln2_g, ln2_b):
        import jax, jax.numpy as jnp
        import numpy as np
        B, T, D, H, E, K = (2, 256, 256, 16, 8, 2)
        HS = D // H
        FF = 4 * D

        def layernorm(x, g, b, eps=1e-05):
            m = jnp.mean(x, axis=-1, keepdims=True)
            v = jnp.mean((x - m) ** 2, axis=-1, keepdims=True)
            return (x - m) * jax.lax.rsqrt(v + eps) * g + b
        b, t, d = x.shape
        q = jnp.einsum('btd,hdf->bhtf', x, Wq)
        k = jnp.einsum('btd,hdf->bhtf', x, Wk)
        v = jnp.einsum('btd,hdf->bhtf', x, Wv)
        wei = jnp.einsum('bhtf,bhsf->bhts', q, k) * d ** (-0.5)
        mask = jnp.tril(jnp.ones((t, t), bool))
        wei = jnp.where(mask, wei, -jnp.inf)
        wei = jax.nn.softmax(wei, axis=-1)
        attn = jnp.einsum('bhts,bhsf->bhtf', wei, v)
        attn = attn.transpose(0, 2, 1, 3).reshape(b, t, d)
        y = x + layernorm(attn, ln1_g, ln1_b)
        flat = y.reshape(-1, d)
        logits = flat @ gate_W
        topv, topi = jax.lax.top_k(logits, K)
        w = jax.nn.softmax(topv, axis=-1)
        combine = jnp.sum(jax.nn.one_hot(topi, E, dtype=flat.dtype) * w[..., None], axis=1)
        h = jax.nn.relu(jnp.einsum('nd,edf->enf', flat, W1) + b1[:, None, :])
        eo = jnp.einsum('enf,efd->end', h, W2) + b2[:, None, :]
        moe = jnp.einsum('ne,end->nd', combine, eo)
        out = y + layernorm(moe.reshape(b, t, d), ln2_g, ln2_b)
        return out
    x = x + _L0_xattn_ref(_layernorm(x, axis=-1), ctx_1024, L0_xattn_Wq, L0_xattn_Wk, L0_xattn_Wv, L0_xattn_Wo, L0_xattn_bo)
    x = x + _L0_attn_ref(_layernorm(x, axis=-1), L0_attn_Wq, L0_attn_Wk, L0_attn_Wv, L0_attn_rel_bias_table, L0_attn_ln_gamma, L0_attn_ln_beta)
    x = x + _L0_ffn_ref(_layernorm(x, axis=-1), L0_ffn_Wq, L0_ffn_Wk, L0_ffn_Wv, L0_ffn_gate_W, L0_ffn_W1, L0_ffn_b1, L0_ffn_W2, L0_ffn_b2, L0_ffn_ln1_g, L0_ffn_ln1_b, L0_ffn_ln2_g, L0_ffn_ln2_b)
    return x

_drawn_inputs = setup_inputs


def setup_inputs(seed=0):
    import zlib

    import numpy as np

    out = dict(_drawn_inputs(seed))
    spreads = {'L0_xattn_bo': (0.0, 0.1),
     'L0_attn_ln_gamma': (1.0, 0.2),
     'L0_attn_ln_beta': (0.0, 0.1),
     'L0_ffn_b1': (0.0, 0.1),
     'L0_ffn_b2': (0.0, 0.1),
     'L0_ffn_ln1_g': (1.0, 0.2),
     'L0_ffn_ln1_b': (0.0, 0.1),
     'L0_ffn_ln2_g': (1.0, 0.2),
     'L0_ffn_ln2_b': (0.0, 0.1)}
    factors = {'L0_xattn_Wq': 4.715, 'L0_xattn_Wk': 4.705, 'L0_ffn_Wq': 3.169}
    for name, (base, spread) in spreads.items():
        noise = np.random.default_rng([zlib.crc32(name.encode()), seed]).standard_normal(out[name].shape)
        drawn = base * np.exp(spread * noise) if base else spread * noise
        out[name] = jnp.asarray(drawn.astype(out[name].dtype))
    for name, factor in factors.items():
        out[name] = (out[name] * factor).astype(out[name].dtype)
    return out
```

```python
from contextlib import ExitStack

import concourse.bass as bass
from concourse import mybir

P = 128
ALU = mybir.AluOpType
ACT = mybir.ActivationFunctionType
F32 = mybir.dt.float32
F32R = mybir.dt.float32r
BF16 = mybir.dt.bfloat16
U32 = mybir.dt.uint32
AX_X = mybir.AxisListType.X
EPS = 1e-5


def perceiver_block(nc, a, out):
    NB, NQ, D = a["x"].shape
    NC_ = a["ctx"].shape[1]
    NT = NB * NQ // P
    KD = D // P
    NH = 16
    INNER = a["xattn_Wq"].shape[1]
    DH = INNER // NH
    NPAIR = NH // 2
    HD = D // NH
    HC = P // HD
    JT = NC_ // P
    ROWS = 512
    TG = ROWS // P
    GB = NH * NQ // ROWS
    NG = GB * NB
    NE, _, FF = a["W1"].shape
    FT = FF // P
    TOK = NB * NQ
    XSCALE = float(DH) ** -0.5
    SSCALE = float(D) ** -0.5
    HEADS_G = ROWS // NQ
    assert (NT, KD, NPAIR, JT, TG, GB, FT, TOK) == (2, 2, 8, 8, 4, 2, 8, 256)

    ctx = ExitStack()
    with ctx:
        def sem(name):
            return ctx.enter_context(nc.semaphore(name))

        def sb(stack, name, shape, dt=F32):
            return stack.enter_context(nc.sbuf_tensor(name, shape, dt))

        S = ctx.enter_context(nc.psum_tensor("S", [P, 4, 512], F32))
        T = ctx.enter_context(nc.psum_tensor("T", [P, 2, 512], F32))
        U = ctx.enter_context(nc.psum_tensor("U", [P, 2, 512], F32))

        ident = sb(ctx, "ident", [P, P])
        ident_bf = sb(ctx, "ident_bf", [P, P], BF16)
        headmask = sb(ctx, "headmask", [P, HC])
        causal = sb(ctx, "causal", [P, NQ])
        causal_bf = sb(ctx, "causal_bf", [P, HC, NQ], BF16)
        iota8 = sb(ctx, "iota8", [P, NE])
        pw = sb(ctx, "pw", [P, 2])
        xr = sb(ctx, "xr", [P, NT, D])
        xb = sb(ctx, "xb", [P, NT, D])
        xn = sb(ctx, "xn", [P, NT, D])
        xnT = sb(ctx, "xnT", [P, KD, TOK])
        vec = sb(ctx, "vec", [P, 7, D])
        stats = sb(ctx, "stats", [P, NT, 6])
        mv = sb(ctx, "mv", [P, NT, 2])
        rstd = sb(ctx, "rstd", [P, NT])
        self_w = sb(ctx, "self_w", [P, 2, 3, KD, D])
        gate = sb(ctx, "gate", [P, KD, NE])
        b1T = sb(ctx, "b1T", [P, NE, FT])
        b2 = sb(ctx, "b2", [NE, D])
        biasT = sb(ctx, "biasT", [P, NPAIR, NQ])
        small = sb(ctx, "small", [P, NT, 16, 8])
        mx8i = sb(ctx, "mx8i", [P, NT, 8], U32)
        cw = sb(ctx, "cw", [P, NT, NE])
        cT = sb(ctx, "cT", [NE, TOK])
        negmax = sb(ctx, "negmax", [P, 2, TG])
        rowsum = sb(ctx, "rowsum", [P, 2, TG])
        rowinv = sb(ctx, "rowinv", [P, 2, TG])

        ra = ExitStack()
        ctxT_hi = sb(ra, "ctxT_hi", [P, KD, NC_], F32R)
        ctxT_lo = sb(ra, "ctxT_lo", [P, KD, NC_], F32R)
        ctx_hi = sb(ra, "ctx_hi", [P, JT, D], F32R)
        ctx_lo = sb(ra, "ctx_lo", [P, JT, D], F32R)
        ctxT_raw = sb(ra, "ctxT_raw", [P, KD, NC_])
        ctx_raw = sb(ra, "ctx_raw", [P, JT // 2, D])
        probs = sb(ra, "probs", [P, 2, TG, NC_])
        pT_hi = sb(ra, "pT_hi", [P, 4, ROWS], F32R)
        pT_lo = sb(ra, "pT_lo", [P, 4, ROWS], F32R)
        qp_hi = sb(ra, "qp_hi", [P, 2, KD, ROWS], F32R)
        qp_lo = sb(ra, "qp_lo", [P, 2, KD, ROWS], F32R)
        Wq = sb(ra, "Wq", [P, KD, INNER])
        WkT = sb(ra, "WkT", [P, NPAIR, D])
        Qblk = sb(ra, "Qblk", [P, NB, NPAIR, 2, NQ])
        rb = ExitStack()
        UT = sb(rb, "UT", [P, KD, NH, TOK])
        Wv = Wq
        OT = Qblk[:, :, :, :, :].rearrange("p b h c q -> p (b h c q)")[:, 0:NPAIR * TOK].rearrange(
            "p (r t) -> p r t", r=NPAIR)
        Wo = ctxT_raw[:, :, :].rearrange("p k n -> p (k n)").rearrange("p (r d) -> p r d", r=NPAIR)
        rb.close()
        ra.close()

        rc = ExitStack()
        Wraw = sb(rc, "Wraw", [P, 2, 2, KD * FF])
        Whi = sb(rc, "Whi", [P, 2, 2, KD * FF], F32R)
        Wlo = sb(rc, "Wlo", [P, 2, 2, KD * FF], F32R)
        yT = sb(rc, "yT", [P, KD, TOK])
        yT_hi = sb(rc, "yT_hi", [P, KD, TOK], F32R)
        yT_lo = sb(rc, "yT_lo", [P, KD, TOK], F32R)
        acc = sb(rc, "acc", [P, NT, D])
        y = sb(rc, "y", [P, NT, D])
        xin = sb(rc, "xin", [P, NT, D])
        fin = sb(rc, "fin", [P, NT, D])
        rd = ExitStack()
        qT = sb(rd, "qT", [P, KD, TOK])
        kblk = sb(rd, "kblk", [P, KD, NB, HC, NQ])
        Vblk = sb(rd, "Vblk", [P, NB, NPAIR, 2 * HD])
        E = sb(rd, "E", [P, NT, NH, NQ])
        PT = sb(rd, "PT", [P, NT, NPAIR, P])
        nm = sb(rd, "nm", [P, NT, NH])
        rs = sb(rd, "rs", [P, NT, NH])
        ri = sb(rd, "ri", [P, NT, NH])
        rd.close()
        re_ = ExitStack()
        hT_hi = sb(re_, "hT_hi", [P, 2, FT, TOK], F32R)
        hT_lo = sb(re_, "hT_lo", [P, 2, FT, TOK], F32R)
        h32 = sb(re_, "h32", [P, 4, 2, TOK])
        re_.close()
        rc.close()

        in_x = sem("in_x")
        in_const = sem("in_const")
        in_Wq = sem("in_Wq")
        in_WkT = sem("in_WkT")
        in_vec = sem("in_vec")
        in_ctxT = sem("in_ctxT")
        in_ctx = sem("in_ctx")
        in_Wv = sem("in_Wv")
        in_Wo = sem("in_Wo")
        in_later = sem("in_later")
        in_W1 = [sem(f"in_W1_{i}") for i in range(2)]
        in_W2 = [sem(f"in_W2_{i}") for i in range(2)]
        stored = sem("stored")
        qblk_zero = sem("qblk_zero")
        q_mm = sem("q_mm")
        q_a = sem("q_a")
        q_v = sem("q_v")
        qp_mm = sem("qp_mm")
        qp_hi_ok = sem("qp_hi_ok")
        qp_lo_ok = sem("qp_lo_ok")
        ctxT_hi_ok = sem("ctxT_hi_ok")
        ctxT_lo_ok = sem("ctxT_lo_ok")
        ctx_hi_ok = sem("ctx_hi_ok")
        ctx_lo_ok = sem("ctx_lo_ok")
        sim_ok = sem("sim_ok")
        max_ok = sem("max_ok")
        exp_ok = sem("exp_ok")
        inv_ok = sem("inv_ok")
        norm_ok = sem("norm_ok")
        tr_ok = sem("tr_ok")
        pT_hi_ok = sem("pT_hi_ok")
        pT_lo_ok = sem("pT_lo_ok")
        av_ok = sem("av_ok")
        ut_a = sem("ut_a")
        ut_v = sem("ut_v")
        o_mm = sem("o_mm")
        o_a = sem("o_a")
        o_v = sem("o_v")
        wo_mm = sem("wo_mm")
        xb_ok = sem("xb_ok")
        mv_ok = sem("mv_ok")
        var_ok = sem("var_ok")
        rstd_ok = sem("rstd_ok")
        xn_ok = sem("xn_ok")
        xnT_mm = sem("xnT_mm")
        xnT_ok = sem("xnT_ok")
        chain = sem("chain")
        pchain = sem("pchain")
        power_ok = sem("power_ok")
        qk_mm = sem("qk_mm")
        v_mm = sem("v_mm")
        sq_ok = sem("sq_ok")
        kb_a = sem("kb_a")
        kb_v = sem("kb_v")
        vzero = sem("vzero")
        vb_a = sem("vb_a")
        vb_v = sem("vb_v")
        sc_mm = sem("sc_mm")
        shift_ok = sem("shift_ok")
        sexp_ok = sem("sexp_ok")
        snorm_ok = sem("snorm_ok")
        str_mm = sem("str_mm")
        pt_a = sem("pt_a")
        pt_v = sem("pt_v")
        ao_mm = sem("ao_mm")
        y_ok = sem("y_ok")
        xin_ok = sem("xin_ok")
        cbf_ok = sem("cbf_ok")
        yT_mm = sem("yT_mm")
        yT_ok = sem("yT_ok")
        yThi_ok = sem("yThi_ok")
        yTlo_ok = sem("yTlo_ok")
        lg_mm = sem("lg_mm")
        gdiff_ok = sem("gdiff_ok")
        gexp_ok = sem("gexp_ok")
        cw_ok = sem("cw_ok")
        cT_mm = sem("cT_mm")
        cT_ok = sem("cT_ok")
        b2_mm = sem("b2_mm")
        w_hi_ok = sem("w_hi_ok")
        w_lo_ok = sem("w_lo_ok")
        h_mm = sem("h_mm")
        relu_ok = sem("relu_ok")
        h_hi_ok = sem("h_hi_ok")
        h_lo_ok = sem("h_lo_ok")
        eo_mm = sem("eo_mm")
        acc_ok = sem("acc_ok")
        res_ok = sem("res_ok")
        fin_ok = sem("fin_ok")

        def f(t):
            return t.bitcast(F32)

        def bc(t, dim, n):
            t = t.unsqueeze(dim)
            return t.broadcast_to([*t.shape[:dim], n, *t.shape[dim + 1:]])

        ctx_v = a["ctx"].rearrange("b (j p) d -> b p j d", p=P)
        ctxT_v = a["ctxT"].rearrange("b (k p) n -> b p k n", p=P)
        W1_v = a["W1"].rearrange("e (k p) f -> e p k f", p=P)
        W2_v = a["W2"].rearrange("e (f p) d -> e p f d", p=P)
        x_v = a["x"].rearrange("b q d -> (b q) d").rearrange("(t p) d -> p t d", p=P)
        out_v = out.rearrange("b q d -> (b q) d").rearrange("(t p) d -> p t d", p=P)

        block = ctx.enter_context(nc.Block())

        @block.sync
        def _(sp):
            sp.dma_start(xr[:, :, :], x_v).then_inc(in_x, 16)
            for dst, name in ((ident, "ident"), (headmask, "headmask"), (causal, "causal"), (iota8, "iota8")):
                sp.dma_start(dst[:, :], a[name]).then_inc(in_const, 16)
            sp.dma_start(Wq[:, :, :], a["xattn_Wq"].rearrange("(k p) n -> p k n", p=P)).then_inc(in_Wq, 16)
            sp.dma_start(WkT[:, :, :], a["xattn_WkT"].rearrange("(r p) d -> p r d", p=P)).then_inc(in_WkT, 16)
            sp.dma_start(ctxT_raw[:, :, :], ctxT_v[0]).then_inc(in_ctxT, 16)
            sp.dma_start(ctx_raw[:, :, :], ctx_v[0][:, 0:JT // 2, :]).then_inc(in_ctx, 16)
            for i, name in enumerate(("bo", "gamma", "beta", "g1", "b1n", "g2", "b2n")):
                sp.dma_start(vec[:, i, :], a[name].partition_broadcast(P)).then_inc(in_vec, 16)
            sp.wait_ge(q_mm, 4)
            sp.dma_start(Wv[:, :, :], a["xattn_Wv"].rearrange("(k p) n -> p k n", p=P)).then_inc(in_Wv, 16)
            for s in range(2):
                for i, name in enumerate(("q", "k", "v")):
                    sp.dma_start(self_w[:, s, i, :, :],
                                 a[f"self{s}_{name}"].rearrange("(k p) n -> p k n", p=P)).then_inc(in_later, 16)
            sp.dma_start(gate[:, :, :], a["gate"].rearrange("(k p) n -> p k n", p=P)).then_inc(in_later, 16)
            sp.dma_start(b1T[:, :, :], a["b1"].rearrange("p (e f) -> p e f", e=NE)).then_inc(in_later, 16)
            sp.dma_start(b2[:, :], a["b2"]).then_inc(in_later, 16)
            sp.dma_start(biasT[:, :, :], a["biasT"]).then_inc(in_later, 16)
            sp.wait_ge(ctx_lo_ok, JT // 2)
            sp.dma_start(ctx_raw[:, :, :], ctx_v[0][:, JT // 2:JT, :]).then_inc(in_ctx, 16)
            with sp.Fori(0, NB - 1) as b:
                sp.wait_ge(ctxT_lo_ok, b * 4 + 4)
                sp.dma_start(ctxT_raw[:, :, :], ctxT_v[bass.ds(b + 1, 1)].rearrange("o p k n -> p (o k) n")
                             ).then_inc(in_ctxT, 16)
                for half in range(2):
                    sp.wait_ge(ctx_lo_ok, b * JT + JT + half * (JT // 2))
                    sp.dma_start(ctx_raw[:, :, :],
                                 ctx_v[bass.ds(b + 1, 1), :, half * (JT // 2):(half + 1) * (JT // 2), :].rearrange(
                                     "o p j d -> p (o j) d")).then_inc(in_ctx, 16)
            sp.wait_ge(ctxT_lo_ok, 4 * NB)
            sp.dma_start(Wo, a["xattn_Wo"].rearrange("(r p) d -> p r d", p=P)).then_inc(in_Wo, 16)
            sp.wait_ge(wo_mm, NT)
            for e in range(2):
                sp.dma_start(Wraw[:, e, 0, :].rearrange("p (k n) -> p k n", k=KD), W1_v[e]).then_inc(in_W1[e], 16)
                sp.dma_start(Wraw[:, e, 1, :].rearrange("p (k n) -> p k n", k=FT), W2_v[e]).then_inc(in_W2[e], 16)
            with sp.Fori(0, NE // 2 - 1) as turn:
                e = turn * 2
                for i in range(2):
                    sp.wait_ge(w_lo_ok, (e + i) * 8 + 4)
                    sp.dma_start(Wraw[:, i, 0, :].rearrange("p (k n) -> p k n", k=KD),
                                 W1_v[bass.ds(e + (i + 2), 1)].rearrange("o p k n -> p (o k) n")
                                 ).then_inc(in_W1[i], 16)
                    sp.wait_ge(w_lo_ok, (e + i) * 8 + 8)
                    sp.dma_start(Wraw[:, i, 1, :].rearrange("p (k n) -> p k n", k=FT),
                                 W2_v[bass.ds(e + (i + 2), 1)].rearrange("o p k n -> p (o k) n")
                                 ).then_inc(in_W2[i], 16)
            for t in range(NT):
                sp.wait_ge(fin_ok, t + 1)
                sp.dma_start(out_v[:, t, :], fin[:, t, :]).then_inc(stored, 16)
            sp.wait_ge(stored, 16 * NT)

        @block.tensor
        def _(pe):
            mm = nc.tensor.matmul

            def passes3(dst, l_hi, l_lo, r_hi, r_lo, start, stop):
                mm(dst, l_hi, r_hi, start=start, stop=False)
                mm(dst, l_hi, r_lo, start=False, stop=False)
                return mm(dst, l_lo, r_hi, start=False, stop=stop)

            def transpose_rows(stage, src):
                for t in range(NT):
                    pe.wait_ge(xn_ok, NT * stage + t + 1)
                    for k in range(KD):
                        last = nc.tensor.transpose(T[:, t, k * P:(k + 1) * P], src[:, t, k * P:(k + 1) * P],
                                                   ident[:, :])
                    last.then_inc(xnT_mm, 1)

            def absorbed_query(g, b, par):
                for k in range(KD):
                    for r in range(TG):
                        pair = TG * g + r
                        last = mm(S[:, 2 * par + k, r * P:(r + 1) * P], WkT[:, pair, k * P:(k + 1) * P],
                                  Qblk[:, b, pair, :, :] if isinstance(b, int) else
                                  Qblk[:, bass.ds(b, 1), pair, :, :].rearrange("p o c q -> p (o c) q"),
                                  start=True, stop=True)
                last.then_inc(qp_mm, 1)

            def scores(gp, r, par, half):
                for k in range(KD):
                    last = passes3(S[:, 2 * par + half, :], qp_hi[:, gp, k, r * P:(r + 1) * P],
                                   qp_lo[:, gp, k, r * P:(r + 1) * P],
                                   ctxT_hi[:, k, half * 512:(half + 1) * 512],
                                   ctxT_lo[:, k, half * 512:(half + 1) * 512], k == 0, k == KD - 1)
                if half == 1:
                    last.then_inc(sim_ok, 1)

            def transpose_probs(gp, j):
                for r in range(TG):
                    last = nc.tensor.transpose(T[:, j % 2, r * P:(r + 1) * P], probs[:, gp, r, j * P:(j + 1) * P],
                                               ident[:, :])
                last.then_inc(tr_ok, 1)

            def attend(G, b, j):
                pe.wait_ge(pT_lo_ok, G * JT + (j + 1))
                pe.wait_ge(ctx_lo_ok, b * JT + (j + 1))
                if j == 0:
                    pe.wait_ge(ut_a, G + 1)
                    pe.wait_ge(ut_v, G + 1)
                for k in range(KD):
                    last = passes3(U[:, k, :], ctx_hi[:, j, k * P:(k + 1) * P], ctx_lo[:, j, k * P:(k + 1) * P],
                                   pT_hi[:, j % 4, :], pT_lo[:, j % 4, :], j == 0, j == JT - 1)
                last.then_inc(av_ok, 1)

            def group(b, g, ahead):
                G = b * GB + g
                gp, nxt, nb = g, 1 - g, b + g
                par = (G + 1) % 2 if isinstance(G, int) else (g + 1) % 2
                pe.wait_ge(norm_ok, G * TG + TG)
                transpose_probs(gp, 0)
                transpose_probs(gp, 1)
                if ahead:
                    absorbed_query(nxt, nb, par)
                attend(G, b, 0)
                transpose_probs(gp, 2)
                attend(G, b, 1)
                for r in range(TG):
                    transpose_probs(gp, r + 3)
                    if ahead:
                        if r == 0:
                            pe.wait_ge(qp_lo_ok, G + 2)
                            pe.wait_ge(ctxT_lo_ok, nb * 4 + 4)
                        if r >= 2:
                            pe.wait_ge(exp_ok, G * TG + (TG + r - 1))
                        scores(nxt, r, (par + 1 + r) % 2, 0)
                        scores(nxt, r, (par + 1 + r) % 2, 1)
                    attend(G, b, r + 2)
                transpose_probs(gp, 7)
                attend(G, b, 6)
                attend(G, b, 7)

            pe.wait_ge(in_const, 64)
            transpose_rows(0, xn)
            pe.wait_ge(in_Wq, 16)
            pe.wait_ge(xnT_ok, NT)
            for pair in range(NPAIR):
                for k in range(KD):
                    last = mm(S[:, pair // 2, (pair % 2) * TOK:(pair % 2 + 1) * TOK],
                              Wq[:, k, pair * P:(pair + 1) * P], xnT[:, k, :], start=(k == 0), stop=(k == KD - 1))
                if pair % 2:
                    last.then_inc(q_mm, 1)
            pe.wait_ge(in_WkT, 16)
            pe.wait_ge(q_a, 4)
            pe.wait_ge(q_v, 4)
            absorbed_query(0, 0, 0)
            pe.wait_ge(qp_lo_ok, 1)
            pe.wait_ge(ctxT_lo_ok, 4)
            for r in range(TG):
                if r >= 2:
                    pe.wait_ge(exp_ok, r - 1)
                scores(0, r, (1 + r) % 2, 0)
                scores(0, r, (1 + r) % 2, 1)
            with pe.Fori(0, NB - 1) as b:
                group(b, 0, True)
                group(b, 1, True)
            group(NB - 1, 0, True)
            group(NB - 1, 1, False)

            pe.wait_ge(in_Wv, 16)
            pe.wait_ge(ut_a, NG + 1)
            pe.wait_ge(ut_v, NG + 1)
            for h in range(NH):
                pair, c = h // 2, h % 2
                for k in range(KD):
                    last = mm(S[c * DH:(c + 1) * DH, pair // 2, (pair % 2) * TOK:(pair % 2 + 1) * TOK],
                              Wv[:, k, h * DH:(h + 1) * DH], UT[:, k, h, :], start=(k == 0), stop=(k == KD - 1))
                if h % 4 == 3:
                    last.then_inc(o_mm, 1)
            pe.wait_ge(in_Wo, 16)
            pe.wait_ge(o_a, 2)
            pe.wait_ge(o_v, 2)
            for t in range(NT):
                for pair in range(NPAIR):
                    last = mm(T[:, t, 0:D], OT[:, pair, t * P:(t + 1) * P], Wo[:, pair, :],
                              start=(pair == 0), stop=(pair == NPAIR - 1))
                last.then_inc(wo_mm, 1)

            def self_attention(s):
                if s == 0:
                    pe.wait_ge(in_later, 160)
                transpose_rows(s + 1, xn if s == 0 else xin)
                pe.wait_ge(xnT_ok, NT * (s + 2))
                for c in range(KD):
                    for k in range(KD):
                        mm(S[:, 0, c * TOK:(c + 1) * TOK], self_w[:, s, 0, k, c * P:(c + 1) * P], xnT[:, k, :],
                           start=(k == 0), stop=(k == KD - 1))
                for c, dst in ((0, S[:, 1, 0:TOK]), (1, U[:, 0, 0:TOK])):
                    for k in range(KD):
                        last = mm(dst, self_w[:, s, 1, k, c * P:(c + 1) * P], xnT[:, k, :],
                                  start=(k == 0), stop=(k == KD - 1))
                last.then_inc(qk_mm, 1)
                for b in range(NB):
                    for k in range(KD):
                        for c in range(2):
                            last = mm(S[c * NQ:(c + 1) * NQ, 2 + b // 2, (b % 2) * D:(b % 2 + 1) * D],
                                      xnT[:, k, b * NQ:(b + 1) * NQ], self_w[:, s, 2, k, :],
                                      start=(k == 0), stop=(k == KD - 1), skip_group_check=True)
                last.then_inc(v_mm, 1)
                pe.wait_ge(sq_ok, s + 1)
                pe.wait_ge(kb_a, s + 1)
                pe.wait_ge(kb_v, s + 1)
                for t, dst in ((0, T), (1, U)):
                    for c in range(KD):
                        if s == 1:
                            if t == 0 and c == 0:
                                pe.wait_ge(cbf_ok, 1)
                            mm(dst[:, c, :], ident_bf[:, :], causal_bf[:, :, :], start=True, stop=False,
                               skip_group_check=True)
                        for i in range(2):
                            b = 2 * t + i
                            last = mm(dst[i * NQ:(i + 1) * NQ, c, :], qT[:, c, b * NQ:(b + 1) * NQ],
                                      kblk[:, c, b, :, :], start=(s == 0), stop=True, skip_group_check=True)
                    last.then_inc(sc_mm, 1)
                pe.wait_ge(vb_a, s + 1)
                pe.wait_ge(vb_v, s + 1)
                for t in range(NT):
                    pe.wait_ge(snorm_ok, NT * s + t + 1)
                    for pair in range(NPAIR):
                        last = nc.tensor.transpose(S[:, 2 * t + pair // 4, (pair % 4) * P:(pair % 4 + 1) * P],
                                                   E[:, t, 2 * pair:2 * pair + 2, :], ident[:, :])
                    last.then_inc(str_mm, 1)
                for t in range(NT):
                    if s == 1:
                        pe.wait_ge(pt_a, t + 1)
                    pe.wait_ge(pt_v, NT * s + t + 1)
                    for i in range(2):
                        for pair in range(NPAIR):
                            last = mm(T[i * NQ:(i + 1) * NQ, t, pair * 2 * HD:(pair + 1) * 2 * HD],
                                      PT[:, t, pair, i * NQ:(i + 1) * NQ], Vblk[:, 2 * t + i, pair, :],
                                      start=True, stop=True, skip_group_check=True)
                    last.then_inc(ao_mm, 1)

            self_attention(0)
            self_attention(1)

            for t in range(NT):
                pe.wait_ge(y_ok, t + 1)
                for k in range(KD):
                    last = nc.tensor.transpose(S[:, t, k * P:(k + 1) * P], y[:, t, k * P:(k + 1) * P], ident[:, :])
                last.then_inc(yT_mm, 1)
            pe.wait_ge(yT_ok, NT)
            for t in range(NT):
                for k in range(KD):
                    last = mm(T[:, t, 0:NE], yT[:, k, t * P:(t + 1) * P], gate[:, k, :],
                              start=(k == 0), stop=(k == KD - 1))
                last.then_inc(lg_mm, 1)

            def hidden(e, i, f2):
                if f2 == 0:
                    pe.wait_ge(w_lo_ok, e * 8 + 4)
                if not isinstance(e, int) or e > 0:
                    pe.wait_ge(relu_ok, (e - 1) * 4 + (f2 + 1))
                for ft in (2 * f2, 2 * f2 + 1):
                    for k in range(KD):
                        w = slice(k * FF + ft * P, k * FF + (ft + 1) * P)
                        last = passes3(S[:, f2, (ft % 2) * TOK:(ft % 2 + 1) * TOK], Whi[:, i, 0, w], Wlo[:, i, 0, w],
                                       yT_hi[:, k, :], yT_lo[:, k, :], k == 0, k == KD - 1)
                last.then_inc(h_mm, 1)

            def expert_out(e, i, f2):
                dst = (T, U)[i]
                pe.wait_ge(h_lo_ok, e * 4 + (f2 + 1))
                if f2 == 0:
                    pe.wait_ge(w_lo_ok, e * 8 + 8)
                    pe.wait_ge(acc_ok, e * NT + NT)
                for t in range(NT):
                    for ft in (2 * f2, 2 * f2 + 1):
                        w = slice(ft * D, (ft + 1) * D)
                        l_hi = hT_hi[:, i, ft, t * P:(t + 1) * P]
                        l_lo = hT_lo[:, i, ft, t * P:(t + 1) * P]
                        last = passes3(dst[:, t, 0:D], l_hi, l_lo, Whi[:, i, 1, w], Wlo[:, i, 1, w],
                                       ft == 0, ft == FT - 1)
                last.then_inc(eo_mm, 1)

            pe.wait_ge(yThi_ok, 1)
            pe.wait_ge(yTlo_ok, 1)
            for f2 in range(4):
                hidden(0, 0, f2)
            pe.wait_ge(cw_ok, NT)
            for t in range(NT):
                last = nc.tensor.transpose(U[0:NE, t, 0:P], cw[:, t, :], ident[:, :])
            last.then_inc(cT_mm, 1)
            pe.wait_ge(cT_ok, 1)
            for t in range(NT):
                last = mm(U[:, t, 0:D], cT[:, t * P:(t + 1) * P], b2[:, :], start=True, stop=True)
            last.then_inc(b2_mm, 1)
            pe.wait_ge(acc_ok, 2 * NT)
            with pe.Fori(0, NE // 2 - 1) as turn:
                e = turn * 2
                for f2 in range(4):
                    hidden(e + 1, 1, f2)
                    expert_out(e, 0, f2)
                for f2 in range(4):
                    hidden(e + 2, 0, f2)
                    expert_out(e + 1, 1, f2)
            for f2 in range(4):
                hidden(NE - 1, 1, f2)
                expert_out(NE - 2, 0, f2)
            for f2 in range(4):
                expert_out(NE - 1, 1, f2)

        @block.scalar
        def _(act):
            def copy(dst, src, scale=1.0):
                return nc.scalar.activation(dst, src, ACT.Copy, scale=scale)

            def rows_T(stage):
                for t in range(NT):
                    act.wait_ge(xnT_mm, NT * stage + t + 1)
                    copy(xnT[:, :, t * P:(t + 1) * P],
                         T[:, t, 0:D].rearrange("p (k q) -> p k q", k=KD)).then_inc(xnT_ok, 1)

            act.sem_inc(ut_a, 1)
            rows_T(0)
            act.wait_ge(qblk_zero, 1)
            for n in range(4):
                act.wait_ge(q_mm, n + 1)
                copy(Qblk[0:DH, :, 2 * n:2 * n + 2, 0, :].rearrange("p b r q -> p r b q"),
                     S[0:DH, n, :].rearrange("p (r b q) -> p r b q", r=2, b=NB)).then_inc(q_a, 1)

            def split_query(G, gp, par):
                act.wait_ge(qp_mm, G + 1)
                copy(qp_hi[:, gp, :, :], S[:, 2 * par:2 * par + 2, :], XSCALE).then_inc(qp_hi_ok, 1)

            def split_ctxT(b):
                act.wait_ge(in_ctxT, b * 16 + 16)
                if not isinstance(b, int) or b > 0:
                    act.wait_ge(sim_ok, b * (GB * TG))
                for n in range(4):
                    k, c = n // 2, n % 2
                    copy(ctxT_hi[:, k, c * 512:(c + 1) * 512],
                         ctxT_raw[:, k, c * 512:(c + 1) * 512]).then_inc(ctxT_hi_ok, 1)

            def exponentials(G, gp, r, par):
                act.wait_ge(max_ok, G * TG + (r + 1))
                nc.scalar.activation(probs[:, gp, r, :], S[:, 2 * par:2 * par + 2, :].rearrange("p a n -> p (a n)"),
                                     ACT.Exp, bias=negmax[:, gp, r:r + 1],
                                     accum_out=rowsum[:, gp, r:r + 1]).then_inc(exp_ok, 1)

            def split_probs(G, j):
                act.wait_ge(tr_ok, G * JT + (j + 1))
                copy(pT_hi[:, j % 4, :], T[:, j % 2, :]).then_inc(pT_hi_ok, 1)

            def group(b, g, ahead):
                G = b * GB + g
                nxt = 1 - g
                par = (G + 1) % 2 if isinstance(G, int) else (g + 1) % 2
                split_probs(G, 0)
                split_probs(G, 1)
                if ahead:
                    split_query(G + 1, nxt, par)
                if ahead and g == 1:
                    split_ctxT(b + 1)
                split_probs(G, 2)
                split_probs(G, 3)
                for r in range(TG):
                    if r < 3:
                        if ahead:
                            exponentials(G + 1, nxt, r, (par + 1 + r) % 2)
                        split_probs(G, r + 4)
                    else:
                        split_probs(G, 7)
                        if ahead:
                            exponentials(G + 1, nxt, r, (par + 1 + r) % 2)
                act.wait_ge(av_ok, G * JT + JT)
                copy(UT[:, 0, g * HEADS_G:(g + 1) * HEADS_G,
                        b * NQ:(b + 1) * NQ] if isinstance(b, int) else
                     UT[:, 0, g * HEADS_G:(g + 1) * HEADS_G, bass.ds(b * NQ, NQ)],
                     U[:, 0, :].rearrange("p (h q) -> p h q", h=HEADS_G)).then_inc(ut_a, 1)

            split_ctxT(0)
            split_query(0, 0, 0)
            for r in range(TG):
                exponentials(0, 0, r, (1 + r) % 2)
            with act.Fori(0, NB - 1) as b:
                group(b, 0, True)
                group(b, 1, True)
            group(NB - 1, 0, True)
            group(NB - 1, 1, False)

            for n in (0, 2):
                act.wait_ge(o_mm, n + 1)
                copy(OT[:, 2 * n:2 * n + 2, :], S[:, n, :].rearrange("p (r t) -> p r t", r=2)).then_inc(o_a, 1)

            def self_attention(s):
                rows_T(s + 1)
                act.wait_ge(qk_mm, s + 1)
                copy(qT[:, :, :], S[:, 0, :].rearrange("p (c t) -> p c t", c=KD)).then_inc(sq_ok, 1)
                for h in range(HC):
                    last = copy(kblk[:, 1, :, h, :], U[:, 0, 0:TOK].rearrange("p (b q) -> p b q", b=NB),
                                headmask[:, h:h + 1])
                last.then_inc(kb_a, 1)
                act.wait_ge(v_mm, s + 1)
                act.wait_ge(vzero, 1)
                copy(Vblk[0:NQ, :, :, 0:HD],
                     S[0:NQ, 2:4, :].rearrange("p a (b r c e) -> p (a b) r c e", b=2, r=NPAIR, c=2)[:, :, :, 0, :]
                     ).then_inc(vb_a, 1)
                for t in range(NT):
                    act.wait_ge(shift_ok, NT * s + t + 1)
                    nc.scalar.activation(E[:, t, :, :], E[:, t, :, :], ACT.Exp, scale=SSCALE).then_inc(sexp_ok, 1)
                if s == 1:
                    for t in range(NT):
                        act.wait_ge(str_mm, NT * s + t + 1)
                        copy(PT[:, t, 0:4, :],
                             S[:, 2 * t, :].rearrange("p (r q) -> p r q", r=4)).then_inc(pt_a, 1)

            self_attention(0)
            self_attention(1)

            for t in range(NT):
                act.wait_ge(yT_mm, t + 1)
                copy(yT[:, :, t * P:(t + 1) * P],
                     S[:, t, 0:D].rearrange("p (k q) -> p k q", k=KD)).then_inc(yT_ok, 1)
            act.wait_ge(yT_ok, NT)
            copy(yT_hi[:, :, :], yT[:, :, :]).then_inc(yThi_ok, 1)

            def split_weights(e, i, m):
                n16 = (e - i) * 8 + 16 if not isinstance(e, int) else (e // 2) * 16 + 16
                act.wait_ge((in_W1, in_W2)[m][i], n16)
                if not isinstance(e, int) or e >= 2:
                    if m == 0:
                        act.wait_ge(h_mm, (e - 1) * 4)
                    else:
                        act.wait_ge(eo_mm, (e - 1) * 4)
                for n in range(4):
                    copy(Whi[:, i, m, n * 512:(n + 1) * 512], Wraw[:, i, m, n * 512:(n + 1) * 512]
                         ).then_inc(w_hi_ok, 1)

            def relu(e, i, f2):
                act.wait_ge(h_mm, e * 4 + (f2 + 1))
                if not isinstance(e, int) or e > 0:
                    act.wait_ge(h_lo_ok, (e - 1) * 4 + (f2 + 1))
                for c in range(2):
                    ft = 2 * f2 + c
                    bias = b1T[:, e, ft:ft + 1] if isinstance(e, int) else b1T[:, bass.ds(e, 1), ft]
                    last = nc.scalar.activation(h32[:, f2, c, :], S[:, f2, c * TOK:(c + 1) * TOK], ACT.Relu,
                                                bias=bias)
                last.then_inc(relu_ok, 1)

            for m in range(2):
                split_weights(0, 0, m)
            for m in range(2):
                split_weights(1, 1, m)
            for t in range(NT):
                act.wait_ge(gdiff_ok, t + 1)
                nc.scalar.activation(small[:, t, 1, 0:1], small[:, t, 1, 1:2], ACT.Exp).then_inc(gexp_ok, 1)
            for f2 in range(4):
                relu(0, 0, f2)
            with act.Fori(0, NE // 2 - 1) as turn:
                e = turn * 2
                for i in range(2):
                    for f2 in range(4):
                        relu(e + (i + 1), 1 - i, f2)
                        if f2 == 0:
                            split_weights(e + (i + 2), i, 0)
                    split_weights(e + (i + 2), i, 1)
            for f2 in range(4):
                relu(NE - 1, 1, f2)

        @block.vector
        def _(dve):
            count = [0]

            def link(ins):
                count[0] += 1
                ins.then_inc(chain, 1)
                dve.wait_ge(chain, count[0])

            sub = ALU.subtract

            def normalise(n, t, src, dst):
                link(nc.vector.bn_stats(stats[:, t, :], src))
                nc.vector.bn_aggr(mv[:, t, :], stats[:, t, :]).then_inc(mv_ok, 1)
                dve.wait_ge(rstd_ok, n + 1)
                return nc.vector.tensor_scalar(dst, src, mv[:, t, 0:1], rstd[:, t:t + 1], sub, ALU.mult)

            dve.sem_inc(ut_v, 1)
            dve.wait_ge(in_x, 16)
            for t in range(NT):
                normalise(t, t, xr[:, t, :], xn[:, t, :]).then_inc(xn_ok, 1)
            dve.wait_ge(in_const, 64)
            nc.vector.tensor_copy(ident_bf[:, :], ident[:, :])
            nc.vector.tensor_copy(causal_bf[:, :, :], bc(causal[:, :], 1, HC)).then_inc(cbf_ok, 1)

            def split_ctxT(b):
                for n in range(4):
                    k, c = n // 2, n % 2
                    w = slice(c * 512, (c + 1) * 512)
                    dve.wait_ge(ctxT_hi_ok, b * 4 + (n + 1))
                    nc.vector.tensor_tensor(ctxT_lo[:, k, w], ctxT_raw[:, k, w], f(ctxT_hi[:, k, w]),
                                            sub).then_inc(ctxT_lo_ok, 1)

            split_ctxT(0)
            dve.wait_ge(qblk_zero, 1)
            for n in range(4):
                dve.wait_ge(q_mm, n + 1)
                nc.vector.tensor_copy(Qblk[DH:P, :, 2 * n:2 * n + 2, 1, :].rearrange("p b r q -> p r b q"),
                                      S[DH:P, n, :].rearrange("p (r b q) -> p r b q", r=2, b=NB)).then_inc(q_v, 1)

            def split_query(G, gp, par):
                dve.wait_ge(qp_hi_ok, G + 1)
                nc.vector.scalar_tensor_tensor(out=qp_lo[:, gp, :, :], in0=S[:, 2 * par:2 * par + 2, :],
                                               scalar=XSCALE, in1=f(qp_hi[:, gp, :, :]), op0=ALU.mult,
                                               op1=sub).then_inc(qp_lo_ok, 1)

            def row_max(G, gp, r, par):
                dve.wait_ge(sim_ok, G * TG + (r + 1))
                nc.vector.tensor_reduce(out=negmax[:, gp, r:r + 1],
                                        in_=S[:, 2 * par:2 * par + 2, :].rearrange("p a n -> p (a n)"),
                                        axis=AX_X, op=ALU.max, negate=True).then_inc(max_ok, 1)

            def row_scale(G, gp, r):
                dve.wait_ge(exp_ok, G * TG + (r + 1))
                nc.vector.reciprocal(rowinv[:, gp, r:r + 1], rowsum[:, gp, r:r + 1]).then_inc(inv_ok, 1)
                dve.wait_ge(inv_ok, G * TG + (r + 1))
                nc.vector.tensor_scalar(probs[:, gp, r, :], probs[:, gp, r, :], rowinv[:, gp, r:r + 1], None,
                                        ALU.mult).then_inc(norm_ok, 1)

            def split_probs(G, j):
                dve.wait_ge(pT_hi_ok, G * JT + (j + 1))
                nc.vector.tensor_tensor(pT_lo[:, j % 4, :], T[:, j % 2, :], f(pT_hi[:, j % 4, :]),
                                        sub).then_inc(pT_lo_ok, 1)

            def group(b, g, ahead):
                G = b * GB + g
                nxt = 1 - g
                par = (G + 1) % 2 if isinstance(G, int) else (g + 1) % 2
                split_probs(G, 0)
                split_probs(G, 1)
                if ahead:
                    split_query(G + 1, nxt, par)
                if ahead and g == 1:
                    split_ctxT(b + 1)
                split_probs(G, 2)
                split_probs(G, 3)
                for r in range(TG):
                    if ahead:
                        row_max(G + 1, nxt, r, (par + 1 + r) % 2)
                    split_probs(G, r + 4)
                    if ahead:
                        row_scale(G + 1, nxt, r)
                dve.wait_ge(av_ok, G * JT + JT)
                nc.vector.tensor_copy(UT[:, 1, g * HEADS_G:(g + 1) * HEADS_G,
                                         b * NQ:(b + 1) * NQ] if isinstance(b, int) else
                                      UT[:, 1, g * HEADS_G:(g + 1) * HEADS_G, bass.ds(b * NQ, NQ)],
                                      U[:, 1, :].rearrange("p (h q) -> p h q", h=HEADS_G)).then_inc(ut_v, 1)

            split_query(0, 0, 0)
            for r in range(TG):
                row_max(0, 0, r, (1 + r) % 2)
                row_scale(0, 0, r)
            with dve.Fori(0, NB - 1) as b:
                group(b, 0, True)
                group(b, 1, True)
            group(NB - 1, 0, True)
            group(NB - 1, 1, False)

            for n in (1, 3):
                dve.wait_ge(o_mm, n + 1)
                nc.vector.tensor_copy(OT[:, 2 * n:2 * n + 2, :],
                                      S[:, n, :].rearrange("p (r t) -> p r t", r=2)).then_inc(o_v, 1)

            def attention_softmax(s):
                dve.wait_ge(qk_mm, s + 1)
                nc.vector.tensor_tensor(kblk[:, 0, :, :, :],
                                        bc(S[:, 1, 0:TOK].rearrange("p (b q) -> p b q", b=NB), 2, HC),
                                        bc(bc(headmask[:, :], 1, NB), 3, NQ), ALU.mult).then_inc(kb_v, 1)
                dve.wait_ge(v_mm, s + 1)
                dve.wait_ge(vzero, 1)
                nc.vector.tensor_copy(
                    Vblk[NQ:P, :, :, HD:2 * HD],
                    S[NQ:P, 2:4, :].rearrange("p a (b r c e) -> p (a b) r c e", b=2, r=NPAIR, c=2)[:, :, :, 1, :]
                ).then_inc(vb_v, 1)
                for t, src in ((0, T), (1, U)):
                    dve.wait_ge(sc_mm, NT * s + t + 1)
                    sc = src[:, :, :].rearrange("p c (h j) -> p (c h) j", h=HC)
                    link(nc.vector.tensor_reduce(out=nm[:, t, :], in_=sc, axis=AX_X, op=ALU.max))
                    nc.vector.tensor_tensor(E[:, t, :, :], sc, bc(nm[:, t, :], 2, NQ), sub).then_inc(shift_ok, 1)
                for t in range(NT):
                    dve.wait_ge(sexp_ok, NT * s + t + 1)
                    link(nc.vector.tensor_reduce(out=rs[:, t, :], in_=E[:, t, :, :], axis=AX_X, op=ALU.add))
                    link(nc.vector.reciprocal(ri[:, t, :], rs[:, t, :]))
                    nc.vector.tensor_tensor(E[:, t, :, :], E[:, t, :, :], bc(ri[:, t, :], 2, NQ),
                                            ALU.mult).then_inc(snorm_ok, 1)
                for t in range(NT):
                    dve.wait_ge(str_mm, NT * s + t + 1)
                    if s == 0:
                        nc.vector.tensor_tensor(
                            PT[:, t, :, :].rearrange("p r (i q) -> p r i q", i=2),
                            S[:, 2 * t:2 * t + 2, :].rearrange("p a (r i q) -> p (a r) i q", r=4, i=2),
                            bc(biasT[:, :, :], 2, 2), ALU.add).then_inc(pt_v, 1)
                    else:
                        nc.vector.tensor_copy(PT[:, t, 4:8, :], S[:, 2 * t + 1, :].rearrange(
                            "p (r q) -> p r q", r=4)).then_inc(pt_v, 1)

            dve.wait_ge(xb_ok, NT)
            for t in range(NT):
                dve.wait_ge(wo_mm, t + 1)
                link(nc.vector.tensor_tensor(xr[:, t, :], T[:, t, 0:D], xb[:, t, :], ALU.add))
                normalise(NT + t, t, xr[:, t, :], xn[:, t, :]).then_inc(xn_ok, 1)
            attention_softmax(0)
            for t in range(NT):
                dve.wait_ge(ao_mm, t + 1)
                link(normalise(2 * NT + 2 * t, t, T[:, t, 0:D], xn[:, t, :]))
                link(nc.vector.tensor_tensor(xn[:, t, :], xn[:, t, :], vec[:, 1, :], ALU.mult))
                link(nc.vector.tensor_tensor(xn[:, t, :], xn[:, t, :], vec[:, 2, :], ALU.add))
                link(nc.vector.tensor_tensor(xr[:, t, :], xn[:, t, :], xr[:, t, :], ALU.add))
                normalise(2 * NT + 2 * t + 1, t, xr[:, t, :], xin[:, t, :]).then_inc(xn_ok, 1)
            attention_softmax(1)
            for t in range(NT):
                dve.wait_ge(ao_mm, NT + t + 1)
                link(normalise(4 * NT + t, t, T[:, t, 0:D], xn[:, t, :]))
                link(nc.vector.tensor_tensor(xn[:, t, :], xn[:, t, :], vec[:, 3, :], ALU.mult))
                link(nc.vector.tensor_tensor(xn[:, t, :], xn[:, t, :], vec[:, 4, :], ALU.add))
                nc.vector.tensor_tensor(y[:, t, :], xn[:, t, :], xin[:, t, :], ALU.add).then_inc(y_ok, 1)
            dve.wait_ge(yThi_ok, 1)
            nc.vector.tensor_tensor(yT_lo[:, :, :], yT[:, :, :], f(yT_hi[:, :, :]), sub).then_inc(yTlo_ok, 1)

            for t in range(NT):
                dve.wait_ge(lg_mm, t + 1)
                lg, top = small[:, t, 0, :], small[:, t, 2, :]
                link(nc.vector.tensor_copy(lg, T[:, t, 0:NE]))
                link(nc.vector.max(top, lg))
                link(nc.vector.max_index(mx8i[:, t, :], top, lg))
                link(nc.vector.tensor_copy(small[:, t, 3, :], mx8i[:, t, :]))
                nc.vector.tensor_tensor(small[:, t, 1, 1:2], top[:, 1:2], top[:, 0:1], sub).then_inc(gdiff_ok, 1)

            def split_weights(e, i, m):
                for n in range(4):
                    w = slice(n * 512, (n + 1) * 512)
                    dve.wait_ge(w_hi_ok, e * 8 + (4 * m + n + 1))
                    nc.vector.tensor_tensor(Wlo[:, i, m, w], Wraw[:, i, m, w], f(Whi[:, i, m, w]),
                                            sub).then_inc(w_lo_ok, 1)

            for e in range(2):
                for m in range(2):
                    split_weights(e, e, m)
            for t in range(NT):
                dve.wait_ge(gexp_ok, t + 1)
                ex, w12, idx = small[:, t, 1, 0:1], small[:, t, 4, :], small[:, t, 3, :]
                link(nc.vector.tensor_scalar(small[:, t, 5, 0:1], ex, 1.0, None, ALU.add))
                link(nc.vector.reciprocal(w12[:, 0:1], small[:, t, 5, 0:1]))
                link(nc.vector.tensor_tensor(w12[:, 1:2], ex, w12[:, 0:1], ALU.mult))
                for n in range(2):
                    link(nc.vector.tensor_scalar(small[:, t, 6 + n, :], iota8[:, :], idx[:, n:n + 1],
                                                 w12[:, n:n + 1], ALU.is_equal, ALU.mult))
                nc.vector.tensor_tensor(cw[:, t, :], small[:, t, 6, :], small[:, t, 7, :], ALU.add).then_inc(cw_ok, 1)

            def split_hidden(e, i, f2):
                dve.wait_ge(h_hi_ok, e * 4 + (f2 + 1))
                nc.vector.tensor_tensor(hT_lo[:, i, 2 * f2:2 * f2 + 2, :], h32[:, f2, :, :],
                                        f(hT_hi[:, i, 2 * f2:2 * f2 + 2, :]), sub).then_inc(h_lo_ok, 1)

            def combine(e, i):
                dve.wait_ge(eo_mm, e * 4 + 4)
                dve.wait_ge(acc_ok, e * NT + 2 * NT)
                for t in range(NT):
                    c = cw[:, t, e:e + 1] if isinstance(e, int) else cw[:, t, bass.ds(e, 1)]
                    nc.vector.scalar_tensor_tensor(out=acc[:, t, :], in0=(T, U)[i][:, t, 0:D], scalar=c,
                                                   in1=acc[:, t, :], op0=ALU.mult, op1=ALU.add).then_inc(acc_ok, 1)

            for f2 in range(4):
                split_hidden(0, 0, f2)
            dve.wait_ge(cT_mm, 1)
            nc.vector.tensor_copy(cT[:, :].rearrange("p (t q) -> p t q", t=NT), U[0:NE, :, 0:P]).then_inc(cT_ok, 1)
            dve.wait_ge(b2_mm, 1)
            for t in range(NT):
                nc.vector.tensor_copy(acc[:, t, :], U[:, t, 0:D]).then_inc(acc_ok, 2)
            with dve.Fori(0, NE // 2 - 1) as turn:
                e = turn * 2
                for i in range(2):
                    for f2 in range(4):
                        split_hidden(e + (i + 1), 1 - i, f2)
                        if f2 == 0:
                            split_weights(e + (i + 2), i, 0)
                    split_weights(e + (i + 2), i, 1)
                    combine(e + i, i)
            for f2 in range(4):
                split_hidden(NE - 1, 1, f2)
            combine(NE - 2, 0)
            combine(NE - 1, 1)
            dve.wait_ge(res_ok, NT)
            dve.wait_ge(acc_ok, NT * NE + 2 * NT)
            for t in range(NT):
                link(normalise(5 * NT + t, t, acc[:, t, :], xn[:, t, :]))
                link(nc.vector.tensor_tensor(xn[:, t, :], xn[:, t, :], vec[:, 5, :], ALU.mult))
                nc.vector.tensor_tensor(fin[:, t, :], xn[:, t, :], xb[:, t, :], ALU.add).then_inc(fin_ok, 1)

        @block.gpsimd
        def _(pool):
            count = [0]

            def link(ins):
                count[0] += 1
                ins.then_inc(pchain, 1)
                pool.wait_ge(pchain, count[0])

            calls = [0]

            def inverse_deviation(t):
                pool.wait_ge(mv_ok, calls[0] + 1)
                link(nc.gpsimd.tensor_scalar(pw[:, 1:2], mv[:, t, 1:2], EPS, 1.0, ALU.add, ALU.mult))
                nc.gpsimd.tensor_tensor(rstd[:, t:t + 1], pw[:, 1:2], pw[:, 0:1], ALU.pow).then_inc(rstd_ok, 1)
                calls[0] += 1

            nc.gpsimd.memset(pw[:, :], -0.5).then_inc(power_ok, 1)
            pool.wait_ge(power_ok, 1)
            for t in range(NT):
                inverse_deviation(t)
            nc.gpsimd.memset(Qblk[:, :, :, :, :], 0.0).then_inc(qblk_zero, 1)

            def split_ctx(b):
                for j in range(JT):
                    jr = j % (JT // 2)
                    if jr == 0:
                        pool.wait_ge(in_ctx, b * 32 + (16 + 32 * j // JT))
                    if b > 0:
                        pool.wait_ge(av_ok, b * (GB * JT) + (j + 1 - JT))
                    nc.gpsimd.tensor_scalar(ctx_hi[:, j, :], ctx_raw[:, jr, :], 1.0, 1.0, ALU.mult,
                                            ALU.mult).then_inc(ctx_hi_ok, 1)
                    pool.wait_ge(ctx_hi_ok, b * JT + (j + 1))
                    nc.gpsimd.tensor_tensor(ctx_lo[:, j, :], ctx_raw[:, jr, :], f(ctx_hi[:, j, :]),
                                            ALU.subtract).then_inc(ctx_lo_ok, 1)

            for b in range(NB):
                split_ctx(b)
            pool.wait_ge(in_vec, 112)
            for t in range(NT):
                nc.gpsimd.tensor_tensor(xb[:, t, :], xr[:, t, :], vec[:, 0, :], ALU.add).then_inc(xb_ok, 1)
            pool.wait_ge(wo_mm, NT)
            nc.gpsimd.memset(Vblk[:, :, :, :], 0.0).then_inc(vzero, 1)
            for n in range(4 * NT):
                inverse_deviation((0, 1, 0, 0, 1, 1, 0, 1)[n])
            for t in range(NT):
                pool.wait_ge(y_ok, t + 1)
                link(nc.gpsimd.tensor_tensor(xb[:, t, :], xr[:, t, :], y[:, t, :], ALU.add))
                nc.gpsimd.tensor_tensor(xb[:, t, :], xb[:, t, :], vec[:, 6, :], ALU.add).then_inc(res_ok, 1)

            def split_hidden(e, i, f2):
                pool.wait_ge(relu_ok, e * 4 + (f2 + 1))
                if e >= 2:
                    pool.wait_ge(eo_mm, (e - 2) * 4 + (f2 + 1))
                nc.gpsimd.tensor_scalar(hT_hi[:, i, 2 * f2:2 * f2 + 2, :], h32[:, f2, :, :], 1.0, 1.0, ALU.mult,
                                        ALU.mult).then_inc(h_hi_ok, 1)

            for e in range(NE):
                for f2 in range(4):
                    split_hidden(e, e % 2, f2)
            for t in range(NT):
                inverse_deviation(t)


def _layouts(np, x, ctx_1024, L0_xattn_Wq, L0_xattn_Wk, L0_xattn_Wv, L0_xattn_Wo, L0_xattn_bo, L0_attn_Wq,
             L0_attn_Wk, L0_attn_Wv, L0_attn_rel_bias_table, L0_attn_ln_gamma, L0_attn_ln_beta, L0_ffn_Wq,
             L0_ffn_Wk, L0_ffn_Wv, L0_ffn_gate_W, L0_ffn_W1, L0_ffn_b1, L0_ffn_W2, L0_ffn_b2, L0_ffn_ln1_g,
             L0_ffn_ln1_b, L0_ffn_ln2_g, L0_ffn_ln2_b):
    nq = x.shape[1]
    d = x.shape[2]
    p = np.arange(128)
    table = L0_attn_rel_bias_table
    bt = np.stack([table[nq - 1 - j:2 * nq - 1 - j, :].T for j in range(nq)])
    nh = table.shape[1]
    bt = bt.reshape(nq, nh // 2, 2, nq).transpose(2, 0, 1, 3).reshape(2 * nq, nh // 2, nq)
    ne, ff = L0_ffn_b1.shape
    heads = lambda w: w.transpose(1, 0, 2).reshape(d, -1)
    return {
        "x": x, "ctx": ctx_1024, "ctxT": ctx_1024.transpose(0, 2, 1),
        "xattn_Wq": L0_xattn_Wq, "xattn_WkT": L0_xattn_Wk.T, "xattn_Wv": L0_xattn_Wv, "xattn_Wo": L0_xattn_Wo,
        "bo": L0_xattn_bo, "gamma": L0_attn_ln_gamma, "beta": L0_attn_ln_beta, "g1": L0_ffn_ln1_g,
        "b1n": L0_ffn_ln1_b, "g2": L0_ffn_ln2_g, "b2n": L0_ffn_ln2_b,
        "self0_q": L0_attn_Wq.T, "self0_k": L0_attn_Wk.T, "self0_v": L0_attn_Wv.T,
        "self1_q": heads(L0_ffn_Wq), "self1_k": heads(L0_ffn_Wk), "self1_v": heads(L0_ffn_Wv),
        "biasT": bt, "gate": L0_ffn_gate_W, "W1": L0_ffn_W1, "W2": L0_ffn_W2, "b2": L0_ffn_b2,
        "b1": L0_ffn_b1.reshape(ne, ff // 128, 128).transpose(2, 0, 1).reshape(128, -1),
        "ident": np.eye(128, dtype=np.float32),
        "headmask": (p[:, None] // 16 == np.arange(8)[None, :]).astype(np.float32),
        "causal": np.where(np.arange(nq)[None, :] <= (p % nq)[:, None], 0.0, -1e30).astype(np.float32),
        "iota8": np.tile(np.arange(ne, dtype=np.float32), (128, 1)),
    }


def kernel(**inputs):
    import numpy as _np
    import concourse.bacc as _bacc
    from concourse.bass_utils import run_bass_kernel_spmd as _run

    laid = _layouts(_np, **{k: _np.asarray(v) for k, v in inputs.items()})
    laid = {k: _np.ascontiguousarray(v) for k, v in laid.items()}
    nc = _bacc.Bacc("TRN2", target_bir_lowering=False, num_devices=1)
    arrays, args = {}, {}
    for name, v in laid.items():
        arrays[f"in_{name}"] = v
        args[name] = nc.dram_tensor(f"in_{name}", v.shape, mybir.dt.from_np(v.dtype), kind="ExternalInput").ap()
    out = nc.dram_tensor("out_x", laid["x"].shape, F32, kind="ExternalOutput").ap()
    perceiver_block(nc, args, out)
    r = _run(nc, [arrays], core_ids=[0])
    return r.results[0]["out_x"]
```

```python
from contextlib import ExitStack

import concourse.bass as bass
from concourse import mybir

P = 128
ALU = mybir.AluOpType
ACT = mybir.ActivationFunctionType
F32 = mybir.dt.float32
F32R = mybir.dt.float32r
BF16 = mybir.dt.bfloat16
U32 = mybir.dt.uint32
AX_X = mybir.AxisListType.X
EPS = 1e-5


def perceiver_block(nc, a, out):
    NB, NQ, D = a["x"].shape
    NC_ = a["ctx"].shape[1]
    NT = NB * NQ // P
    KD = D // P
    NH = 16
    INNER = a["xattn_Wq"].shape[1]
    DH = INNER // NH
    NPAIR = NH // 2
    HD = D // NH
    HC = P // HD
    JT = NC_ // P
    ROWS = 512
    TG = ROWS // P
    GB = NH * NQ // ROWS
    NG = GB * NB
    NE, _, FF = a["W1"].shape
    FT = FF // P
    TOK = NB * NQ
    XSCALE = float(DH) ** -0.5
    SSCALE = float(D) ** -0.5
    HEADS_G = ROWS // NQ
    assert (NT, KD, NPAIR, JT, TG, GB, FT, TOK) == (2, 2, 8, 8, 4, 2, 8, 256)

    ctx = ExitStack()
    with ctx:
        def sem(name):
            return ctx.enter_context(nc.semaphore(name))

        def halves(name):
            return [sem(f"{name}_{t}") for t in range(NT)]

        def sb(stack, name, shape, dt=F32):
            return stack.enter_context(nc.sbuf_tensor(name, shape, dt))

        S = ctx.enter_context(nc.psum_tensor("S", [P, 4, 512], F32))
        T = ctx.enter_context(nc.psum_tensor("T", [P, 2, 512], F32))
        U = ctx.enter_context(nc.psum_tensor("U", [P, 2, 512], F32))
        front = (S[:, 0:2, :], T[:, :, :])
        back = (S[:, 2:4, :], U[:, :, :])
        query_bank = (S[:, 2, :], S[:, 3, :], T[:, 0, :], T[:, 1, :])

        ident = sb(ctx, "ident", [P, P])
        ident_bf = sb(ctx, "ident_bf", [P, P], BF16)
        headmask = sb(ctx, "headmask", [P, HC])
        causal = sb(ctx, "causal", [P, NQ])
        causal_bf = sb(ctx, "causal_bf", [P, NQ], BF16)
        iota8 = sb(ctx, "iota8", [P, NE])
        pw = sb(ctx, "pw", [P, 1])
        xr = sb(ctx, "xr", [P, NT, D])
        xb = sb(ctx, "xb", [P, NT, D])
        xn = sb(ctx, "xn", [P, NT, D])
        xnT = sb(ctx, "xnT", [P, KD, TOK])
        vec = sb(ctx, "vec", [P, 7, D])
        stats = sb(ctx, "stats", [P, NT, 6])
        mv = sb(ctx, "mv", [P, NT, 3])
        rstd = sb(ctx, "rstd", [P, NT])
        self_w = sb(ctx, "self_w", [P, 2, 3, KD, D])
        gate = sb(ctx, "gate", [P, KD, NE])
        b1T = sb(ctx, "b1T", [P, NE, FT])
        b2 = sb(ctx, "b2", [NE, D])
        biasT = sb(ctx, "biasT", [P, NPAIR, NQ])
        small = sb(ctx, "small", [P, NT, 8, 8])
        mx8i = sb(ctx, "mx8i", [P, NT, 8], U32)
        cw = sb(ctx, "cw", [P, NT, NE])
        cT = sb(ctx, "cT", [NE, TOK])
        negmax = sb(ctx, "negmax", [P, 2, TG])
        rowsum = sb(ctx, "rowsum", [P, 2, TG])
        rowinv = sb(ctx, "rowinv", [P, 2, TG])

        ra = ExitStack()
        ctxT_hi = sb(ra, "ctxT_hi", [P, KD, NC_], F32R)
        ctxT_lo = sb(ra, "ctxT_lo", [P, KD, NC_], F32R)
        qp_hi = sb(ra, "qp_hi", [P, 2, KD, ROWS], F32R)
        qp_lo = sb(ra, "qp_lo", [P, 2, KD, ROWS], F32R)
        WkT = sb(ra, "WkT", [P, NPAIR, D])
        probs = sb(ra, "probs", [P, 2, TG, NC_])
        ctx_hi = sb(ra, "ctx_hi", [P, JT, D], F32R)
        ctx_lo = sb(ra, "ctx_lo", [P, JT, D], F32R)
        ctxT_raw = sb(ra, "ctxT_raw", [P, KD, NC_])
        ctx_raw = sb(ra, "ctx_raw", [P, JT // 2, D])
        pT_hi = sb(ra, "pT_hi", [P, 4, ROWS], F32R)
        pT_lo = sb(ra, "pT_lo", [P, 4, ROWS], F32R)
        Wq = sb(ra, "Wq", [P, KD, INNER])
        Qblk = sb(ra, "Qblk", [P, NB, NPAIR, 2, NQ])
        UT = sb(ra, "UT", [P, KD, NH, TOK])
        Wv = Wq
        OT = Qblk[:, :, :, :, :].rearrange("p b h c q -> p (b h c q)")[:, 0:NPAIR * TOK].rearrange(
            "p (r t) -> p r t", r=NPAIR)
        Wo = ctxT_raw[:, :, :].rearrange("p k n -> p (k n)").rearrange("p (r d) -> p r d", r=NPAIR)
        ra.close()

        rd = ExitStack()
        Vblk = sb(rd, "Vblk", [P, NB, NPAIR, 2, HD + 1])
        qT = sb(rd, "qT", [P, KD, TOK])
        kblk = sb(rd, "kblk", [P, KD, NB, HC, NQ])
        E = sb(rd, "E", [P, NT, NH, NQ])
        PT = sb(rd, "PT", [P, NT, NPAIR, P])
        nm = sb(rd, "nm", [P, NT, NH])
        ri = sb(rd, "ri", [P, NT, NH])
        rd.close()
        rc = ExitStack()
        hT_hi = sb(rc, "hT_hi", [P, 2, FT, TOK], F32R)
        hT_lo = sb(rc, "hT_lo", [P, 2, FT, TOK], F32R)
        h32 = sb(rc, "h32", [P, 4, 2, TOK])
        Wraw = [None, None]
        Wraw[0] = sb(rc, "Wraw_0", [P, 2, KD * FF])
        y = sb(rc, "y", [P, NT, D])
        xin = sb(rc, "xin", [P, NT, D])
        fin = sb(rc, "fin", [P, NT, D])
        acc = sb(rc, "acc", [P, NT, D])
        yT = sb(rc, "yT", [P, KD, TOK])
        yT_hi = sb(rc, "yT_hi", [P, KD, TOK], F32R)
        yT_lo = sb(rc, "yT_lo", [P, KD, TOK], F32R)
        Wraw[1] = sb(rc, "Wraw_1", [P, 2, KD * FF])
        Whi = sb(rc, "Whi", [P, 2, 2, KD * FF], F32R)
        Wlo = sb(rc, "Wlo", [P, 2, 2, KD * FF], F32R)
        rc.close()

        in_x = sem("in_x")
        in_ident = sem("in_ident")
        in_const = sem("in_const")
        in_Wq = sem("in_Wq")
        in_WkT = sem("in_WkT")
        in_vec = sem("in_vec")
        in_ctxT = sem("in_ctxT")
        in_ctx = sem("in_ctx")
        in_Wv = sem("in_Wv")
        in_Wo = sem("in_Wo")
        in_later = sem("in_later")
        in_W1 = [sem(f"in_W1_{i}") for i in range(2)]
        in_W2 = [sem(f"in_W2_{i}") for i in range(2)]
        stored = sem("stored")
        qblk_zero = sem("qblk_zero")
        q_mm = sem("q_mm")
        q_a = sem("q_a")
        q_v = sem("q_v")
        qp_mm = sem("qp_mm")
        qp_hi_ok = sem("qp_hi_ok")
        qp_lo_ok = sem("qp_lo_ok")
        ctxT_hi_ok = sem("ctxT_hi_ok")
        ctxT_lo_ok = sem("ctxT_lo_ok")
        ctx_hi_ok = sem("ctx_hi_ok")
        ctx_lo_ok = sem("ctx_lo_ok")
        sim_ok = sem("sim_ok")
        max_ok = sem("max_ok")
        exp_ok = sem("exp_ok")
        inv_ok = sem("inv_ok")
        norm_ok = sem("norm_ok")
        tr_ok = sem("tr_ok")
        pT_hi_ok = sem("pT_hi_ok")
        pT_lo_ok = sem("pT_lo_ok")
        av_ok = sem("av_ok")
        ut_a = sem("ut_a")
        ut_v = sem("ut_v")
        o_mm = halves("o_mm")
        o_a = halves("o_a")
        o_v = halves("o_v")
        wo_mm = halves("wo_mm")
        xb_ok = sem("xb_ok")
        xbeta_ok = halves("xbeta_ok")
        xb1_ok = halves("xb1_ok")
        mv_ok = sem("mv_ok")
        var_ok = sem("var_ok")
        rstd_ok = sem("rstd_ok")
        xn_ok = halves("xn_ok")
        xnT_mm = halves("xnT_mm")
        xnT_ok = halves("xnT_ok")
        chain = sem("chain")
        pchain = sem("pchain")
        power_ok = sem("power_ok")
        qk_mm = halves("qk_mm")
        v_mm = halves("v_mm")
        sq_ok = halves("sq_ok")
        kb_a = halves("kb_a")
        kb_v = halves("kb_v")
        vzero = sem("vzero")
        vb_a = halves("vb_a")
        vb_v = halves("vb_v")
        sc_mm = halves("sc_mm")
        shift_ok = halves("shift_ok")
        sexp_ok = halves("sexp_ok")
        str_mm = halves("str_mm")
        pt_a = halves("pt_a")
        pt_v = halves("pt_v")
        ao_mm = halves("ao_mm")
        bv_mm = halves("bv_mm")
        cw_ok = sem("cw_ok")
        y_ok = halves("y_ok")
        xin_ok = sem("xin_ok")
        cbf_ok = sem("cbf_ok")
        yT_mm = sem("yT_mm")
        yT_ok = sem("yT_ok")
        yThi_ok = sem("yThi_ok")
        yTlo_ok = sem("yTlo_ok")
        lg_mm = sem("lg_mm")
        gdiff_ok = sem("gdiff_ok")
        gexp_ok = sem("gexp_ok")
        cT_mm = sem("cT_mm")
        cT_ok = sem("cT_ok")
        b2_mm = sem("b2_mm")
        w_hi_ok = sem("w_hi_ok")
        w_lo_ok = sem("w_lo_ok")
        h_mm = sem("h_mm")
        relu_ok = sem("relu_ok")
        h_hi_ok = sem("h_hi_ok")
        h_lo_ok = sem("h_lo_ok")
        eo_mm = sem("eo_mm")
        acc_ok = sem("acc_ok")
        res_ok = sem("res_ok")
        fin_ok = sem("fin_ok")

        def f(t):
            return t.bitcast(F32)

        def bc(t, dim, n):
            t = t.unsqueeze(dim)
            return t.broadcast_to([*t.shape[:dim], n, *t.shape[dim + 1:]])

        ctx_v = a["ctx"].rearrange("b (j p) d -> b p j d", p=P)
        ctxT_v = a["ctxT"].rearrange("b (k p) n -> b p k n", p=P)
        W1_v = a["W1"].rearrange("e (k p) f -> e p k f", p=P)
        W2_v = a["W2"].rearrange("e (f p) d -> e p f d", p=P)
        x_v = a["x"].rearrange("b q d -> (b q) d").rearrange("(t p) d -> p t d", p=P)
        out_v = out.rearrange("b q d -> (b q) d").rearrange("(t p) d -> p t d", p=P)

        block = ctx.enter_context(nc.Block())

        @block.sync
        def _(sp):
            sp.dma_start(xr[:, :, :], x_v).then_inc(in_x, 16)
            sp.dma_start(ident[:, :], a["ident"]).then_inc(in_ident, 16)
            for dst, name in ((headmask, "headmask"), (causal, "causal"), (iota8, "iota8")):
                sp.dma_start(dst[:, :], a[name]).then_inc(in_const, 16)
            sp.dma_start(Wq[:, :, :], a["xattn_Wq"].rearrange("(k p) n -> p k n", p=P)).then_inc(in_Wq, 16)
            sp.dma_start(WkT[:, :, :], a["xattn_WkT"].rearrange("(r p) d -> p r d", p=P)).then_inc(in_WkT, 16)
            sp.dma_start(ctxT_raw[:, :, :], ctxT_v[0]).then_inc(in_ctxT, 16)
            sp.dma_start(ctx_raw[:, :, :], ctx_v[0][:, 0:JT // 2, :]).then_inc(in_ctx, 16)
            for i, name in enumerate(("bo", "gamma", "beta", "g1", "b1n", "g2", "b2n")):
                sp.dma_start(vec[:, i, :], a[name].partition_broadcast(P)).then_inc(in_vec, 16)
            sp.wait_ge(q_mm, 4)
            sp.dma_start(Wv[:, :, :], a["xattn_Wv"].rearrange("(k p) n -> p k n", p=P)).then_inc(in_Wv, 16)
            for s in range(2):
                for i, name in enumerate(("q", "k", "v")):
                    sp.dma_start(self_w[:, s, i, :, :],
                                 a[f"self{s}_{name}"].rearrange("(k p) n -> p k n", p=P)).then_inc(in_later, 16)
            sp.dma_start(gate[:, :, :], a["gate"].rearrange("(k p) n -> p k n", p=P)).then_inc(in_later, 16)
            sp.dma_start(b1T[:, :, :], a["b1"].rearrange("p (e f) -> p e f", e=NE)).then_inc(in_later, 16)
            sp.dma_start(b2[:, :], a["b2"]).then_inc(in_later, 16)
            sp.dma_start(biasT[:, :, :], a["biasT"]).then_inc(in_later, 16)
            sp.wait_ge(ctx_lo_ok, JT // 2)
            sp.dma_start(ctx_raw[:, :, :], ctx_v[0][:, JT // 2:JT, :]).then_inc(in_ctx, 16)
            with sp.Fori(0, NB - 1) as b:
                sp.wait_ge(ctxT_lo_ok, b * 4 + 4)
                sp.dma_start(ctxT_raw[:, :, :], ctxT_v[bass.ds(b + 1, 1)].rearrange("o p k n -> p (o k) n")
                             ).then_inc(in_ctxT, 16)
                for half in range(2):
                    sp.wait_ge(ctx_lo_ok, b * JT + JT + half * (JT // 2))
                    sp.dma_start(ctx_raw[:, :, :],
                                 ctx_v[bass.ds(b + 1, 1), :, half * (JT // 2):(half + 1) * (JT // 2), :].rearrange(
                                     "o p j d -> p (o j) d")).then_inc(in_ctx, 16)
            sp.wait_ge(ctxT_lo_ok, 4 * NB)
            sp.dma_start(Wo, a["xattn_Wo"].rearrange("(r p) d -> p r d", p=P)).then_inc(in_Wo, 16)
            def load_expert(i, e, m):
                src = (W1_v, W2_v)[m]
                src = src[e] if isinstance(e, int) else src[bass.ds(e, 1)].rearrange("o p k n -> p (o k) n")
                sp.dma_start(Wraw[i][:, m, :].rearrange("p (k n) -> p k n", k=(KD, FT)[m]), src
                             ).then_inc((in_W1, in_W2)[m][i], 16)

            sp.wait_ge(tr_ok, (NG - 1) * JT)
            for m in range(2):
                load_expert(0, 0, m)
            sp.wait_ge(wo_mm[0], 1)
            sp.wait_ge(wo_mm[1], 1)
            for m in range(2):
                load_expert(1, 1, m)
            with sp.Fori(0, NE // 2 - 1) as turn:
                e = turn * 2
                for i in range(2):
                    sp.wait_ge(w_lo_ok, (e + i) * 8 + 4)
                    load_expert(i, e + (i + 2), 0)
                    sp.wait_ge(w_lo_ok, (e + i) * 8 + 8)
                    load_expert(i, e + (i + 2), 1)
            for t in range(NT):
                sp.wait_ge(fin_ok, t + 1)
                sp.dma_start(out_v[:, t, :], fin[:, t, :]).then_inc(stored, 16)
            sp.wait_ge(stored, 16 * NT)

        @block.tensor
        def _(pe):
            mm = nc.tensor.matmul

            def passes3(dst, l_hi, l_lo, r_hi, r_lo, start, stop):
                mm(dst, l_hi, r_hi, start=start, stop=False)
                mm(dst, l_hi, r_lo, start=False, stop=False)
                return mm(dst, l_lo, r_hi, start=False, stop=stop)

            def transpose_rows(t, src, dst, ready):
                for k in range(KD):
                    last = nc.tensor.transpose(dst[:, k * P:(k + 1) * P], src[:, t, k * P:(k + 1) * P], ident[:, :])
                last.then_inc(ready, 1)

            def absorbed_query(g, b, par):
                for k in range(KD):
                    for r in range(TG):
                        pair = TG * g + r
                        last = mm(S[:, 2 * par + k, r * P:(r + 1) * P], WkT[:, pair, k * P:(k + 1) * P],
                                  Qblk[:, b, pair, :, :] if isinstance(b, int) else
                                  Qblk[:, bass.ds(b, 1), pair, :, :].rearrange("p o c q -> p (o c) q"),
                                  start=True, stop=True)
                last.then_inc(qp_mm, 1)

            def scores(gp, r, par, half):
                for k in range(KD):
                    last = passes3(S[:, 2 * par + half, :], qp_hi[:, gp, k, r * P:(r + 1) * P],
                                   qp_lo[:, gp, k, r * P:(r + 1) * P],
                                   ctxT_hi[:, k, half * 512:(half + 1) * 512],
                                   ctxT_lo[:, k, half * 512:(half + 1) * 512], k == 0, k == KD - 1)
                if half == 1:
                    last.then_inc(sim_ok, 1)

            def transpose_probs(gp, j):
                for r in range(TG):
                    last = nc.tensor.transpose(T[:, j % 2, r * P:(r + 1) * P], probs[:, gp, r, j * P:(j + 1) * P],
                                               ident[:, :])
                last.then_inc(tr_ok, 1)

            def attend(G, b, j):
                pe.wait_ge(pT_lo_ok, G * JT + (j + 1))
                pe.wait_ge(ctx_lo_ok, b * JT + (j + 1))
                if j == 0:
                    pe.wait_ge(ut_a, G + 1)
                    pe.wait_ge(ut_v, G + 1)
                for k in range(KD):
                    last = passes3(U[:, k, :], ctx_hi[:, j, k * P:(k + 1) * P], ctx_lo[:, j, k * P:(k + 1) * P],
                                   pT_hi[:, j % 4, :], pT_lo[:, j % 4, :], j == 0, j == JT - 1)
                last.then_inc(av_ok, 1)

            def group(b, g, ahead):
                G = b * GB + g
                gp, nxt, nb = g, 1 - g, b + g
                par = (G + 1) % 2 if isinstance(G, int) else (g + 1) % 2
                pe.wait_ge(norm_ok, G * TG + TG)
                transpose_probs(gp, 0)
                transpose_probs(gp, 1)
                if ahead:
                    absorbed_query(nxt, nb, par)
                attend(G, b, 0)
                transpose_probs(gp, 2)
                attend(G, b, 1)
                for r in range(TG):
                    transpose_probs(gp, r + 3)
                    if ahead:
                        if r == 0:
                            pe.wait_ge(qp_lo_ok, G + 2)
                            pe.wait_ge(ctxT_lo_ok, nb * 4 + 2)
                        if r >= 2:
                            pe.wait_ge(exp_ok, G * TG + (TG + r - 1))
                        scores(nxt, r, (par + 1 + r) % 2, 0)
                        if r == 0:
                            pe.wait_ge(ctxT_lo_ok, nb * 4 + 4)
                        scores(nxt, r, (par + 1 + r) % 2, 1)
                    attend(G, b, r + 2)
                transpose_probs(gp, 7)
                attend(G, b, 6)
                attend(G, b, 7)

            pe.wait_ge(in_ident, 16)
            for n in range(10):
                mm(U[:, 0, 0:P], ident[:, :], ident[:, :], start=True, stop=True)
            for t in range(NT):
                pe.wait_ge(xn_ok[t], 1)
                transpose_rows(t, xn, T[:, t, :], xnT_mm[t])
            pe.wait_ge(in_Wq, 16)
            for t in range(NT):
                pe.wait_ge(xnT_ok[t], 1)

            def queries(n):
                for i in range(2):
                    pair = 2 * n + i
                    for k in range(KD):
                        last = mm(query_bank[n][:, i * TOK:(i + 1) * TOK], Wq[:, k, pair * P:(pair + 1) * P],
                                  xnT[:, k, :], start=(k == 0), stop=(k == KD - 1))
                last.then_inc(q_mm, 1)

            queries(0)
            queries(1)
            pe.wait_ge(in_WkT, 16)
            pe.wait_ge(q_a, 2)
            pe.wait_ge(q_v, 2)
            absorbed_query(0, 0, 0)
            queries(2)
            queries(3)
            pe.wait_ge(qp_lo_ok, 1)
            pe.wait_ge(ctxT_lo_ok, 2)
            for r in range(TG):
                if r >= 2:
                    pe.wait_ge(exp_ok, r - 1)
                scores(0, r, (1 + r) % 2, 0)
                if r == 0:
                    pe.wait_ge(ctxT_lo_ok, 4)
                scores(0, r, (1 + r) % 2, 1)
            pe.wait_ge(q_a, 4)
            pe.wait_ge(q_v, 4)
            with pe.Fori(0, NB - 1) as b:
                group(b, 0, True)
                group(b, 1, True)
            group(NB - 1, 0, True)

            def heads_T(t):
                pe.wait_ge(in_Wv, 16)
                pe.wait_ge(ut_a, (t + 1) * NG // 2 + 1)
                pe.wait_ge(ut_v, (t + 1) * NG // 2 + 1)
                for h in range(NH):
                    pair, c = h // 2, h % 2
                    for k in range(KD):
                        last = mm(front[t][c * DH:(c + 1) * DH, pair // 4, (pair % 4) * P:(pair % 4 + 1) * P],
                                  Wv[:, k, h * DH:(h + 1) * DH], UT[:, k, h, t * P:(t + 1) * P],
                                  start=(k == 0), stop=(k == KD - 1))
                    if h % 8 == 7:
                        last.then_inc(o_mm[t], 1)

            def out_product(t):
                pe.wait_ge(in_Wo, 16)
                pe.wait_ge(o_a[t], 1)
                pe.wait_ge(o_v[t], 1)
                for pair in range(NPAIR):
                    last = mm(back[t][:, 0, 0:D], OT[:, pair, t * P:(t + 1) * P], Wo[:, pair, :],
                              start=(pair == 0), stop=(pair == NPAIR - 1))
                last.then_inc(wo_mm[t], 1)

            def rows_T(s, t):
                pe.wait_ge(xn_ok[t], s + 2)
                transpose_rows(t, xn if s == 0 else xin, back[t][:, 1, :], xnT_mm[t])

            def projections(s, t):
                if s == 0 and t == 0:
                    pe.wait_ge(in_later, 160)
                pe.wait_ge(xnT_ok[t], s + 2)
                tok = slice(t * P, (t + 1) * P)
                for i in range(2):
                    for c in range(KD):
                        for k in range(KD):
                            dst = back[t][:, 0, 0:P] if (i, c) == (1, 0) else \
                                front[t][:, 0, (i + c) * P:(i + c + 1) * P]
                            last = mm(dst, self_w[:, s, i, k, c * P:(c + 1) * P], xnT[:, k, tok],
                                      start=(k == 0), stop=(k == KD - 1))
                last.then_inc(qk_mm[t], 1)
                for i in range(2):
                    b = 2 * t + i
                    for k in range(KD):
                        for c in range(2):
                            last = mm(front[t][c * NQ:(c + 1) * NQ, 1, i * D:(i + 1) * D],
                                      xnT[:, k, b * NQ:(b + 1) * NQ], self_w[:, s, 2, k, :],
                                      start=(k == 0), stop=(k == KD - 1), skip_group_check=True)
                last.then_inc(v_mm[t], 1)

            def self_scores(s, t):
                pe.wait_ge(sq_ok[t], s + 1)
                for c in range(KD):
                    pe.wait_ge((kb_v, kb_a)[c][t], s + 1)
                    if s == 1:
                        pe.wait_ge(cbf_ok, 1)
                        mm(back[t][:, c, :], ident_bf[:, :], bc(causal_bf[:, :], 1, HC), start=True, stop=False,
                           skip_group_check=True)
                    for i in range(2):
                        b = 2 * t + i
                        last = mm(back[t][i * NQ:(i + 1) * NQ, c, :], qT[:, c, b * NQ:(b + 1) * NQ],
                                  kblk[:, c, b, :, :], start=(s == 0), stop=True, skip_group_check=True)
                last.then_inc(sc_mm[t], 1)

            def transpose_exps(s, t):
                pe.wait_ge(vb_a[t], s + 1)
                pe.wait_ge(vb_v[t], s + 1)
                pe.wait_ge(sexp_ok[t], s + 1)
                for pair in range(NPAIR):
                    last = nc.tensor.transpose(front[t][:, pair // 4, (pair % 4) * P:(pair % 4 + 1) * P],
                                               E[:, t, 2 * pair:2 * pair + 2, :], ident[:, :])
                last.then_inc(str_mm[t], 1)

            def times_v(t, n, weights):
                for i in range(2):
                    for pair in range(NPAIR):
                        w = slice(pair * 2 * (HD + 1), (pair + 1) * 2 * (HD + 1))
                        last = mm(back[t][i * NQ:(i + 1) * NQ, n, w], weights(i, pair),
                                  Vblk[:, 2 * t + i, pair, :, :], start=True, stop=True, skip_group_check=True)
                return last

            def bias_product(t):
                times_v(t, 1, lambda i, pair: biasT[:, pair, :]).then_inc(bv_mm[t], 1)

            def self_out(s, t):
                pe.wait_ge(pt_a[t], s + 1)
                pe.wait_ge(pt_v[t], s + 1)
                times_v(t, 0, lambda i, pair: PT[:, t, pair, i * NQ:(i + 1) * NQ]).then_inc(ao_mm[t], 1)

            def y_T(t):
                pe.wait_ge(y_ok[t], 1)
                transpose_rows(t, y, back[t][:, 1, :], yT_mm)

            G = NG - 1
            pe.wait_ge(norm_ok, G * TG + TG)
            transpose_probs(1, 0)
            transpose_probs(1, 1)
            heads_T(0)
            attend(G, NB - 1, 0)
            transpose_probs(1, 2)
            attend(G, NB - 1, 1)
            transpose_probs(1, 3)
            attend(G, NB - 1, 2)
            out_product(0)
            transpose_probs(1, 4)
            attend(G, NB - 1, 3)
            transpose_probs(1, 5)
            attend(G, NB - 1, 4)
            rows_T(0, 0)
            transpose_probs(1, 6)
            attend(G, NB - 1, 5)
            projections(0, 0)
            transpose_probs(1, 7)
            attend(G, NB - 1, 6)
            attend(G, NB - 1, 7)

            self_scores(0, 0)
            heads_T(1)
            transpose_exps(0, 0)
            out_product(1)
            bias_product(0)
            self_out(0, 0)
            rows_T(0, 1)
            projections(0, 1)
            rows_T(1, 0)
            self_scores(0, 1)
            projections(1, 0)
            transpose_exps(0, 1)
            bias_product(1)
            self_out(0, 1)
            self_scores(1, 0)
            rows_T(1, 1)
            projections(1, 1)
            transpose_exps(1, 0)
            self_scores(1, 1)
            self_out(1, 0)
            transpose_exps(1, 1)
            self_out(1, 1)
            y_T(0)
            y_T(1)

            def hidden(e, i, f2):
                if f2 == 0:
                    pe.wait_ge(w_lo_ok, e * 8 + 4)
                if not isinstance(e, int) or e > 0:
                    pe.wait_ge(relu_ok, (e - 1) * 4 + (f2 + 1))
                for ft in (2 * f2, 2 * f2 + 1):
                    for k in range(KD):
                        w = slice(k * FF + ft * P, k * FF + (ft + 1) * P)
                        last = passes3(S[:, f2, (ft % 2) * TOK:(ft % 2 + 1) * TOK], Whi[:, i, 0, w], Wlo[:, i, 0, w],
                                       yT_hi[:, k, :], yT_lo[:, k, :], k == 0, k == KD - 1)
                last.then_inc(h_mm, 1)

            def expert_out(e, i, f2):
                dst = (T, U)[i]
                pe.wait_ge(h_lo_ok, e * 4 + (f2 + 1))
                if f2 == 0:
                    pe.wait_ge(w_lo_ok, e * 8 + 8)
                    pe.wait_ge(acc_ok, e * NT + NT)
                for t in range(NT):
                    for ft in (2 * f2, 2 * f2 + 1):
                        w = slice(ft * D, (ft + 1) * D)
                        l_hi = hT_hi[:, i, ft, t * P:(t + 1) * P]
                        l_lo = hT_lo[:, i, ft, t * P:(t + 1) * P]
                        last = passes3(dst[:, t, 0:D], l_hi, l_lo, Whi[:, i, 1, w], Wlo[:, i, 1, w],
                                       ft == 0, ft == FT - 1)
                last.then_inc(eo_mm, 1)

            pe.wait_ge(yTlo_ok, NT)
            hidden(0, 0, 0)
            hidden(0, 0, 1)
            pe.wait_ge(yT_ok, NT)
            for t in range(NT):
                for k in range(KD):
                    last = mm(U[:, t, 0:NE], yT[:, k, t * P:(t + 1) * P], gate[:, k, :],
                              start=(k == 0), stop=(k == KD - 1))
                last.then_inc(lg_mm, 1)
            hidden(0, 0, 2)
            hidden(0, 0, 3)
            with pe.Fori(0, NE // 2 - 1) as turn:
                e = turn * 2
                for f2 in range(4):
                    hidden(e + 1, 1, f2)
                    expert_out(e, 0, f2)
                pe.wait_ge(cw_ok, NT)
                for f2 in range(4):
                    hidden(e + 2, 0, f2)
                    expert_out(e + 1, 1, f2)
            for f2 in range(4):
                hidden(NE - 1, 1, f2)
                expert_out(NE - 2, 0, f2)
            pe.wait_ge(cw_ok, NT)
            pe.wait_ge(relu_ok, NE * 4)
            for t in range(NT):
                last = nc.tensor.transpose(S[0:NE, 0, t * P:(t + 1) * P], cw[:, t, :], ident[:, :])
            last.then_inc(cT_mm, 1)
            expert_out(NE - 1, 1, 0)
            pe.wait_ge(cT_ok, 1)
            for t in range(NT):
                last = mm(S[:, 1, t * D:(t + 1) * D], cT[:, t * P:(t + 1) * P], b2[:, :], start=True, stop=True)
            last.then_inc(b2_mm, 1)
            for f2 in range(1, 4):
                expert_out(NE - 1, 1, f2)

        @block.scalar
        def _(act):
            def copy(dst, src, scale=1.0):
                return nc.scalar.activation(dst, src, ACT.Copy, scale=scale)

            def rows_T(stage, t, src):
                act.wait_ge(xnT_mm[t], stage + 1)
                copy(xnT[:, :, t * P:(t + 1) * P],
                     src[:, 0:D].rearrange("p (k q) -> p k q", k=KD)).then_inc(xnT_ok[t], 1)

            act.sem_inc(ut_a, 1)
            for t in range(NT):
                rows_T(0, t, T[:, t, :])
            act.wait_ge(qblk_zero, 1)

            def queries(n):
                act.wait_ge(q_mm, n + 1)
                copy(Qblk[0:DH, :, 2 * n:2 * n + 2, 0, :].rearrange("p b r q -> p r b q"),
                     query_bank[n][0:DH, :].rearrange("p (r b q) -> p r b q", r=2, b=NB)).then_inc(q_a, 1)

            for n in range(2):
                queries(n)

            def split_query(G, gp, par):
                act.wait_ge(qp_mm, G + 1)
                copy(qp_hi[:, gp, :, :], S[:, 2 * par:2 * par + 2, :], XSCALE).then_inc(qp_hi_ok, 1)

            def split_ctxT(b, pieces=range(4)):
                act.wait_ge(in_ctxT, b * 16 + 16)
                if not isinstance(b, int) or b > 0:
                    act.wait_ge(sim_ok, b * (GB * TG))
                for n in pieces:
                    k, c = n % 2, n // 2
                    copy(ctxT_hi[:, k, c * 512:(c + 1) * 512],
                         ctxT_raw[:, k, c * 512:(c + 1) * 512]).then_inc(ctxT_hi_ok, 1)

            def exponentials(G, gp, r, par):
                act.wait_ge(max_ok, G * TG + (r + 1))
                nc.scalar.activation(probs[:, gp, r, :], S[:, 2 * par:2 * par + 2, :].rearrange("p a n -> p (a n)"),
                                     ACT.Exp, bias=negmax[:, gp, r:r + 1],
                                     accum_out=rowsum[:, gp, r:r + 1]).then_inc(exp_ok, 1)

            def split_probs(G, j):
                act.wait_ge(tr_ok, G * JT + (j + 1))
                copy(pT_hi[:, j % 4, :], T[:, j % 2, :]).then_inc(pT_hi_ok, 1)

            def group(b, g, ahead):
                G = b * GB + g
                nxt = 1 - g
                par = (G + 1) % 2 if isinstance(G, int) else (g + 1) % 2
                split_probs(G, 0)
                split_probs(G, 1)
                if ahead:
                    split_query(G + 1, nxt, par)
                if ahead and g == 1:
                    split_ctxT(b + 1)
                split_probs(G, 2)
                split_probs(G, 3)
                for r in range(TG):
                    if r < 3:
                        if ahead:
                            exponentials(G + 1, nxt, r, (par + 1 + r) % 2)
                        split_probs(G, r + 4)
                    else:
                        split_probs(G, 7)
                        if ahead:
                            exponentials(G + 1, nxt, r, (par + 1 + r) % 2)
                act.wait_ge(av_ok, G * JT + JT)
                copy(UT[:, 0, g * HEADS_G:(g + 1) * HEADS_G,
                        b * NQ:(b + 1) * NQ] if isinstance(b, int) else
                     UT[:, 0, g * HEADS_G:(g + 1) * HEADS_G, bass.ds(b * NQ, NQ)],
                     U[:, 0, :].rearrange("p (h q) -> p h q", h=HEADS_G)).then_inc(ut_a, 1)

            split_ctxT(0, range(2))
            split_query(0, 0, 0)
            split_ctxT(0, range(2, 4))
            queries(2)
            queries(3)
            for r in range(TG):
                exponentials(0, 0, r, (1 + r) % 2)
            with act.Fori(0, NB - 1) as b:
                group(b, 0, True)
                group(b, 1, True)
            group(NB - 1, 0, True)

            def heads_T(t):
                act.wait_ge(o_mm[t], 1)
                copy(OT[:, 0:4, t * P:(t + 1) * P],
                     front[t][:, 0, :].rearrange("p (r t) -> p r t", r=4)).then_inc(o_a[t], 1)

            def split_weights(e, i, m):
                n16 = (e - i) * 8 + 16 if not isinstance(e, int) else (e // 2) * 16 + 16
                act.wait_ge((in_W1, in_W2)[m][i], n16)
                if isinstance(e, int) and e == 0 and m == 0:
                    act.wait_ge(wo_mm[1], 1)
                if not isinstance(e, int) or e >= 2:
                    if m == 0:
                        act.wait_ge(h_mm, (e - 1) * 4)
                    else:
                        act.wait_ge(eo_mm, (e - 1) * 4)
                for n in range(4):
                    copy(Whi[:, i, m, n * 512:(n + 1) * 512], Wraw[i][:, m, n * 512:(n + 1) * 512]
                         ).then_inc(w_hi_ok, 1)

            def query_T(s, t):
                act.wait_ge(qk_mm[t], s + 1)
                copy(qT[:, :, t * P:(t + 1) * P],
                     front[t][:, 0, 0:TOK].rearrange("p (c t) -> p c t", c=KD)).then_inc(sq_ok[t], 1)

            def keys_values(s, t):
                for h in range(HC):
                    last = copy(kblk[:, 1, 2 * t:2 * t + 2, h, :],
                                front[t][:, 0, 2 * P:3 * P].rearrange("p (b q) -> p b q", b=2), headmask[:, h:h + 1])
                last.then_inc(kb_a[t], 1)
                act.wait_ge(v_mm[t], s + 1)
                act.wait_ge(vzero, 3)
                copy(Vblk[0:NQ, 2 * t:2 * t + 2, :, 0, 0:HD],
                     front[t][0:NQ, 1, :].rearrange("p (b r c e) -> p b r c e", b=2, r=NPAIR, c=2)[:, :, :, 0, :]
                     ).then_inc(vb_a[t], 1)

            def self_exp(s, t):
                act.wait_ge(shift_ok[t], s + 1)
                nc.scalar.activation(E[:, t, :, :], E[:, t, :, :], ACT.Exp, scale=SSCALE).then_inc(sexp_ok[t], 1)

            def exps_T(s, t):
                act.wait_ge(str_mm[t], s + 1)
                copy(PT[:, t, 0:4, :], front[t][:, 0, :].rearrange("p (r q) -> p r q", r=4)).then_inc(pt_a[t], 1)

            G = NG - 1
            split_probs(G, 0)
            split_probs(G, 1)
            heads_T(0)
            for j in range(2, 6):
                split_probs(G, j)
            rows_T(1, 0, back[0][:, 1, :])
            split_probs(G, 6)
            query_T(0, 0)
            split_probs(G, 7)
            keys_values(0, 0)
            act.wait_ge(av_ok, G * JT + JT)
            copy(UT[:, 0, HEADS_G:2 * HEADS_G, (NB - 1) * NQ:NB * NQ],
                 U[:, 0, :].rearrange("p (h q) -> p h q", h=HEADS_G)).then_inc(ut_a, 1)

            self_exp(0, 0)
            heads_T(1)
            exps_T(0, 0)
            split_weights(0, 0, 0)
            rows_T(1, 1, back[1][:, 1, :])
            query_T(0, 1)
            keys_values(0, 1)
            rows_T(2, 0, back[0][:, 1, :])
            self_exp(0, 1)
            query_T(1, 0)
            exps_T(0, 1)
            keys_values(1, 0)
            split_weights(0, 0, 1)
            rows_T(2, 1, back[1][:, 1, :])
            self_exp(1, 0)
            query_T(1, 1)
            keys_values(1, 1)
            exps_T(1, 0)
            split_weights(1, 1, 0)
            self_exp(1, 1)
            exps_T(1, 1)
            split_weights(1, 1, 1)

            def relu(e, i, f2):
                act.wait_ge(h_mm, e * 4 + (f2 + 1))
                if not isinstance(e, int) or e > 0:
                    act.wait_ge(h_lo_ok, (e - 1) * 4 + (f2 + 1))
                for c in range(2):
                    ft = 2 * f2 + c
                    bias = b1T[:, e, ft:ft + 1] if isinstance(e, int) else b1T[:, bass.ds(e, 1), ft]
                    last = nc.scalar.activation(h32[:, f2, c, :], S[:, f2, c * TOK:(c + 1) * TOK], ACT.Relu,
                                                bias=bias)
                last.then_inc(relu_ok, 1)

            for t in range(NT):
                act.wait_ge(yT_mm, t + 1)
                copy(yT_hi[:, :, t * P:(t + 1) * P],
                     back[t][:, 1, 0:D].rearrange("p (k q) -> p k q", k=KD)).then_inc(yThi_ok, 1)
            for t in range(NT):
                act.wait_ge(yTlo_ok, t + 1)
                copy(yT[:, :, t * P:(t + 1) * P],
                     back[t][:, 1, 0:D].rearrange("p (k q) -> p k q", k=KD)).then_inc(yT_ok, 1)
            relu(0, 0, 0)
            relu(0, 0, 1)
            for t in range(NT):
                act.wait_ge(gdiff_ok, t + 1)
                nc.scalar.activation(small[:, t, 1, 0:1], small[:, t, 1, 1:2], ACT.Exp).then_inc(gexp_ok, 1)
            relu(0, 0, 2)
            relu(0, 0, 3)
            with act.Fori(0, NE // 2 - 1) as turn:
                e = turn * 2
                for i in range(2):
                    for f2 in range(4):
                        relu(e + (i + 1), 1 - i, f2)
                        if f2 == 0:
                            split_weights(e + (i + 2), i, 0)
                    split_weights(e + (i + 2), i, 1)
            for f2 in range(4):
                relu(NE - 1, 1, f2)
            act.wait_ge(cT_mm, 1)
            copy(cT[:, :], S[0:NE, 0, 0:TOK]).then_inc(cT_ok, 1)

        @block.vector
        def _(dve):
            count = [0]

            def link(ins):
                count[0] += 1
                ins.then_inc(chain, 1)
                dve.wait_ge(chain, count[0])

            sub = ALU.subtract

            def statistics(t, src):
                link(nc.vector.bn_stats(stats[:, t, :], src))
                link(nc.vector.bn_aggr(mv[:, t, 0:2], stats[:, t, :]))
                nc.vector.tensor_scalar(mv[:, t, 2:3], mv[:, t, 1:2], EPS, None, ALU.add).then_inc(mv_ok, 1)

            def centred(n, t, src, dst):
                dve.wait_ge(rstd_ok, n + 1)
                return nc.vector.tensor_scalar(dst, src, mv[:, t, 0:1], rstd[:, t:t + 1], sub, ALU.mult)

            def scaled_residual(n, t, src, scale, dst):
                link(nc.vector.scalar_tensor_tensor(out=src, in0=src, scalar=mv[:, t, 0:1], in1=scale, op0=sub,
                                                    op1=ALU.mult))
                dve.wait_ge(rstd_ok, n + 1)
                return nc.vector.scalar_tensor_tensor(out=dst, in0=src, scalar=rstd[:, t:t + 1], in1=xb[:, t, :],
                                                      op0=ALU.mult, op1=ALU.add)

            dve.sem_inc(ut_v, 1)
            dve.wait_ge(in_x, 16)
            for t in range(NT):
                statistics(t, xr[:, t, :])
            for t in range(NT):
                centred(t, t, xr[:, t, :], xn[:, t, :]).then_inc(xn_ok[t], 1)
            dve.wait_ge(in_const, 48)
            nc.vector.tensor_copy(ident_bf[:, :], ident[:, :])
            nc.vector.tensor_copy(causal_bf[:, :], causal[:, :]).then_inc(cbf_ok, 1)

            def split_ctxT(b, pieces=range(4)):
                for n in pieces:
                    k, c = n % 2, n // 2
                    w = slice(c * 512, (c + 1) * 512)
                    dve.wait_ge(ctxT_hi_ok, b * 4 + (n + 1))
                    nc.vector.tensor_tensor(ctxT_lo[:, k, w], ctxT_raw[:, k, w], f(ctxT_hi[:, k, w]),
                                            sub).then_inc(ctxT_lo_ok, 1)

            dve.wait_ge(qblk_zero, 1)

            def queries(n):
                dve.wait_ge(q_mm, n + 1)
                nc.vector.tensor_copy(Qblk[DH:P, :, 2 * n:2 * n + 2, 1, :].rearrange("p b r q -> p r b q"),
                                      query_bank[n][DH:P, :].rearrange("p (r b q) -> p r b q", r=2, b=NB)
                                      ).then_inc(q_v, 1)

            def split_query(G, gp, par):
                dve.wait_ge(qp_hi_ok, G + 1)
                nc.vector.scalar_tensor_tensor(out=qp_lo[:, gp, :, :], in0=S[:, 2 * par:2 * par + 2, :],
                                               scalar=XSCALE, in1=f(qp_hi[:, gp, :, :]), op0=ALU.mult,
                                               op1=sub).then_inc(qp_lo_ok, 1)

            def row_max(G, gp, r, par):
                dve.wait_ge(sim_ok, G * TG + (r + 1))
                nc.vector.tensor_reduce(out=negmax[:, gp, r:r + 1],
                                        in_=S[:, 2 * par:2 * par + 2, :].rearrange("p a n -> p (a n)"),
                                        axis=AX_X, op=ALU.max, negate=True).then_inc(max_ok, 1)

            def row_scale(G, gp, r):
                dve.wait_ge(exp_ok, G * TG + (r + 1))
                nc.vector.reciprocal(rowinv[:, gp, r:r + 1], rowsum[:, gp, r:r + 1]).then_inc(inv_ok, 1)
                dve.wait_ge(inv_ok, G * TG + (r + 1))
                nc.vector.tensor_scalar(probs[:, gp, r, :], probs[:, gp, r, :], rowinv[:, gp, r:r + 1], None,
                                        ALU.mult).then_inc(norm_ok, 1)

            def split_probs(G, j):
                dve.wait_ge(pT_hi_ok, G * JT + (j + 1))
                nc.vector.tensor_tensor(pT_lo[:, j % 4, :], T[:, j % 2, :], f(pT_hi[:, j % 4, :]),
                                        sub).then_inc(pT_lo_ok, 1)

            def group(b, g, ahead):
                G = b * GB + g
                nxt = 1 - g
                par = (G + 1) % 2 if isinstance(G, int) else (g + 1) % 2
                split_probs(G, 0)
                split_probs(G, 1)
                if ahead:
                    split_query(G + 1, nxt, par)
                if ahead and g == 1:
                    split_ctxT(b + 1)
                split_probs(G, 2)
                split_probs(G, 3)
                for r in range(TG):
                    if ahead:
                        row_max(G + 1, nxt, r, (par + 1 + r) % 2)
                    split_probs(G, r + 4)
                    if ahead:
                        row_scale(G + 1, nxt, r)
                dve.wait_ge(av_ok, G * JT + JT)
                nc.vector.tensor_copy(UT[:, 1, g * HEADS_G:(g + 1) * HEADS_G,
                                         b * NQ:(b + 1) * NQ] if isinstance(b, int) else
                                      UT[:, 1, g * HEADS_G:(g + 1) * HEADS_G, bass.ds(b * NQ, NQ)],
                                      U[:, 1, :].rearrange("p (h q) -> p h q", h=HEADS_G)).then_inc(ut_v, 1)

            queries(0)
            queries(1)
            split_ctxT(0, range(2))
            split_query(0, 0, 0)
            split_ctxT(0, range(2, 4))
            queries(2)
            queries(3)
            row_max(0, 0, 0, 1)
            for r in range(1, TG):
                row_max(0, 0, r, (1 + r) % 2)
                row_scale(0, 0, r - 1)
            row_scale(0, 0, TG - 1)
            with dve.Fori(0, NB - 1) as b:
                group(b, 0, True)
                group(b, 1, True)
            group(NB - 1, 0, True)

            def heads_T(t):
                dve.wait_ge(o_mm[t], 2)
                nc.vector.tensor_copy(OT[:, 4:8, t * P:(t + 1) * P],
                                      front[t][:, 1, :].rearrange("p (r t) -> p r t", r=4)).then_inc(o_v[t], 1)

            def first_residual(t):
                dve.wait_ge(xb_ok, NT)
                dve.wait_ge(wo_mm[t], 1)
                link(nc.vector.tensor_tensor(xr[:, t, :], back[t][:, 0, 0:D], xb[:, t, :], ALU.add))
                statistics(t, xr[:, t, :])

            def keys_values(s, t):
                dve.wait_ge(qk_mm[t], s + 1)
                nc.vector.tensor_tensor(kblk[:, 0, 2 * t:2 * t + 2, :, :],
                                        bc(back[t][:, 0, 0:P].rearrange("p (b q) -> p b q", b=2), 2, HC),
                                        bc(bc(headmask[:, :], 1, 2), 3, NQ), ALU.mult).then_inc(kb_v[t], 1)
                dve.wait_ge(v_mm[t], s + 1)
                dve.wait_ge(vzero, 3)
                nc.vector.tensor_copy(
                    Vblk[NQ:P, 2 * t:2 * t + 2, :, 1, 0:HD],
                    front[t][NQ:P, 1, :].rearrange("p (b r c e) -> p b r c e", b=2, r=NPAIR, c=2)[:, :, :, 1, :]
                ).then_inc(vb_v[t], 1)

            def shift(s, t):
                dve.wait_ge(sc_mm[t], s + 1)
                sc = back[t].rearrange("p c (h j) -> p (c h) j", h=HC)
                link(nc.vector.tensor_reduce(out=nm[:, t, :], in_=sc, axis=AX_X, op=ALU.max))
                nc.vector.tensor_tensor(E[:, t, :, :], sc, bc(nm[:, t, :], 2, NQ), sub).then_inc(shift_ok[t], 1)

            def exps_T(s, t):
                dve.wait_ge(str_mm[t], s + 1)
                nc.vector.tensor_copy(PT[:, t, 4:8, :],
                                      front[t][:, 1, :].rearrange("p (r q) -> p r q", r=4)).then_inc(pt_v[t], 1)

            def heads_out(s, t):
                dve.wait_ge(ao_mm[t], s + 1)
                heads = back[t][:, 0, 0:NH * (HD + 1)].rearrange("p (h e) -> p h e", h=NH)
                rows = xn[:, t, :].rearrange("p (h e) -> p h e", h=NH)
                link(nc.vector.reciprocal(ri[:, t, :], heads[:, :, HD]))
                link(nc.vector.tensor_tensor(rows, heads[:, :, 0:HD], bc(ri[:, t, :], 2, HD), ALU.mult))
                if s == 0:
                    dve.wait_ge(bv_mm[t], 1)
                    link(nc.vector.tensor_tensor(rows, back[t][:, 1, 0:NH * (HD + 1)].rearrange(
                        "p (h e) -> p h e", h=NH)[:, :, 0:HD], rows, ALU.add))
                statistics(t, xn[:, t, :])

            def second_residual(n, t):
                dve.wait_ge(xbeta_ok[t], 1)
                link(scaled_residual(n, t, xn[:, t, :], vec[:, 1, :], xr[:, t, :]))
                statistics(t, xr[:, t, :])
                centred(n + 1, t, xr[:, t, :], xin[:, t, :]).then_inc(xn_ok[t], 1)

            def moe_input(n, t):
                dve.wait_ge(xb1_ok[t], 1)
                scaled_residual(n, t, xn[:, t, :], vec[:, 3, :], y[:, t, :]).then_inc(y_ok[t], 1)

            G = NG - 1
            split_probs(G, 0)
            split_probs(G, 1)
            heads_T(0)
            split_probs(G, 2)
            split_probs(G, 3)
            first_residual(0)
            split_probs(G, 4)
            centred(2, 0, xr[:, 0, :], xn[:, 0, :]).then_inc(xn_ok[0], 1)
            split_probs(G, 5)
            split_probs(G, 6)
            split_probs(G, 7)
            keys_values(0, 0)
            dve.wait_ge(av_ok, G * JT + JT)
            nc.vector.tensor_copy(UT[:, 1, HEADS_G:2 * HEADS_G, (NB - 1) * NQ:NB * NQ],
                                  U[:, 1, :].rearrange("p (h q) -> p h q", h=HEADS_G)).then_inc(ut_v, 1)

            shift(0, 0)
            heads_T(1)
            exps_T(0, 0)
            first_residual(1)
            centred(3, 1, xr[:, 1, :], xn[:, 1, :]).then_inc(xn_ok[1], 1)
            heads_out(0, 0)
            second_residual(4, 0)
            keys_values(0, 1)
            shift(0, 1)
            keys_values(1, 0)
            exps_T(0, 1)
            heads_out(0, 1)
            second_residual(6, 1)
            shift(1, 0)
            keys_values(1, 1)
            exps_T(1, 0)
            shift(1, 1)
            heads_out(1, 0)
            exps_T(1, 1)
            moe_input(8, 0)
            heads_out(1, 1)
            moe_input(9, 1)
            for t in range(NT):
                dve.wait_ge(yThi_ok, t + 1)
                nc.vector.tensor_tensor(yT_lo[:, :, t * P:(t + 1) * P],
                                        back[t][:, 1, 0:D].rearrange("p (k q) -> p k q", k=KD),
                                        f(yT_hi[:, :, t * P:(t + 1) * P]), sub).then_inc(yTlo_ok, 1)

            def split_weights(e, i, m):
                for n in range(4):
                    w = slice(n * 512, (n + 1) * 512)
                    dve.wait_ge(w_hi_ok, e * 8 + (4 * m + n + 1))
                    nc.vector.tensor_tensor(Wlo[:, i, m, w], Wraw[i][:, m, w], f(Whi[:, i, m, w]),
                                            sub).then_inc(w_lo_ok, 1)

            def split_hidden(e, i, f2):
                dve.wait_ge(h_hi_ok, e * 4 + (f2 + 1))
                nc.vector.tensor_tensor(hT_lo[:, i, 2 * f2:2 * f2 + 2, :], h32[:, f2, :, :],
                                        f(hT_hi[:, i, 2 * f2:2 * f2 + 2, :]), sub).then_inc(h_lo_ok, 1)

            def combine(e, i):
                dve.wait_ge(eo_mm, e * 4 + 4)
                dve.wait_ge(acc_ok, e * NT + 2 * NT)
                for t in range(NT):
                    c = cw[:, t, e:e + 1] if isinstance(e, int) else cw[:, t, bass.ds(e, 1)]
                    nc.vector.scalar_tensor_tensor(out=acc[:, t, :], in0=(T, U)[i][:, t, 0:D], scalar=c,
                                                   in1=acc[:, t, :], op0=ALU.mult, op1=ALU.add).then_inc(acc_ok, 1)

            split_hidden(0, 0, 0)
            split_hidden(0, 0, 1)
            for t in range(NT):
                dve.wait_ge(lg_mm, t + 1)
                lg, top = small[:, t, 0, :], small[:, t, 2, :]
                link(nc.vector.tensor_copy(lg, U[:, t, 0:NE]))
                link(nc.vector.max(top, lg))
                link(nc.vector.max_index(mx8i[:, t, :], top, lg))
                link(nc.vector.tensor_copy(small[:, t, 3, :], mx8i[:, t, :]))
                nc.vector.tensor_tensor(small[:, t, 1, 1:2], top[:, 1:2], top[:, 0:1], sub).then_inc(gdiff_ok, 1)
            split_hidden(0, 0, 2)
            split_hidden(0, 0, 3)
            for t in range(NT):
                dve.wait_ge(gexp_ok, t + 1)
                ex, w12, idx = small[:, t, 1, 0:1], small[:, t, 4, :], small[:, t, 3, :]
                link(nc.vector.tensor_scalar(small[:, t, 5, 0:1], ex, 1.0, None, ALU.add))
                link(nc.vector.reciprocal(w12[:, 0:1], small[:, t, 5, 0:1]))
                link(nc.vector.tensor_tensor(w12[:, 1:2], ex, w12[:, 0:1], ALU.mult))
                for n in range(2):
                    link(nc.vector.tensor_scalar(small[:, t, 6 + n, :], iota8[:, :], idx[:, n:n + 1],
                                                 w12[:, n:n + 1], ALU.is_equal, ALU.mult))
                nc.vector.tensor_tensor(cw[:, t, :], small[:, t, 6, :], small[:, t, 7, :], ALU.add).then_inc(cw_ok, 1)
            dve.wait_ge(cw_ok, NT)
            with dve.Fori(0, NE // 2 - 1) as turn:
                e = turn * 2
                for i in range(2):
                    for f2 in range(4):
                        split_hidden(e + (i + 1), 1 - i, f2)
                        if f2 == 0:
                            split_weights(e + (i + 2), i, 0)
                    split_weights(e + (i + 2), i, 1)
                    combine(e + i, i)
            for f2 in range(4):
                split_hidden(NE - 1, 1, f2)
            combine(NE - 2, 0)
            dve.wait_ge(b2_mm, 1)
            dve.wait_ge(acc_ok, NT * (NE - 1) + 2 * NT)
            link(nc.vector.tensor_tensor(acc[:, :, :], S[:, 1, :].rearrange("p (t d) -> p t d", t=NT), acc[:, :, :],
                                         ALU.add))
            combine(NE - 1, 1)
            dve.wait_ge(res_ok, NT)
            dve.wait_ge(acc_ok, NT * NE + 2 * NT)
            for t in range(NT):
                statistics(t, acc[:, t, :])
            for t in range(NT):
                scaled_residual(5 * NT + t, t, acc[:, t, :], vec[:, 5, :], fin[:, t, :]).then_inc(fin_ok, 1)

        @block.gpsimd
        def _(pool):
            count = [0]

            def link(ins):
                count[0] += 1
                ins.then_inc(pchain, 1)
                pool.wait_ge(pchain, count[0])

            calls = [0]

            def inverse_deviation(t):
                pool.wait_ge(mv_ok, calls[0] + 1)
                nc.gpsimd.tensor_tensor(rstd[:, t:t + 1], mv[:, t, 2:3], pw[:, :], ALU.pow).then_inc(rstd_ok, 1)
                calls[0] += 1

            nc.gpsimd.memset(pw[:, :], -0.5).then_inc(power_ok, 1)
            pool.wait_ge(power_ok, 1)
            for t in range(NT):
                inverse_deviation(t)
            nc.gpsimd.memset(Qblk[:, :, :, :, :], 0.0).then_inc(qblk_zero, 1)

            def split_ctx(b):
                for j in range(JT):
                    jr = j % (JT // 2)
                    if jr == 0:
                        pool.wait_ge(in_ctx, b * 32 + (16 + 32 * j // JT))
                    if b > 0:
                        pool.wait_ge(av_ok, b * (GB * JT) + (j + 1 - JT))
                    nc.gpsimd.tensor_scalar(ctx_hi[:, j, :], ctx_raw[:, jr, :], 1.0, 1.0, ALU.mult,
                                            ALU.mult).then_inc(ctx_hi_ok, 1)
                    pool.wait_ge(ctx_hi_ok, b * JT + (j + 1))
                    nc.gpsimd.tensor_tensor(ctx_lo[:, j, :], ctx_raw[:, jr, :], f(ctx_hi[:, j, :]),
                                            ALU.subtract).then_inc(ctx_lo_ok, 1)

            for b in range(NB):
                split_ctx(b)
            pool.wait_ge(in_vec, 112)
            for t in range(NT):
                nc.gpsimd.tensor_tensor(xb[:, t, :], xr[:, t, :], vec[:, 0, :], ALU.add).then_inc(xb_ok, 1)

            def split_weights(e, m, pieces=range(4)):
                for n in pieces:
                    w = slice(n * 512, (n + 1) * 512)
                    pool.wait_ge(w_hi_ok, e * 8 + m * 4 + n + 1)
                    nc.gpsimd.tensor_tensor(Wlo[:, e, m, w], Wraw[e][:, m, w], f(Whi[:, e, m, w]),
                                            ALU.subtract).then_inc(w_lo_ok, 1)

            pool.wait_ge(sim_ok, NG * TG)
            nc.gpsimd.memset(Vblk[:, :, :, :, :], 0.0).then_inc(vzero, 1)
            pool.wait_ge(vzero, 1)
            for c in range(2):
                nc.gpsimd.memset(Vblk[c * NQ:(c + 1) * NQ, :, :, c, HD:HD + 1], 1.0).then_inc(vzero, 1)
                pool.wait_ge(vzero, c + 2)
            for t in range(NT):
                inverse_deviation(t)
                pool.wait_ge(xn_ok[t], 2)
                nc.gpsimd.tensor_tensor(xb[:, t, :], xr[:, t, :], vec[:, 2, :], ALU.add).then_inc(xbeta_ok[t], 1)
            pool.wait_ge(wo_mm[1], 1)
            nc.gpsimd.memset(acc[:, :, :], 0.0).then_inc(acc_ok, 2 * NT)
            for t in range(NT):
                inverse_deviation(t)
                inverse_deviation(t)
                pool.wait_ge(xn_ok[t], 3)
                nc.gpsimd.tensor_tensor(xb[:, t, :], xin[:, t, :], vec[:, 4, :], ALU.add).then_inc(xb1_ok[t], 1)
                split_weights(0, t)
            inverse_deviation(0)
            split_weights(1, 0)
            inverse_deviation(1)
            for t in range(NT):
                pool.wait_ge(y_ok[t], 1)
                link(nc.gpsimd.tensor_tensor(xb[:, t, :], xr[:, t, :], y[:, t, :], ALU.add))
                nc.gpsimd.tensor_tensor(xb[:, t, :], xb[:, t, :], vec[:, 6, :], ALU.add).then_inc(res_ok, 1)

            def split_hidden(e, i, f2):
                pool.wait_ge(relu_ok, e * 4 + (f2 + 1))
                if e >= 2:
                    pool.wait_ge(eo_mm, (e - 2) * 4 + (f2 + 1))
                nc.gpsimd.tensor_scalar(hT_hi[:, i, 2 * f2:2 * f2 + 2, :], h32[:, f2, :, :], 1.0, 1.0, ALU.mult,
                                        ALU.mult).then_inc(h_hi_ok, 1)

            for e in range(NE):
                for f2 in range(4):
                    split_hidden(e, e % 2, f2)
                    if e == 0:
                        split_weights(1, 1, [f2])
            for t in range(NT):
                inverse_deviation(t)


def _layouts(np, x, ctx_1024, L0_xattn_Wq, L0_xattn_Wk, L0_xattn_Wv, L0_xattn_Wo, L0_xattn_bo, L0_attn_Wq,
             L0_attn_Wk, L0_attn_Wv, L0_attn_rel_bias_table, L0_attn_ln_gamma, L0_attn_ln_beta, L0_ffn_Wq,
             L0_ffn_Wk, L0_ffn_Wv, L0_ffn_gate_W, L0_ffn_W1, L0_ffn_b1, L0_ffn_W2, L0_ffn_b2, L0_ffn_ln1_g,
             L0_ffn_ln1_b, L0_ffn_ln2_g, L0_ffn_ln2_b):
    nq = x.shape[1]
    d = x.shape[2]
    p = np.arange(128)
    table = L0_attn_rel_bias_table
    bt = np.stack([table[nq - 1 - j:2 * nq - 1 - j, :].T for j in range(nq)])
    nh = table.shape[1]
    bt = bt.reshape(nq, nh // 2, 2, nq).transpose(2, 0, 1, 3).reshape(2 * nq, nh // 2, nq)
    ne, ff = L0_ffn_b1.shape
    heads = lambda w: w.transpose(1, 0, 2).reshape(d, -1)
    return {
        "x": x, "ctx": ctx_1024, "ctxT": ctx_1024.transpose(0, 2, 1),
        "xattn_Wq": L0_xattn_Wq, "xattn_WkT": L0_xattn_Wk.T, "xattn_Wv": L0_xattn_Wv, "xattn_Wo": L0_xattn_Wo,
        "bo": L0_xattn_bo, "gamma": L0_attn_ln_gamma, "beta": L0_attn_ln_beta, "g1": L0_ffn_ln1_g,
        "b1n": L0_ffn_ln1_b, "g2": L0_ffn_ln2_g, "b2n": L0_ffn_ln2_b,
        "self0_q": L0_attn_Wq.T, "self0_k": L0_attn_Wk.T, "self0_v": L0_attn_Wv.T,
        "self1_q": heads(L0_ffn_Wq), "self1_k": heads(L0_ffn_Wk), "self1_v": heads(L0_ffn_Wv),
        "biasT": bt, "gate": L0_ffn_gate_W, "W1": L0_ffn_W1, "W2": L0_ffn_W2, "b2": L0_ffn_b2,
        "b1": L0_ffn_b1.reshape(ne, ff // 128, 128).transpose(2, 0, 1).reshape(128, -1),
        "ident": np.eye(128, dtype=np.float32),
        "headmask": (p[:, None] // 16 == np.arange(8)[None, :]).astype(np.float32),
        "causal": np.where(np.arange(nq)[None, :] <= (p % nq)[:, None], 0.0, -1e30).astype(np.float32),
        "iota8": np.tile(np.arange(ne, dtype=np.float32), (128, 1)),
    }


def kernel(**inputs):
    import numpy as _np
    import concourse.bacc as _bacc
    from concourse.bass_utils import run_bass_kernel_spmd as _run

    laid = _layouts(_np, **{k: _np.asarray(v) for k, v in inputs.items()})
    laid = {k: _np.ascontiguousarray(v) for k, v in laid.items()}
    nc = _bacc.Bacc("TRN2", target_bir_lowering=False, num_devices=1)
    arrays, args = {}, {}
    for name, v in laid.items():
        arrays[f"in_{name}"] = v
        args[name] = nc.dram_tensor(f"in_{name}", v.shape, mybir.dt.from_np(v.dtype), kind="ExternalInput").ap()
    out = nc.dram_tensor("out_x", laid["x"].shape, F32, kind="ExternalOutput").ap()
    perceiver_block(nc, args, out)
    r = _run(nc, [arrays], core_ids=[0])
    return r.results[0]["out_x"]
```

```python
from contextlib import ExitStack

import concourse.bass as bass
from concourse import mybir

P = 128
ALU = mybir.AluOpType
ACT = mybir.ActivationFunctionType
F32 = mybir.dt.float32
F32R = mybir.dt.float32r
BF16 = mybir.dt.bfloat16
U32 = mybir.dt.uint32
AX_X = mybir.AxisListType.X
EPS = 1e-5


def perceiver_block(nc, a, out):
    NB, NQ, D = a["x"].shape
    NC_ = a["ctx"].shape[1]
    NT = NB * NQ // P
    KD = D // P
    NH = 16
    INNER = a["xattn_Wq"].shape[1]
    DH = INNER // NH
    NPAIR = NH // 2
    HD = D // NH
    HC = P // HD
    JT = NC_ // P
    ROWS = 512
    TG = ROWS // P
    GB = NH * NQ // ROWS
    NG = GB * NB
    NE, _, FF = a["W1"].shape
    FT = FF // P
    TOK = NB * NQ
    XSCALE = float(DH) ** -0.5
    SSCALE = float(D) ** -0.5
    HEADS_G = ROWS // NQ
    assert (NT, KD, NPAIR, JT, TG, GB, FT, TOK) == (2, 2, 8, 8, 4, 2, 8, 256)

    ctx = ExitStack()
    with ctx:
        def sem(name):
            return ctx.enter_context(nc.semaphore(name))

        def halves(name):
            return [sem(f"{name}_{t}") for t in range(NT)]

        def sb(stack, name, shape, dt=F32):
            return stack.enter_context(nc.sbuf_tensor(name, shape, dt))

        S = ctx.enter_context(nc.psum_tensor("S", [P, 4, 512], F32))
        T = ctx.enter_context(nc.psum_tensor("T", [P, 2, 512], F32))
        U = ctx.enter_context(nc.psum_tensor("U", [P, 2, 512], F32))
        front = (S[:, 0:2, :], T[:, :, :])
        back = (S[:, 2:4, :], U[:, :, :])
        query_bank = (S[:, 2, :], S[:, 3, :], T[:, 0, :], T[:, 1, :])

        ident = sb(ctx, "ident", [P, P])
        ident_bf = sb(ctx, "ident_bf", [P, P], BF16)
        headmask = sb(ctx, "headmask", [P, HC])
        causal = sb(ctx, "causal", [P, NQ])
        causal_bf = sb(ctx, "causal_bf", [P, NQ], BF16)
        iota8 = sb(ctx, "iota8", [P, NE])
        pw = sb(ctx, "pw", [P, 1])
        xr = sb(ctx, "xr", [P, NT, D])
        xb = sb(ctx, "xb", [P, NT, D])
        xn = sb(ctx, "xn", [P, NT, D])
        xnT = sb(ctx, "xnT", [P, KD, TOK])
        vec = sb(ctx, "vec", [P, 7, D])
        stats = sb(ctx, "stats", [P, NT, 6])
        mv = sb(ctx, "mv", [P, NT, 3])
        rstd = sb(ctx, "rstd", [P, NT])
        self_w = sb(ctx, "self_w", [P, 2, 3, KD, D])
        gate = sb(ctx, "gate", [P, KD, NE])
        b1T = sb(ctx, "b1T", [P, NE, FT])
        b2 = sb(ctx, "b2", [NE, D])
        biasT = sb(ctx, "biasT", [P, NPAIR, NQ])
        small = sb(ctx, "small", [P, NT, 8, 8])
        mx8i = sb(ctx, "mx8i", [P, NT, 8], U32)
        cw = sb(ctx, "cw", [P, NT, NE])
        cT = sb(ctx, "cT", [NE, TOK])
        negmax = sb(ctx, "negmax", [P, 2, TG])
        rowsum = sb(ctx, "rowsum", [P, 2, TG])
        rowinv = sb(ctx, "rowinv", [P, 2, TG])

        ra = ExitStack()
        ctxT_hi = sb(ra, "ctxT_hi", [P, KD, NC_], F32R)
        ctxT_lo = sb(ra, "ctxT_lo", [P, KD, NC_], F32R)
        qp_hi = sb(ra, "qp_hi", [P, 2, KD, ROWS], F32R)
        qp_lo = sb(ra, "qp_lo", [P, 2, KD, ROWS], F32R)
        WkT = sb(ra, "WkT", [P, NPAIR, D])
        probs = sb(ra, "probs", [P, 2, TG, NC_])
        ctx_hi = sb(ra, "ctx_hi", [P, JT, D], F32R)
        ctx_lo = sb(ra, "ctx_lo", [P, JT, D], F32R)
        ctxT_raw = sb(ra, "ctxT_raw", [P, KD, NC_])
        ctx_raw = sb(ra, "ctx_raw", [P, JT // 2, D])
        pT_hi = sb(ra, "pT_hi", [P, 4, ROWS], F32R)
        pT_lo = sb(ra, "pT_lo", [P, 4, ROWS], F32R)
        Wq = sb(ra, "Wq", [P, KD, INNER])
        Qblk = sb(ra, "Qblk", [P, NB, NPAIR, 2, NQ])
        UT = sb(ra, "UT", [P, KD, NH, TOK])
        Wv = Wq
        OT = Qblk[:, :, :, :, :].rearrange("p b h c q -> p (b h c q)")[:, 0:NPAIR * TOK].rearrange(
            "p (r t) -> p r t", r=NPAIR)
        Wo = ctxT_raw[:, :, :].rearrange("p k n -> p (k n)").rearrange("p (r d) -> p r d", r=NPAIR)
        ra.close()

        rd = ExitStack()
        Vblk = sb(rd, "Vblk", [P, NB, NPAIR, 2, HD + 1])
        qT = sb(rd, "qT", [P, KD, TOK])
        kblk = sb(rd, "kblk", [P, KD, NB, HC, NQ])
        E = sb(rd, "E", [P, NT, NH, NQ])
        PT = sb(rd, "PT", [P, NT, NPAIR, P])
        nm = sb(rd, "nm", [P, NT, NH])
        ri = sb(rd, "ri", [P, NT, NH])
        rd.close()
        rc = ExitStack()
        hT_hi = sb(rc, "hT_hi", [P, 2, FT, TOK], F32R)
        hT_lo = sb(rc, "hT_lo", [P, 2, FT, TOK], F32R)
        h32 = sb(rc, "h32", [P, 4, 2, TOK])
        Wraw = [None, None]
        Wraw[0] = sb(rc, "Wraw_0", [P, 2, KD * FF])
        y = sb(rc, "y", [P, NT, D])
        xin = sb(rc, "xin", [P, NT, D])
        fin = sb(rc, "fin", [P, NT, D])
        acc = sb(rc, "acc", [P, NT, D])
        yT = sb(rc, "yT", [P, KD, TOK])
        yT_hi = sb(rc, "yT_hi", [P, KD, TOK], F32R)
        yT_lo = sb(rc, "yT_lo", [P, KD, TOK], F32R)
        Wraw[1] = sb(rc, "Wraw_1", [P, 2, KD * FF])
        Whi = sb(rc, "Whi", [P, 2, 2, KD * FF], F32R)
        Wlo = sb(rc, "Wlo", [P, 2, 2, KD * FF], F32R)
        rc.close()

        in_x = sem("in_x")
        in_ident = sem("in_ident")
        in_const = sem("in_const")
        in_Wq = sem("in_Wq")
        in_WkT = sem("in_WkT")
        in_Wq_rest = sem("in_Wq_rest")
        in_WkT_rest = sem("in_WkT_rest")
        in_vec = sem("in_vec")
        in_ctxT = sem("in_ctxT")
        in_ctx = sem("in_ctx")
        in_Wv = sem("in_Wv")
        in_Wo = sem("in_Wo")
        in_later = sem("in_later")
        in_W1 = [sem(f"in_W1_{i}") for i in range(2)]
        in_W2 = [sem(f"in_W2_{i}") for i in range(2)]
        stored = sem("stored")
        qblk_zero = sem("qblk_zero")
        q_mm = sem("q_mm")
        q_a = sem("q_a")
        q_v = sem("q_v")
        qp_mm = sem("qp_mm")
        qp_hi_ok = sem("qp_hi_ok")
        qp_lo_ok = sem("qp_lo_ok")
        ctxT_hi_ok = sem("ctxT_hi_ok")
        ctxT_lo_ok = sem("ctxT_lo_ok")
        ctx_hi_ok = sem("ctx_hi_ok")
        ctx_lo_ok = sem("ctx_lo_ok")
        sim_ok = sem("sim_ok")
        max_ok = sem("max_ok")
        exp_ok = sem("exp_ok")
        inv_ok = sem("inv_ok")
        norm_ok = sem("norm_ok")
        norm_start_ok = sem("norm_start_ok")
        tr_ok = sem("tr_ok")
        pT_hi_ok = sem("pT_hi_ok")
        pT_lo_ok = sem("pT_lo_ok")
        av_ok = sem("av_ok")
        ut_a = sem("ut_a")
        ut_v = sem("ut_v")
        o_mm = halves("o_mm")
        o_a = halves("o_a")
        o_v = halves("o_v")
        wo_mm = halves("wo_mm")
        xb_ok = sem("xb_ok")
        xbeta_ok = halves("xbeta_ok")
        xb1_ok = halves("xb1_ok")
        mv_ok = sem("mv_ok")
        rstd_ok = sem("rstd_ok")
        xn_ok = halves("xn_ok")
        xnT_mm = halves("xnT_mm")
        xnT_ok = halves("xnT_ok")
        chain = sem("chain")
        pchain = sem("pchain")
        power_ok = sem("power_ok")
        warm_ok = sem("warm_ok")
        qk_mm = halves("qk_mm")
        v_mm = halves("v_mm")
        sq_ok = halves("sq_ok")
        kb_a = halves("kb_a")
        kb_v = halves("kb_v")
        vzero = sem("vzero")
        vb_a = halves("vb_a")
        vb_v = halves("vb_v")
        sc_mm = halves("sc_mm")
        shift_ok = halves("shift_ok")
        sexp_ok = halves("sexp_ok")
        str_mm = halves("str_mm")
        pt_a = halves("pt_a")
        pt_v = halves("pt_v")
        ao_mm = halves("ao_mm")
        bv_mm = halves("bv_mm")
        cw_ok = sem("cw_ok")
        y_ok = halves("y_ok")
        cbf_ok = sem("cbf_ok")
        yT_mm = sem("yT_mm")
        yT_ok = sem("yT_ok")
        yThi_ok = sem("yThi_ok")
        yTlo_ok = sem("yTlo_ok")
        lg_mm = sem("lg_mm")
        gdiff_ok = sem("gdiff_ok")
        gexp_ok = sem("gexp_ok")
        cT_mm = sem("cT_mm")
        cT_ok = sem("cT_ok")
        b2_mm = sem("b2_mm")
        w_hi_ok = sem("w_hi_ok")
        w_lo_ok = sem("w_lo_ok")
        h_mm = sem("h_mm")
        relu_ok = sem("relu_ok")
        h_hi_ok = sem("h_hi_ok")
        h_lo_ok = sem("h_lo_ok")
        eo_mm = sem("eo_mm")
        last_mm = sem("last_mm")
        acc_ok = sem("acc_ok")
        res_ok = sem("res_ok")
        fin_ok = sem("fin_ok")

        def f(t):
            return t.bitcast(F32)

        def bc(t, dim, n):
            t = t.unsqueeze(dim)
            return t.broadcast_to([*t.shape[:dim], n, *t.shape[dim + 1:]])

        ctx_v = a["ctx"].rearrange("b (j p) d -> b p j d", p=P)
        ctxT_v = a["ctxT"].rearrange("b (k p) n -> b p k n", p=P)
        W1_v = a["W1"].rearrange("e (k p) f -> e p k f", p=P)
        W2_v = a["W2"].rearrange("e (f p) d -> e p f d", p=P)
        x_v = a["x"].rearrange("b q d -> (b q) d").rearrange("(t p) d -> p t d", p=P)
        out_v = out.rearrange("b q d -> (b q) d").rearrange("(t p) d -> p t d", p=P)

        block = ctx.enter_context(nc.Block())

        @block.sync
        def _(sp):
            sp.dma_start(xr[:, :, :], x_v).then_inc(in_x, 16)
            sp.dma_start(ident[:, :], a["ident"]).then_inc(in_ident, 16)
            Wq_v = a["xattn_Wq"].rearrange("(k p) n -> p k n", p=P)
            WkT_v = a["xattn_WkT"].rearrange("(r p) d -> p r d", p=P)
            sp.dma_start(Wq[:, :, 0:TG * P], Wq_v[:, :, 0:TG * P]).then_inc(in_Wq, 16)
            sp.dma_start(WkT[:, 0:TG, :], WkT_v[:, 0:TG, :]).then_inc(in_WkT, 16)
            sp.dma_start(Wq[:, :, TG * P:2 * TG * P], Wq_v[:, :, TG * P:2 * TG * P]).then_inc(in_Wq_rest, 16)
            sp.dma_start(ctxT_raw[:, :, :], ctxT_v[0]).then_inc(in_ctxT, 16)
            sp.dma_start(ctx_raw[:, :, :], ctx_v[0][:, 0:JT // 2, :]).then_inc(in_ctx, 16)
            sp.dma_start(WkT[:, TG:2 * TG, :], WkT_v[:, TG:2 * TG, :]).then_inc(in_WkT_rest, 16)
            for dst, name in ((headmask, "headmask"), (causal, "causal"), (iota8, "iota8")):
                sp.dma_start(dst[:, :], a[name]).then_inc(in_const, 16)
            for i, name in enumerate(("bo", "gamma", "beta", "g1", "b1n", "g2", "b2n")):
                sp.dma_start(vec[:, i, :], a[name].partition_broadcast(P)).then_inc(in_vec, 16)
            sp.wait_ge(q_mm, 4)
            sp.dma_start(Wv[:, :, :], a["xattn_Wv"].rearrange("(k p) n -> p k n", p=P)).then_inc(in_Wv, 16)
            for s in range(2):
                for i, name in enumerate(("q", "k", "v")):
                    sp.dma_start(self_w[:, s, i, :, :],
                                 a[f"self{s}_{name}"].rearrange("(k p) n -> p k n", p=P)).then_inc(in_later, 16)
            sp.dma_start(gate[:, :, :], a["gate"].rearrange("(k p) n -> p k n", p=P)).then_inc(in_later, 16)
            sp.dma_start(b1T[:, :, :], a["b1"].rearrange("p (e f) -> p e f", e=NE)).then_inc(in_later, 16)
            sp.dma_start(b2[:, :], a["b2"]).then_inc(in_later, 16)
            sp.dma_start(biasT[:, :, :], a["biasT"]).then_inc(in_later, 16)
            sp.wait_ge(ctx_lo_ok, JT // 2)
            sp.dma_start(ctx_raw[:, :, :], ctx_v[0][:, JT // 2:JT, :]).then_inc(in_ctx, 16)
            with sp.Fori(0, NB - 1) as b:
                sp.wait_ge(ctxT_lo_ok, b * 4 + 4)
                sp.dma_start(ctxT_raw[:, :, :], ctxT_v[bass.ds(b + 1, 1)].rearrange("o p k n -> p (o k) n")
                             ).then_inc(in_ctxT, 16)
                for half in range(2):
                    sp.wait_ge(ctx_lo_ok, b * JT + JT + half * (JT // 2))
                    sp.dma_start(ctx_raw[:, :, :],
                                 ctx_v[bass.ds(b + 1, 1), :, half * (JT // 2):(half + 1) * (JT // 2), :].rearrange(
                                     "o p j d -> p (o j) d")).then_inc(in_ctx, 16)
            sp.wait_ge(ctxT_lo_ok, 4 * NB)
            sp.dma_start(Wo, a["xattn_Wo"].rearrange("(r p) d -> p r d", p=P)).then_inc(in_Wo, 16)
            def load_expert(i, e, m):
                src = (W1_v, W2_v)[m]
                src = src[e] if isinstance(e, int) else src[bass.ds(e, 1)].rearrange("o p k n -> p (o k) n")
                sp.dma_start(Wraw[i][:, m, :].rearrange("p (k n) -> p k n", k=(KD, FT)[m]), src
                             ).then_inc((in_W1, in_W2)[m][i], 16)

            sp.wait_ge(tr_ok, (NG - 1) * JT)
            for m in range(2):
                load_expert(0, 0, m)
            sp.wait_ge(wo_mm[0], 1)
            sp.wait_ge(wo_mm[1], 1)
            for m in range(2):
                load_expert(1, 1, m)
            with sp.Fori(0, NE // 2 - 1) as turn:
                e = turn * 2
                for i in range(2):
                    sp.wait_ge(w_lo_ok, (e + i) * 8 + 4)
                    load_expert(i, e + (i + 2), 0)
                    sp.wait_ge(w_lo_ok, (e + i) * 8 + 8)
                    load_expert(i, e + (i + 2), 1)
            for t in range(NT):
                sp.wait_ge(fin_ok, t + 1)
                sp.dma_start(out_v[:, t, :], fin[:, t, :]).then_inc(stored, 16)
            sp.wait_ge(stored, 16 * NT)

        @block.tensor
        def _(pe):
            mm = nc.tensor.matmul

            def keep_warm(n, free, operand=ident[:, :]):
                for _ in range(n):
                    mm(free, operand, operand, start=True, stop=True)

            def passes3(dst, l_hi, l_lo, r_hi, r_lo, start, stop):
                mm(dst, l_hi, r_hi, start=start, stop=False)
                mm(dst, l_hi, r_lo, start=False, stop=False)
                return mm(dst, l_lo, r_hi, start=False, stop=stop)

            def transpose_rows(t, src, dst, ready):
                for k in range(KD):
                    last = nc.tensor.transpose(dst[:, k * P:(k + 1) * P], src[:, t, k * P:(k + 1) * P], ident[:, :])
                last.then_inc(ready, 1)

            def absorbed_query(g, b, par, stored=False):
                for r in range(TG):
                    pair = TG * g + r
                    if stored and r % 2 == 0:
                        pe.wait_ge(q_a, r // 2 + 1)
                        pe.wait_ge(q_v, r // 2 + 1)
                    for k in range(KD):
                        last = mm(S[:, 2 * par + k, r * P:(r + 1) * P], WkT[:, pair, k * P:(k + 1) * P],
                                  Qblk[:, b, pair, :, :] if isinstance(b, int) else
                                  Qblk[:, bass.ds(b, 1), pair, :, :].rearrange("p o c q -> p (o c) q"),
                                  start=True, stop=True)
                last.then_inc(qp_mm, 1)

            def scores(gp, r, par, half):
                for k in range(KD):
                    last = passes3(S[:, 2 * par + half, :], qp_hi[:, gp, k, r * P:(r + 1) * P],
                                   qp_lo[:, gp, k, r * P:(r + 1) * P],
                                   ctxT_hi[:, k, half * 512:(half + 1) * 512],
                                   ctxT_lo[:, k, half * 512:(half + 1) * 512], k == 0, k == KD - 1)
                if half == 1:
                    last.then_inc(sim_ok, 1)

            def transpose_probs(gp, j, G=None):
                for r in range(TG):
                    if G is not None:
                        if r < TG - 1:
                            pe.wait_ge(norm_ok, G * TG + (r + 1))
                        else:
                            pe.wait_ge(norm_start_ok, G + 1)
                    last = nc.tensor.transpose(T[:, j % 2, r * P:(r + 1) * P], probs[:, gp, r, j * P:(j + 1) * P],
                                               ident[:, :])
                last.then_inc(tr_ok, 1)

            def attend(G, b, j):
                pe.wait_ge(pT_lo_ok, G * JT + (j + 1))
                pe.wait_ge(ctx_lo_ok, b * JT + (j + 1))
                if j == 0:
                    pe.wait_ge(ut_a, G + 1)
                    pe.wait_ge(ut_v, G + 1)
                for k in range(KD):
                    last = passes3(U[:, k, :], ctx_hi[:, j, k * P:(k + 1) * P], ctx_lo[:, j, k * P:(k + 1) * P],
                                   pT_hi[:, j % 4, :], pT_lo[:, j % 4, :], j == 0, j == JT - 1)
                last.then_inc(av_ok, 1)

            def group(b, g):
                G = b * GB + g
                gp, nxt, nb = g, 1 - g, b + g
                par = (g + 1) % 2
                pe.wait_ge(norm_ok, G * TG + TG)
                transpose_probs(gp, 1)
                absorbed_query(nxt, nb, par)
                attend(G, b, 0)
                transpose_probs(gp, 2)
                attend(G, b, 1)
                for r in range(TG):
                    if r == 0:
                        pe.wait_ge(qp_lo_ok, G + 2)
                        pe.wait_ge(ctxT_lo_ok, nb * 4 + 2)
                    if r >= 2:
                        pe.wait_ge(exp_ok, G * TG + (TG + r - 1))
                    scores(nxt, r, (par + 1 + r) % 2, 0)
                    if r == 0:
                        pe.wait_ge(ctxT_lo_ok, nb * 4 + 4)
                    scores(nxt, r, (par + 1 + r) % 2, 1)
                    transpose_probs(gp, r + 3)
                    attend(G, b, r + 2)
                transpose_probs(gp, 7)
                attend(G, b, 6)
                transpose_probs(nxt, 0, G + 1)
                attend(G, b, 7)

            pe.wait_ge(warm_ok, 1)
            keep_warm(9, U[:, 0, 0:P], xnT[:, 0, 0:P])
            pe.wait_ge(in_ident, 16)
            for t in range(NT):
                pe.wait_ge(xn_ok[t], 1)
                transpose_rows(t, xn, T[:, t, :], xnT_mm[t])
            keep_warm(2, U[:, 0, 0:P])
            pe.wait_ge(in_Wq, 16)
            for t in range(NT):
                pe.wait_ge(xnT_ok[t], 1)

            def queries(n):
                for i in range(2):
                    pair = 2 * n + i
                    for k in range(KD):
                        last = mm(query_bank[n][:, i * TOK:(i + 1) * TOK], Wq[:, k, pair * P:(pair + 1) * P],
                                  xnT[:, k, :], start=(k == 0), stop=(k == KD - 1))
                last.then_inc(q_mm, 1)

            queries(0)
            queries(1)
            pe.wait_ge(in_WkT, 16)
            absorbed_query(0, 0, 0, stored=True)
            pe.wait_ge(in_Wq_rest, 16)
            queries(2)
            keep_warm(3, U[:, 0, 0:P])
            pe.wait_ge(qp_lo_ok, 1)
            pe.wait_ge(ctxT_lo_ok, 2)
            for r in range(TG):
                if r >= 2:
                    pe.wait_ge(exp_ok, r - 1)
                scores(0, r, (1 + r) % 2, 0)
                if r == 0:
                    pe.wait_ge(ctxT_lo_ok, 4)
                scores(0, r, (1 + r) % 2, 1)
            queries(3)
            keep_warm(10, U[:, 0, 0:P])
            pe.wait_ge(q_a, 3)
            pe.wait_ge(q_v, 3)
            transpose_probs(0, 0, 0)
            pe.wait_ge(in_WkT_rest, 16)
            pe.wait_ge(q_a, 4)
            pe.wait_ge(q_v, 4)
            with pe.Fori(0, NB - 1) as b:
                group(b, 0)
                group(b, 1)
            group(NB - 1, 0)

            def heads_T(t):
                pe.wait_ge(in_Wv, 16)
                pe.wait_ge(ut_a, (t + 1) * NG // 2 + 1)
                pe.wait_ge(ut_v, (t + 1) * NG // 2 + 1)
                for h in range(NH):
                    pair, c = h // 2, h % 2
                    for k in range(KD):
                        last = mm(front[t][c * DH:(c + 1) * DH, pair // 4, (pair % 4) * P:(pair % 4 + 1) * P],
                                  Wv[:, k, h * DH:(h + 1) * DH], UT[:, k, h, t * P:(t + 1) * P],
                                  start=(k == 0), stop=(k == KD - 1))
                    if h % 8 == 7:
                        last.then_inc(o_mm[t], 1)

            def out_product(t):
                pe.wait_ge(in_Wo, 16)
                pe.wait_ge(o_a[t], 1)
                pe.wait_ge(o_v[t], 1)
                for pair in range(NPAIR):
                    last = mm(back[t][:, 0, 0:D], OT[:, pair, t * P:(t + 1) * P], Wo[:, pair, :],
                              start=(pair == 0), stop=(pair == NPAIR - 1))
                last.then_inc(wo_mm[t], 1)

            def rows_T(s, t):
                pe.wait_ge(xn_ok[t], s + 2)
                transpose_rows(t, xn if s == 0 else xin, back[t][:, 1, :], xnT_mm[t])

            def queries_keys(s, t):
                if s == 0 and t == 0:
                    pe.wait_ge(in_later, 160)
                pe.wait_ge(xnT_ok[t], s + 2)
                tok = slice(t * P, (t + 1) * P)
                for i in range(2):
                    for c in range(KD):
                        for k in range(KD):
                            dst = back[t][:, 0, 0:P] if (i, c) == (1, 0) else \
                                front[t][:, 0, (i + c) * P:(i + c + 1) * P]
                            last = mm(dst, self_w[:, s, i, k, c * P:(c + 1) * P], xnT[:, k, tok],
                                      start=(k == 0), stop=(k == KD - 1))
                last.then_inc(qk_mm[t], 1)

            def values(s, t):
                for i in range(2):
                    b = 2 * t + i
                    for k in range(KD):
                        for c in range(2):
                            last = mm(front[t][c * NQ:(c + 1) * NQ, 1, i * D:(i + 1) * D],
                                      xnT[:, k, b * NQ:(b + 1) * NQ], self_w[:, s, 2, k, :],
                                      start=(k == 0), stop=(k == KD - 1), skip_group_check=True)
                last.then_inc(v_mm[t], 1)

            def self_scores(s, t):
                pe.wait_ge(sq_ok[t], s + 1)
                for c in range(KD):
                    pe.wait_ge((kb_v, kb_a)[c][t], s + 1)
                    if s == 1:
                        pe.wait_ge(cbf_ok, 1)
                        mm(back[t][:, c, :], ident_bf[:, :], bc(causal_bf[:, :], 1, HC), start=True, stop=False,
                           skip_group_check=True)
                    for i in range(2):
                        b = 2 * t + i
                        last = mm(back[t][i * NQ:(i + 1) * NQ, c, :], qT[:, c, b * NQ:(b + 1) * NQ],
                                  kblk[:, c, b, :, :], start=(s == 0), stop=True, skip_group_check=True)
                    last.then_inc(sc_mm[t], 1)

            def transpose_exps(s, t):
                for c in range(KD):
                    if c == 1:
                        pe.wait_ge(vb_a[t], s + 1)
                        pe.wait_ge(vb_v[t], s + 1)
                    pe.wait_ge(sexp_ok[t], KD * s + c + 1)
                    for r in range(4):
                        pair = 4 * c + r
                        last = nc.tensor.transpose(front[t][:, c, r * P:(r + 1) * P],
                                                   E[:, t, 2 * pair:2 * pair + 2, :], ident[:, :])
                    last.then_inc(str_mm[t], 1)

            def times_v(t, n, c, weights):
                for i in range(2):
                    for pair in range(4 * c, 4 * c + 4):
                        w = slice(pair * 2 * (HD + 1), (pair + 1) * 2 * (HD + 1))
                        last = mm(back[t][i * NQ:(i + 1) * NQ, n, w], weights(i, pair),
                                  Vblk[:, 2 * t + i, pair, :, :], start=True, stop=True, skip_group_check=True)
                return last

            def bias_product(t):
                times_v(t, 1, 0, lambda i, pair: biasT[:, pair, :])
                times_v(t, 1, 1, lambda i, pair: biasT[:, pair, :]).then_inc(bv_mm[t], 1)

            def self_out(s, t):
                for c in range(KD):
                    pe.wait_ge((pt_a, pt_v)[c][t], s + 1)
                    last = times_v(t, 0, c, lambda i, pair: PT[:, t, pair, i * NQ:(i + 1) * NQ])
                last.then_inc(ao_mm[t], 1)

            def y_T(t):
                pe.wait_ge(y_ok[t], 1)
                transpose_rows(t, y, back[t][:, 1, :], yT_mm)

            G = NG - 1
            pe.wait_ge(norm_ok, G * TG + TG)
            transpose_probs(1, 1)
            heads_T(0)
            attend(G, NB - 1, 0)
            transpose_probs(1, 2)
            attend(G, NB - 1, 1)
            transpose_probs(1, 3)
            attend(G, NB - 1, 2)
            out_product(0)
            transpose_probs(1, 4)
            attend(G, NB - 1, 3)
            transpose_probs(1, 5)
            attend(G, NB - 1, 4)
            rows_T(0, 0)
            transpose_probs(1, 6)
            attend(G, NB - 1, 5)
            queries_keys(0, 0)
            values(0, 0)
            transpose_probs(1, 7)
            attend(G, NB - 1, 6)
            attend(G, NB - 1, 7)

            self_scores(0, 0)
            heads_T(1)
            transpose_exps(0, 0)
            out_product(1)
            bias_product(0)
            self_out(0, 0)
            rows_T(0, 1)
            keep_warm(3, S[:, 0, 0:P])
            queries_keys(0, 1)
            values(0, 1)
            self_scores(0, 1)
            keep_warm(2, S[:, 0, 0:P])
            rows_T(1, 0)
            keep_warm(3, S[:, 0, 0:P])
            queries_keys(1, 0)
            transpose_exps(0, 1)
            bias_product(1)
            self_out(0, 1)
            values(1, 0)
            self_scores(1, 0)
            keep_warm(4, S[:, 0, 0:P])
            rows_T(1, 1)
            keep_warm(3, S[:, 0, 0:P])
            queries_keys(1, 1)
            values(1, 1)
            transpose_exps(1, 0)
            self_scores(1, 1)
            self_out(1, 0)
            transpose_exps(1, 1)
            self_out(1, 1)
            y_T(0)
            keep_warm(8, S[:, 0, 0:P])
            y_T(1)
            keep_warm(4, S[:, 0, 0:P])

            def hidden(e, i, f2):
                if f2 == 0:
                    pe.wait_ge(w_lo_ok, e * 8 + 4)
                if not isinstance(e, int) or e > 0:
                    pe.wait_ge(relu_ok, (e - 1) * 4 + (f2 + 1))
                for ft in (2 * f2, 2 * f2 + 1):
                    for k in range(KD):
                        w = slice(k * FF + ft * P, k * FF + (ft + 1) * P)
                        last = passes3(S[:, f2, (ft % 2) * TOK:(ft % 2 + 1) * TOK], Whi[:, i, 0, w], Wlo[:, i, 0, w],
                                       yT_hi[:, k, :], yT_lo[:, k, :], k == 0, k == KD - 1)
                last.then_inc(h_mm, 1)

            def expert_half(e, i, f2, t):
                pe.wait_ge(h_lo_ok, e * 4 + (f2 + 1))
                if f2 == 0:
                    pe.wait_ge(w_lo_ok, e * 8 + 8)
                    pe.wait_ge(acc_ok, e * NT + NT)
                for ft in (2 * f2, 2 * f2 + 1):
                    w = slice(ft * D, (ft + 1) * D)
                    l_hi = hT_hi[:, i, ft, t * P:(t + 1) * P]
                    l_lo = hT_lo[:, i, ft, t * P:(t + 1) * P]
                    last = passes3((T, U)[i][:, t, 0:D], l_hi, l_lo, Whi[:, i, 1, w], Wlo[:, i, 1, w],
                                   ft == 0, ft == FT - 1)
                return last

            def expert_out(e, i, f2):
                for t in range(NT):
                    last = expert_half(e, i, f2, t)
                last.then_inc(eo_mm, 1)

            pe.wait_ge(yTlo_ok, NT)
            hidden(0, 0, 0)
            hidden(0, 0, 1)
            pe.wait_ge(yT_ok, NT)
            for t in range(NT):
                for k in range(KD):
                    last = mm(U[:, t, 0:NE], yT[:, k, t * P:(t + 1) * P], gate[:, k, :],
                              start=(k == 0), stop=(k == KD - 1))
                last.then_inc(lg_mm, 1)
            hidden(0, 0, 2)
            hidden(0, 0, 3)
            with pe.Fori(0, NE // 2 - 1) as turn:
                e = turn * 2
                for f2 in range(4):
                    hidden(e + 1, 1, f2)
                    expert_out(e, 0, f2)
                pe.wait_ge(cw_ok, 1)
                for f2 in range(4):
                    hidden(e + 2, 0, f2)
                    expert_out(e + 1, 1, f2)
            for f2 in range(4):
                hidden(NE - 1, 1, f2)
                expert_out(NE - 2, 0, f2)
            pe.wait_ge(cw_ok, 1)
            pe.wait_ge(relu_ok, NE * 4)
            for t in range(NT):
                last = nc.tensor.transpose(S[0:NE, 0, t * P:(t + 1) * P], cw[:, t, :], ident[:, :])
            last.then_inc(cT_mm, 1)
            for f2 in range(4):
                last = expert_half(NE - 1, 1, f2, 0)
                if f2 == 0:
                    pe.wait_ge(cT_ok, 1)
                    for t in range(NT):
                        b2_last = mm(S[:, 1, t * D:(t + 1) * D], cT[:, t * P:(t + 1) * P], b2[:, :],
                                     start=True, stop=True)
                    b2_last.then_inc(b2_mm, 1)
            last.then_inc(last_mm, 1)
            for f2 in range(4):
                last = expert_half(NE - 1, 1, f2, 1)
            last.then_inc(last_mm, 1)

        @block.scalar
        def _(act):
            def copy(dst, src, scale=1.0):
                return nc.scalar.activation(dst, src, ACT.Copy, scale=scale)

            def rows_T(stage, t, src):
                act.wait_ge(xnT_mm[t], stage + 1)
                copy(xnT[:, :, t * P:(t + 1) * P],
                     src[:, 0:D].rearrange("p (k q) -> p k q", k=KD)).then_inc(xnT_ok[t], 1)

            act.sem_inc(ut_a, 1)
            for t in range(NT):
                rows_T(0, t, T[:, t, :])
            act.wait_ge(qblk_zero, 1)

            def queries(n):
                act.wait_ge(q_mm, n + 1)
                copy(Qblk[0:DH, :, 2 * n:2 * n + 2, 0, :].rearrange("p b r q -> p r b q"),
                     query_bank[n][0:DH, :].rearrange("p (r b q) -> p r b q", r=2, b=NB)).then_inc(q_a, 1)

            for n in range(2):
                queries(n)

            def split_query(G, gp, par):
                act.wait_ge(qp_mm, G + 1)
                copy(qp_hi[:, gp, :, :], S[:, 2 * par:2 * par + 2, :], XSCALE).then_inc(qp_hi_ok, 1)

            def split_ctxT(b, pieces=range(4)):
                act.wait_ge(in_ctxT, b * 16 + 16)
                if not isinstance(b, int) or b > 0:
                    act.wait_ge(sim_ok, b * (GB * TG))
                for n in pieces:
                    k, c = n % 2, n // 2
                    copy(ctxT_hi[:, k, c * 512:(c + 1) * 512],
                         ctxT_raw[:, k, c * 512:(c + 1) * 512]).then_inc(ctxT_hi_ok, 1)

            def exponentials(G, gp, r, par):
                act.wait_ge(max_ok, G * TG + (r + 1))
                nc.scalar.activation(probs[:, gp, r, :], S[:, 2 * par:2 * par + 2, :].rearrange("p a n -> p (a n)"),
                                     ACT.Exp, bias=negmax[:, gp, r:r + 1],
                                     accum_out=rowsum[:, gp, r:r + 1]).then_inc(exp_ok, 1)

            def split_probs(G, j):
                act.wait_ge(tr_ok, G * JT + (j + 1))
                copy(pT_hi[:, j % 4, :], T[:, j % 2, :]).then_inc(pT_hi_ok, 1)

            def group(b, g):
                G = b * GB + g
                nxt = 1 - g
                par = (g + 1) % 2
                split_probs(G, 1)
                if g == 1:
                    split_ctxT(b + 1, range(2))
                split_query(G + 1, nxt, par)
                if g == 1:
                    split_ctxT(b + 1, range(2, 4))
                split_probs(G, 2)
                for r in range(TG):
                    split_probs(G, r + 3)
                    exponentials(G + 1, nxt, r, (par + 1 + r) % 2)
                split_probs(G, 7)
                split_probs(G + 1, 0)
                act.wait_ge(av_ok, G * JT + JT)
                copy(UT[:, 0, g * HEADS_G:(g + 1) * HEADS_G,
                        b * NQ:(b + 1) * NQ] if isinstance(b, int) else
                     UT[:, 0, g * HEADS_G:(g + 1) * HEADS_G, bass.ds(b * NQ, NQ)],
                     U[:, 0, :].rearrange("p (h q) -> p h q", h=HEADS_G)).then_inc(ut_a, 1)

            split_ctxT(0, range(2))
            split_query(0, 0, 0)
            split_ctxT(0, range(2, 4))
            queries(2)
            for r in range(TG):
                exponentials(0, 0, r, (1 + r) % 2)
            queries(3)
            split_probs(0, 0)
            with act.Fori(0, NB - 1) as b:
                group(b, 0)
                group(b, 1)
            group(NB - 1, 0)

            def heads_T(t):
                act.wait_ge(o_mm[t], 1)
                copy(OT[:, 0:4, t * P:(t + 1) * P],
                     front[t][:, 0, :].rearrange("p (r t) -> p r t", r=4)).then_inc(o_a[t], 1)

            def split_weights(e, i, m):
                n16 = (e - i) * 8 + 16 if not isinstance(e, int) else (e // 2) * 16 + 16
                act.wait_ge((in_W1, in_W2)[m][i], n16)
                if isinstance(e, int) and e == 0 and m == 0:
                    act.wait_ge(wo_mm[1], 1)
                if not isinstance(e, int) or e >= 2:
                    if m == 0:
                        act.wait_ge(h_mm, (e - 1) * 4)
                    else:
                        act.wait_ge(eo_mm, (e - 1) * 4)
                for n in range(4):
                    copy(Whi[:, i, m, n * 512:(n + 1) * 512], Wraw[i][:, m, n * 512:(n + 1) * 512]
                         ).then_inc(w_hi_ok, 1)

            def query_T(s, t):
                act.wait_ge(qk_mm[t], s + 1)
                copy(qT[:, :, t * P:(t + 1) * P],
                     front[t][:, 0, 0:TOK].rearrange("p (c t) -> p c t", c=KD)).then_inc(sq_ok[t], 1)

            def keys(s, t):
                for h in range(HC):
                    last = copy(kblk[:, 1, 2 * t:2 * t + 2, h, :],
                                front[t][:, 0, 2 * P:3 * P].rearrange("p (b q) -> p b q", b=2), headmask[:, h:h + 1])
                last.then_inc(kb_a[t], 1)

            def values(s, t):
                act.wait_ge(v_mm[t], s + 1)
                act.wait_ge(vzero, 3)
                copy(Vblk[0:NQ, 2 * t:2 * t + 2, :, 0, 0:HD],
                     front[t][0:NQ, 1, :].rearrange("p (b r c e) -> p b r c e", b=2, r=NPAIR, c=2)[:, :, :, 0, :]
                     ).then_inc(vb_a[t], 1)

            def self_exp(s, t):
                for c in range(KD):
                    w = slice(c * HC, (c + 1) * HC)
                    act.wait_ge(shift_ok[t], KD * s + c + 1)
                    nc.scalar.activation(E[:, t, w, :], E[:, t, w, :], ACT.Exp, scale=SSCALE).then_inc(sexp_ok[t], 1)

            def exps_T(s, t):
                act.wait_ge(str_mm[t], KD * s + 1)
                copy(PT[:, t, 0:4, :], front[t][:, 0, :].rearrange("p (r q) -> p r q", r=4)).then_inc(pt_a[t], 1)

            G = NG - 1
            split_probs(G, 1)
            heads_T(0)
            for j in range(2, 6):
                split_probs(G, j)
            rows_T(1, 0, back[0][:, 1, :])
            split_probs(G, 6)
            query_T(0, 0)
            split_probs(G, 7)
            keys(0, 0)
            values(0, 0)
            act.wait_ge(av_ok, G * JT + JT)
            copy(UT[:, 0, HEADS_G:2 * HEADS_G, (NB - 1) * NQ:NB * NQ],
                 U[:, 0, :].rearrange("p (h q) -> p h q", h=HEADS_G)).then_inc(ut_a, 1)

            self_exp(0, 0)
            heads_T(1)
            exps_T(0, 0)
            split_weights(0, 0, 0)
            rows_T(1, 1, back[1][:, 1, :])
            query_T(0, 1)
            keys(0, 1)
            values(0, 1)
            rows_T(2, 0, back[0][:, 1, :])
            self_exp(0, 1)
            query_T(1, 0)
            exps_T(0, 1)
            keys(1, 0)
            values(1, 0)
            split_weights(0, 0, 1)
            rows_T(2, 1, back[1][:, 1, :])
            self_exp(1, 0)
            query_T(1, 1)
            keys(1, 1)
            values(1, 1)
            exps_T(1, 0)
            split_weights(1, 1, 0)
            self_exp(1, 1)
            exps_T(1, 1)
            split_weights(1, 1, 1)

            def relu(e, i, f2):
                act.wait_ge(h_mm, e * 4 + (f2 + 1))
                if not isinstance(e, int) or e > 0:
                    act.wait_ge(h_lo_ok, (e - 1) * 4 + (f2 + 1))
                for c in range(2):
                    ft = 2 * f2 + c
                    bias = b1T[:, e, ft:ft + 1] if isinstance(e, int) else b1T[:, bass.ds(e, 1), ft]
                    last = nc.scalar.activation(h32[:, f2, c, :], S[:, f2, c * TOK:(c + 1) * TOK], ACT.Relu,
                                                bias=bias)
                last.then_inc(relu_ok, 1)

            for t in range(NT):
                act.wait_ge(yT_mm, t + 1)
                copy(yT_hi[:, :, t * P:(t + 1) * P],
                     back[t][:, 1, 0:D].rearrange("p (k q) -> p k q", k=KD)).then_inc(yThi_ok, 1)
            for t in range(NT):
                act.wait_ge(yTlo_ok, t + 1)
                copy(yT[:, :, t * P:(t + 1) * P],
                     back[t][:, 1, 0:D].rearrange("p (k q) -> p k q", k=KD)).then_inc(yT_ok, 1)
            relu(0, 0, 0)
            relu(0, 0, 1)
            for t in range(NT):
                act.wait_ge(gdiff_ok, t + 1)
                nc.scalar.activation(small[:, t, 1, 0:1], small[:, t, 1, 1:2], ACT.Exp).then_inc(gexp_ok, 1)
            relu(0, 0, 2)
            relu(0, 0, 3)
            with act.Fori(0, NE // 2 - 1) as turn:
                e = turn * 2
                for i in range(2):
                    for f2 in range(4):
                        relu(e + (i + 1), 1 - i, f2)
                        if f2 == 1:
                            split_weights(e + (i + 2), i, 0)
                    split_weights(e + (i + 2), i, 1)
            for f2 in range(4):
                relu(NE - 1, 1, f2)
            act.wait_ge(cT_mm, 1)
            copy(cT[:, :], S[0:NE, 0, 0:TOK]).then_inc(cT_ok, 1)

        @block.vector
        def _(dve):
            count = [0]

            def link(ins):
                count[0] += 1
                ins.then_inc(chain, 1)
                dve.wait_ge(chain, count[0])

            sub = ALU.subtract

            def statistics(t, src):
                link(nc.vector.bn_stats(stats[:, t, :], src))
                link(nc.vector.bn_aggr(mv[:, t, 0:2], stats[:, t, :]))
                nc.vector.tensor_scalar(mv[:, t, 2:3], mv[:, t, 1:2], EPS, None, ALU.add).then_inc(mv_ok, 1)

            def centred(n, t, src, dst):
                dve.wait_ge(rstd_ok, n + 1)
                return nc.vector.tensor_scalar(dst, src, mv[:, t, 0:1], rstd[:, t:t + 1], sub, ALU.mult)

            def scaled_residual(n, t, src, scale, dst):
                link(nc.vector.scalar_tensor_tensor(out=src, in0=src, scalar=mv[:, t, 0:1], in1=scale, op0=sub,
                                                    op1=ALU.mult))
                dve.wait_ge(rstd_ok, n + 1)
                return nc.vector.scalar_tensor_tensor(out=dst, in0=src, scalar=rstd[:, t:t + 1], in1=xb[:, t, :],
                                                      op0=ALU.mult, op1=ALU.add)

            dve.sem_inc(ut_v, 1)
            dve.wait_ge(in_x, 16)
            for t in range(NT):
                statistics(t, xr[:, t, :])
            for t in range(NT):
                centred(t, t, xr[:, t, :], xn[:, t, :]).then_inc(xn_ok[t], 1)

            def split_ctxT(b, pieces=range(4)):
                for n in pieces:
                    k, c = n % 2, n // 2
                    w = slice(c * 512, (c + 1) * 512)
                    dve.wait_ge(ctxT_hi_ok, b * 4 + (n + 1))
                    nc.vector.tensor_tensor(ctxT_lo[:, k, w], ctxT_raw[:, k, w], f(ctxT_hi[:, k, w]),
                                            sub).then_inc(ctxT_lo_ok, 1)

            dve.wait_ge(qblk_zero, 1)

            def queries(n):
                dve.wait_ge(q_mm, n + 1)
                nc.vector.tensor_copy(Qblk[DH:P, :, 2 * n:2 * n + 2, 1, :].rearrange("p b r q -> p r b q"),
                                      query_bank[n][DH:P, :].rearrange("p (r b q) -> p r b q", r=2, b=NB)
                                      ).then_inc(q_v, 1)

            def split_query(G, gp, par):
                dve.wait_ge(qp_hi_ok, G + 1)
                nc.vector.scalar_tensor_tensor(out=qp_lo[:, gp, :, :], in0=S[:, 2 * par:2 * par + 2, :],
                                               scalar=XSCALE, in1=f(qp_hi[:, gp, :, :]), op0=ALU.mult,
                                               op1=sub).then_inc(qp_lo_ok, 1)

            def row_max(G, gp, r, par):
                dve.wait_ge(sim_ok, G * TG + (r + 1))
                nc.vector.tensor_reduce(out=negmax[:, gp, r:r + 1],
                                        in_=S[:, 2 * par:2 * par + 2, :].rearrange("p a n -> p (a n)"),
                                        axis=AX_X, op=ALU.max, negate=True).then_inc(max_ok, 1)

            def row_scale(G, gp, r, first=0):
                if first == 0:
                    row_inverse(G, gp, r)
                nc.vector.tensor_scalar(probs[:, gp, r, first:NC_], probs[:, gp, r, first:NC_],
                                        rowinv[:, gp, r:r + 1], None, ALU.mult).then_inc(norm_ok, 1)

            def row_inverse(G, gp, r):
                dve.wait_ge(exp_ok, G * TG + (r + 1))
                nc.vector.reciprocal(rowinv[:, gp, r:r + 1], rowsum[:, gp, r:r + 1]).then_inc(inv_ok, 1)
                dve.wait_ge(inv_ok, G * TG + (r + 1))

            def row_start(G, gp):
                row_inverse(G, gp, TG - 1)
                nc.vector.tensor_scalar(probs[:, gp, TG - 1, 0:P], probs[:, gp, TG - 1, 0:P],
                                        rowinv[:, gp, TG - 1:TG], None, ALU.mult).then_inc(norm_start_ok, 1)

            def split_probs(G, j):
                dve.wait_ge(pT_hi_ok, G * JT + (j + 1))
                nc.vector.tensor_tensor(pT_lo[:, j % 4, :], T[:, j % 2, :], f(pT_hi[:, j % 4, :]),
                                        sub).then_inc(pT_lo_ok, 1)

            def group(b, g):
                G = b * GB + g
                nxt = 1 - g
                par = (g + 1) % 2
                split_probs(G, 1)
                if g == 1:
                    split_ctxT(b + 1, range(2))
                split_query(G + 1, nxt, par)
                if g == 1:
                    split_ctxT(b + 1, range(2, 4))
                split_probs(G, 2)
                for r in range(TG):
                    row_max(G + 1, nxt, r, (par + 1 + r) % 2)
                    split_probs(G, r + 3)
                    if r < TG - 1:
                        row_scale(G + 1, nxt, r)
                row_start(G + 1, nxt)
                split_probs(G, 7)
                row_scale(G + 1, nxt, TG - 1, first=P)
                split_probs(G + 1, 0)
                dve.wait_ge(av_ok, G * JT + JT)
                nc.vector.tensor_copy(UT[:, 1, g * HEADS_G:(g + 1) * HEADS_G,
                                         b * NQ:(b + 1) * NQ] if isinstance(b, int) else
                                      UT[:, 1, g * HEADS_G:(g + 1) * HEADS_G, bass.ds(b * NQ, NQ)],
                                      U[:, 1, :].rearrange("p (h q) -> p h q", h=HEADS_G)).then_inc(ut_v, 1)

            queries(0)
            queries(1)
            split_ctxT(0, range(2))
            split_query(0, 0, 0)
            split_ctxT(0, range(2, 4))
            queries(2)
            row_max(0, 0, 0, 1)
            for r in range(1, TG):
                row_max(0, 0, r, (1 + r) % 2)
                row_scale(0, 0, r - 1)
            queries(3)
            row_start(0, 0)
            row_scale(0, 0, TG - 1, first=P)
            dve.wait_ge(in_ident, 16)
            dve.wait_ge(in_const, 48)
            nc.vector.tensor_copy(ident_bf[:, :], ident[:, :])
            nc.vector.tensor_copy(causal_bf[:, :], causal[:, :]).then_inc(cbf_ok, 1)
            split_probs(0, 0)
            with dve.Fori(0, NB - 1) as b:
                group(b, 0)
                group(b, 1)
            group(NB - 1, 0)

            def heads_T(t):
                dve.wait_ge(o_mm[t], 2)
                nc.vector.tensor_copy(OT[:, 4:8, t * P:(t + 1) * P],
                                      front[t][:, 1, :].rearrange("p (r t) -> p r t", r=4)).then_inc(o_v[t], 1)

            def first_residual(t):
                dve.wait_ge(xb_ok, NT)
                dve.wait_ge(wo_mm[t], 1)
                link(nc.vector.tensor_tensor(xr[:, t, :], back[t][:, 0, 0:D], xb[:, t, :], ALU.add))
                statistics(t, xr[:, t, :])

            def keys(s, t):
                dve.wait_ge(qk_mm[t], s + 1)
                nc.vector.tensor_tensor(kblk[:, 0, 2 * t:2 * t + 2, :, :],
                                        bc(back[t][:, 0, 0:P].rearrange("p (b q) -> p b q", b=2), 2, HC),
                                        bc(bc(headmask[:, :], 1, 2), 3, NQ), ALU.mult).then_inc(kb_v[t], 1)

            def values(s, t):
                dve.wait_ge(v_mm[t], s + 1)
                dve.wait_ge(vzero, 3)
                nc.vector.tensor_copy(
                    Vblk[NQ:P, 2 * t:2 * t + 2, :, 1, 0:HD],
                    front[t][NQ:P, 1, :].rearrange("p (b r c e) -> p b r c e", b=2, r=NPAIR, c=2)[:, :, :, 1, :]
                ).then_inc(vb_v[t], 1)

            def shift(s, t):
                for c in range(KD):
                    w = slice(c * HC, (c + 1) * HC)
                    dve.wait_ge(sc_mm[t], KD * s + c + 1)
                    sc = back[t][:, c, :].rearrange("p (h j) -> p h j", h=HC)
                    link(nc.vector.tensor_reduce(out=nm[:, t, w], in_=sc, axis=AX_X, op=ALU.max))
                    nc.vector.tensor_tensor(E[:, t, w, :], sc, bc(nm[:, t, w], 2, NQ), sub).then_inc(shift_ok[t], 1)

            def exps_T(s, t):
                dve.wait_ge(str_mm[t], KD * s + 2)
                nc.vector.tensor_copy(PT[:, t, 4:8, :],
                                      front[t][:, 1, :].rearrange("p (r q) -> p r q", r=4)).then_inc(pt_v[t], 1)

            def heads_out(s, t):
                dve.wait_ge(ao_mm[t], s + 1)
                heads = back[t][:, 0, 0:NH * (HD + 1)].rearrange("p (h e) -> p h e", h=NH)
                rows = xn[:, t, :].rearrange("p (h e) -> p h e", h=NH)
                link(nc.vector.reciprocal(ri[:, t, :], heads[:, :, HD]))
                link(nc.vector.tensor_tensor(rows, heads[:, :, 0:HD], bc(ri[:, t, :], 2, HD), ALU.mult))
                if s == 0:
                    dve.wait_ge(bv_mm[t], 1)
                    link(nc.vector.tensor_tensor(rows, back[t][:, 1, 0:NH * (HD + 1)].rearrange(
                        "p (h e) -> p h e", h=NH)[:, :, 0:HD], rows, ALU.add))
                statistics(t, xn[:, t, :])

            def second_residual(n, t):
                dve.wait_ge(xbeta_ok[t], 1)
                link(scaled_residual(n, t, xn[:, t, :], vec[:, 1, :], xr[:, t, :]))
                statistics(t, xr[:, t, :])
                centred(n + 1, t, xr[:, t, :], xin[:, t, :]).then_inc(xn_ok[t], 1)

            def moe_input(n, t):
                dve.wait_ge(xb1_ok[t], 1)
                scaled_residual(n, t, xn[:, t, :], vec[:, 3, :], y[:, t, :]).then_inc(y_ok[t], 1)

            G = NG - 1
            split_probs(G, 1)
            heads_T(0)
            split_probs(G, 2)
            split_probs(G, 3)
            first_residual(0)
            split_probs(G, 4)
            centred(2, 0, xr[:, 0, :], xn[:, 0, :]).then_inc(xn_ok[0], 1)
            split_probs(G, 5)
            split_probs(G, 6)
            split_probs(G, 7)
            keys(0, 0)
            values(0, 0)
            dve.wait_ge(av_ok, G * JT + JT)
            nc.vector.tensor_copy(UT[:, 1, HEADS_G:2 * HEADS_G, (NB - 1) * NQ:NB * NQ],
                                  U[:, 1, :].rearrange("p (h q) -> p h q", h=HEADS_G)).then_inc(ut_v, 1)

            shift(0, 0)
            heads_T(1)
            exps_T(0, 0)
            first_residual(1)
            centred(3, 1, xr[:, 1, :], xn[:, 1, :]).then_inc(xn_ok[1], 1)
            heads_out(0, 0)
            keys(0, 1)
            second_residual(4, 0)
            values(0, 1)
            shift(0, 1)
            keys(1, 0)
            exps_T(0, 1)
            heads_out(0, 1)
            values(1, 0)
            second_residual(6, 1)
            shift(1, 0)
            keys(1, 1)
            values(1, 1)
            exps_T(1, 0)
            shift(1, 1)
            heads_out(1, 0)
            exps_T(1, 1)
            moe_input(8, 0)
            heads_out(1, 1)
            moe_input(9, 1)
            for t in range(NT):
                dve.wait_ge(yThi_ok, t + 1)
                nc.vector.tensor_tensor(yT_lo[:, :, t * P:(t + 1) * P],
                                        back[t][:, 1, 0:D].rearrange("p (k q) -> p k q", k=KD),
                                        f(yT_hi[:, :, t * P:(t + 1) * P]), sub).then_inc(yTlo_ok, 1)

            def split_weights(e, i, m):
                for n in range(4):
                    w = slice(n * 512, (n + 1) * 512)
                    dve.wait_ge(w_hi_ok, e * 8 + (4 * m + n + 1))
                    nc.vector.tensor_tensor(Wlo[:, i, m, w], Wraw[i][:, m, w], f(Whi[:, i, m, w]),
                                            sub).then_inc(w_lo_ok, 1)

            def split_hidden(e, i, f2):
                dve.wait_ge(h_hi_ok, e * 4 + (f2 + 1))
                nc.vector.tensor_tensor(hT_lo[:, i, 2 * f2:2 * f2 + 2, :], h32[:, f2, :, :],
                                        f(hT_hi[:, i, 2 * f2:2 * f2 + 2, :]), sub).then_inc(h_lo_ok, 1)

            def combine(e, i):
                dve.wait_ge(eo_mm, e * 4 + 4)
                dve.wait_ge(acc_ok, e * NT + 2 * NT)
                for t in range(NT):
                    c = cw[:, t, e:e + 1] if isinstance(e, int) else cw[:, t, bass.ds(e, 1)]
                    nc.vector.scalar_tensor_tensor(out=acc[:, t, :], in0=(T, U)[i][:, t, 0:D], scalar=c,
                                                   in1=acc[:, t, :], op0=ALU.mult, op1=ALU.add).then_inc(acc_ok, 1)

            split_hidden(0, 0, 0)
            split_hidden(0, 0, 1)
            for t in range(NT):
                dve.wait_ge(lg_mm, t + 1)
                lg, top = small[:, t, 0, :], small[:, t, 2, :]
                link(nc.vector.tensor_copy(lg, U[:, t, 0:NE]))
                link(nc.vector.max(top, lg))
                link(nc.vector.max_index(mx8i[:, t, :], top, lg))
                link(nc.vector.tensor_copy(small[:, t, 3, :], mx8i[:, t, :]))
                nc.vector.tensor_tensor(small[:, t, 1, 1:2], top[:, 1:2], top[:, 0:1], sub).then_inc(gdiff_ok, 1)
            split_hidden(0, 0, 2)
            split_hidden(0, 0, 3)
            dve.wait_ge(gexp_ok, NT)
            ex, w12 = small[:, :, 1, 0:1], small[:, :, 4, :]
            link(nc.vector.tensor_scalar(small[:, :, 5, 0:1], ex, 1.0, None, ALU.add))
            link(nc.vector.reciprocal(w12[:, :, 0:1], small[:, :, 5, 0:1]))
            link(nc.vector.tensor_tensor(w12[:, :, 1:2], ex, w12[:, :, 0:1], ALU.mult))
            for t in range(NT):
                for n in range(2):
                    last = nc.vector.tensor_scalar(small[:, t, 6 + n, :], iota8[:, :], small[:, t, 3, n:n + 1],
                                                   w12[:, t, n:n + 1], ALU.is_equal, ALU.mult)
            link(last)
            nc.vector.tensor_tensor(cw[:, :, :], small[:, :, 6, :], small[:, :, 7, :], ALU.add).then_inc(cw_ok, 1)
            dve.wait_ge(cw_ok, 1)
            with dve.Fori(0, NE // 2 - 1) as turn:
                e = turn * 2
                for i in range(2):
                    for f2 in range(4):
                        split_hidden(e + (i + 1), 1 - i, f2)
                        if f2 == 1:
                            split_weights(e + (i + 2), i, 0)
                    split_weights(e + (i + 2), i, 1)
                    combine(e + i, i)
            for f2 in range(4):
                split_hidden(NE - 1, 1, f2)
            combine(NE - 2, 0)
            dve.wait_ge(b2_mm, 1)
            dve.wait_ge(acc_ok, NT * (NE - 1) + 2 * NT)
            link(nc.vector.tensor_tensor(acc[:, :, :], S[:, 1, :].rearrange("p (t d) -> p t d", t=NT), acc[:, :, :],
                                         ALU.add))
            dve.wait_ge(res_ok, NT)
            for t in range(NT):
                dve.wait_ge(last_mm, t + 1)
                link(nc.vector.scalar_tensor_tensor(out=acc[:, t, :], in0=U[:, t, 0:D], scalar=cw[:, t, NE - 1:NE],
                                                    in1=acc[:, t, :], op0=ALU.mult, op1=ALU.add))
                statistics(t, acc[:, t, :])
                scaled_residual(5 * NT + t, t, acc[:, t, :], vec[:, 5, :], fin[:, t, :]).then_inc(fin_ok, 1)

        @block.gpsimd
        def _(pool):
            count = [0]

            def link(ins):
                count[0] += 1
                ins.then_inc(pchain, 1)
                pool.wait_ge(pchain, count[0])

            calls = [0]

            def inverse_deviation(t):
                pool.wait_ge(mv_ok, calls[0] + 1)
                nc.gpsimd.tensor_tensor(rstd[:, t:t + 1], mv[:, t, 2:3], pw[:, :], ALU.pow).then_inc(rstd_ok, 1)
                calls[0] += 1

            nc.gpsimd.memset(xnT[:, 0, 0:P], 0.0).then_inc(warm_ok, 1)
            nc.gpsimd.memset(pw[:, :], -0.5).then_inc(power_ok, 1)
            pool.wait_ge(power_ok, 1)
            for t in range(NT):
                inverse_deviation(t)
            nc.gpsimd.memset(Qblk[:, :, :, :, :], 0.0).then_inc(qblk_zero, 1)

            def split_ctx(b):
                for j in range(JT):
                    jr = j % (JT // 2)
                    if jr == 0:
                        pool.wait_ge(in_ctx, b * 32 + (16 + 32 * j // JT))
                    if b > 0:
                        pool.wait_ge(av_ok, b * (GB * JT) + (j + 1 - JT))
                    nc.gpsimd.tensor_scalar(ctx_hi[:, j, :], ctx_raw[:, jr, :], 1.0, 1.0, ALU.mult,
                                            ALU.mult).then_inc(ctx_hi_ok, 1)
                    pool.wait_ge(ctx_hi_ok, b * JT + (j + 1))
                    nc.gpsimd.tensor_tensor(ctx_lo[:, j, :], ctx_raw[:, jr, :], f(ctx_hi[:, j, :]),
                                            ALU.subtract).then_inc(ctx_lo_ok, 1)

            for b in range(NB):
                split_ctx(b)
            pool.wait_ge(in_vec, 112)
            for t in range(NT):
                nc.gpsimd.tensor_tensor(xb[:, t, :], xr[:, t, :], vec[:, 0, :], ALU.add).then_inc(xb_ok, 1)

            def split_weights(e, m, pieces=range(4)):
                for n in pieces:
                    w = slice(n * 512, (n + 1) * 512)
                    pool.wait_ge(w_hi_ok, e * 8 + m * 4 + n + 1)
                    nc.gpsimd.tensor_tensor(Wlo[:, e, m, w], Wraw[e][:, m, w], f(Whi[:, e, m, w]),
                                            ALU.subtract).then_inc(w_lo_ok, 1)

            pool.wait_ge(sim_ok, NG * TG)
            nc.gpsimd.memset(Vblk[:, :, :, :, :], 0.0).then_inc(vzero, 1)
            pool.wait_ge(vzero, 1)
            for c in range(2):
                nc.gpsimd.memset(Vblk[c * NQ:(c + 1) * NQ, :, :, c, HD:HD + 1], 1.0).then_inc(vzero, 1)
                pool.wait_ge(vzero, c + 2)
            for t in range(NT):
                inverse_deviation(t)
                pool.wait_ge(xn_ok[t], 2)
                nc.gpsimd.tensor_tensor(xb[:, t, :], xr[:, t, :], vec[:, 2, :], ALU.add).then_inc(xbeta_ok[t], 1)
            pool.wait_ge(wo_mm[1], 1)
            nc.gpsimd.memset(acc[:, :, :], 0.0).then_inc(acc_ok, 2 * NT)
            for t in range(NT):
                inverse_deviation(t)
                inverse_deviation(t)
                pool.wait_ge(xn_ok[t], 3)
                nc.gpsimd.tensor_tensor(xb[:, t, :], xin[:, t, :], vec[:, 4, :], ALU.add).then_inc(xb1_ok[t], 1)
                split_weights(0, t)
            inverse_deviation(0)
            split_weights(1, 0, range(2))
            inverse_deviation(1)
            split_weights(1, 0, range(2, 4))

            def split_hidden(e, i, f2):
                pool.wait_ge(relu_ok, e * 4 + (f2 + 1))
                if e >= 2:
                    pool.wait_ge(eo_mm, (e - 2) * 4 + (f2 + 1))
                nc.gpsimd.tensor_scalar(hT_hi[:, i, 2 * f2:2 * f2 + 2, :], h32[:, f2, :, :], 1.0, 1.0, ALU.mult,
                                        ALU.mult).then_inc(h_hi_ok, 1)

            for e in range(NE):
                for f2 in range(4):
                    split_hidden(e, e % 2, f2)
                    if e == 0:
                        split_weights(1, 1, [f2])
            for t in range(NT):
                pool.wait_ge(y_ok[t], 1)
                link(nc.gpsimd.tensor_tensor(xb[:, t, :], xr[:, t, :], y[:, t, :], ALU.add))
                nc.gpsimd.tensor_tensor(xb[:, t, :], xb[:, t, :], vec[:, 6, :], ALU.add).then_inc(res_ok, 1)
            for t in range(NT):
                inverse_deviation(t)


def _layouts(np, x, ctx_1024, L0_xattn_Wq, L0_xattn_Wk, L0_xattn_Wv, L0_xattn_Wo, L0_xattn_bo, L0_attn_Wq,
             L0_attn_Wk, L0_attn_Wv, L0_attn_rel_bias_table, L0_attn_ln_gamma, L0_attn_ln_beta, L0_ffn_Wq,
             L0_ffn_Wk, L0_ffn_Wv, L0_ffn_gate_W, L0_ffn_W1, L0_ffn_b1, L0_ffn_W2, L0_ffn_b2, L0_ffn_ln1_g,
             L0_ffn_ln1_b, L0_ffn_ln2_g, L0_ffn_ln2_b):
    nq = x.shape[1]
    d = x.shape[2]
    p = np.arange(128)
    table = L0_attn_rel_bias_table
    bt = np.stack([table[nq - 1 - j:2 * nq - 1 - j, :].T for j in range(nq)])
    nh = table.shape[1]
    bt = bt.reshape(nq, nh // 2, 2, nq).transpose(2, 0, 1, 3).reshape(2 * nq, nh // 2, nq)
    ne, ff = L0_ffn_b1.shape
    heads = lambda w: w.transpose(1, 0, 2).reshape(d, -1)
    return {
        "x": x, "ctx": ctx_1024, "ctxT": ctx_1024.transpose(0, 2, 1),
        "xattn_Wq": L0_xattn_Wq, "xattn_WkT": L0_xattn_Wk.T, "xattn_Wv": L0_xattn_Wv, "xattn_Wo": L0_xattn_Wo,
        "bo": L0_xattn_bo, "gamma": L0_attn_ln_gamma, "beta": L0_attn_ln_beta, "g1": L0_ffn_ln1_g,
        "b1n": L0_ffn_ln1_b, "g2": L0_ffn_ln2_g, "b2n": L0_ffn_ln2_b,
        "self0_q": L0_attn_Wq.T, "self0_k": L0_attn_Wk.T, "self0_v": L0_attn_Wv.T,
        "self1_q": heads(L0_ffn_Wq), "self1_k": heads(L0_ffn_Wk), "self1_v": heads(L0_ffn_Wv),
        "biasT": bt, "gate": L0_ffn_gate_W, "W1": L0_ffn_W1, "W2": L0_ffn_W2, "b2": L0_ffn_b2,
        "b1": L0_ffn_b1.reshape(ne, ff // 128, 128).transpose(2, 0, 1).reshape(128, -1),
        "ident": np.eye(128, dtype=np.float32),
        "headmask": (p[:, None] // 16 == np.arange(8)[None, :]).astype(np.float32),
        "causal": np.where(np.arange(nq)[None, :] <= (p % nq)[:, None], 0.0, -1e30).astype(np.float32),
        "iota8": np.tile(np.arange(ne, dtype=np.float32), (128, 1)),
    }


def kernel(**inputs):
    import numpy as _np
    import concourse.bacc as _bacc
    from concourse.bass_utils import run_bass_kernel_spmd as _run

    laid = _layouts(_np, **{k: _np.asarray(v) for k, v in inputs.items()})
    laid = {k: _np.ascontiguousarray(v) for k, v in laid.items()}
    nc = _bacc.Bacc("TRN2", target_bir_lowering=False, num_devices=1)
    arrays, args = {}, {}
    for name, v in laid.items():
        arrays[f"in_{name}"] = v
        args[name] = nc.dram_tensor(f"in_{name}", v.shape, mybir.dt.from_np(v.dtype), kind="ExternalInput").ap()
    out = nc.dram_tensor("out_x", laid["x"].shape, F32, kind="ExternalOutput").ap()
    perceiver_block(nc, args, out)
    r = _run(nc, [arrays], core_ids=[0])
    return r.results[0]["out_x"]
```
